# Optimizing a Trainium2 kernel written in Bass

```python
import numpy as np
import jax
import jax.numpy as jnp

def _softmax(x, axis=-1):
    return jax.nn.softmax(x, axis=axis)

def _gelu(x):
    return jax.nn.gelu(x, approximate=True)

def _silu(x):
    return jax.nn.silu(x)

def _sigmoid(x):
    return jax.nn.sigmoid(x)

def _layernorm(x, axis=-1, eps=1e-05):
    m = jnp.mean(x, axis=axis, keepdims=True)
    v = jnp.var(x, axis=axis, keepdims=True)
    return (x - m) / jnp.sqrt(v + eps)

def _scatter_add(tgt, idx, src, axis=0):
    return tgt.at[idx].add(src)

def _segment_sum(src, seg, n):
    return jax.ops.segment_sum(src, seg, n)
kernel_name = 'mk_macaron_d2_jaxref_r8_f4e529'

def setup_inputs(seed: int=0):
    np.random.seed(seed)
    _w = jnp.asarray

    def _L0_attn_setup():
        import math
        import jax, jax.numpy as jnp
        import numpy as np
        D_MODEL = 128
        N_HEADS = 16
        D_K = D_MODEL // N_HEADS
        D_C = 32
        B, S = (2, 256)
        key = jax.random.key(seed)
        ks = jax.random.split(key, 7)
        sd = lambda fan_in: 1.0 / math.sqrt(fan_in)
        return {'x': jax.random.normal(ks[0], (B, S, D_MODEL), dtype=jnp.float32), 'W_dq': jax.random.uniform(ks[1], (D_MODEL, D_C), minval=-sd(D_MODEL), maxval=sd(D_MODEL), dtype=jnp.float32), 'W_uq': jax.random.uniform(ks[2], (D_C, N_HEADS * D_K), minval=-sd(D_C), maxval=sd(D_C), dtype=jnp.float32), 'W_dkv': jax.random.uniform(ks[3], (D_MODEL, D_C), minval=-sd(D_MODEL), maxval=sd(D_MODEL), dtype=jnp.float32), 'W_uk': jax.random.uniform(ks[4], (D_C, N_HEADS * D_K), minval=-sd(D_C), maxval=sd(D_C), dtype=jnp.float32), 'W_uv': jax.random.uniform(ks[5], (D_C, N_HEADS * D_K), minval=-sd(D_C), maxval=sd(D_C), dtype=jnp.float32), 'W_o': jax.random.uniform(ks[6], (N_HEADS * D_K, D_MODEL), minval=-sd(N_HEADS * D_K), maxval=sd(N_HEADS * D_K), dtype=jnp.float32)}
    _L0_attn_in = _L0_attn_setup()

    def _L0_ffn_setup():
        import jax, jax.numpy as jnp
        import numpy as np
        DIM = 128
        HID = 352
        E = 8
        TOP_K = 2
        EPS = 1e-06

        def _rmsnorm(x, w):
            var = jnp.mean(jnp.square(x), axis=-1, keepdims=True)
            return x * jax.lax.rsqrt(var + EPS) * w
        key = jax.random.key(seed)
        ks = jax.random.split(key, 5)
        x = jax.random.normal(ks[0], (4, 256, DIM), dtype=jnp.float32)
        norm_weight = jnp.ones((DIM,), dtype=jnp.float32)
        router_weight = jax.random.normal(ks[1], (E, DIM), dtype=jnp.float32) * 0.02
        gate_up_weight = jax.random.normal(ks[2], (E, 2 * HID, DIM), dtype=jnp.float32) * (0.02 / np.sqrt(E))
        down_weight = jax.random.normal(ks[3], (E, DIM, HID), dtype=jnp.float32) * (0.02 / np.sqrt(E))
        residual_alpha = jnp.float32(1.0)
        return {'x': x, 'norm_weight': norm_weight, 'router_weight': router_weight, 'gate_up_weight': gate_up_weight, 'down_weight': down_weight, 'residual_alpha': residual_alpha}
    _L0_ffn_in = _L0_ffn_setup()

    def _L1_attn_setup():
        import jax, jax.numpy as jnp
        import numpy as np
        SHIFTS = (-32, -16, -4, -1, 1, 4, 16, 32)
        LN_EPS = 1e-05
        key = jax.random.key(seed)
        k_x, k_g, k_v, k_gm, k_bt = jax.random.split(key, 5)
        B, L, D = (4, 512, 128)
        n = len(SHIFTS) + 1
        scale = 1.0 / np.sqrt(D)
        x = jax.random.normal(k_x, (B, L, D), dtype=jnp.float32)
        gate_W = jax.random.normal(k_g, (n * D, D), dtype=jnp.float32) * scale
        value_W = jax.random.normal(k_v, (D, D), dtype=jnp.float32) * scale
        gamma = jnp.ones((D,), dtype=jnp.float32)
        beta = jnp.zeros((D,), dtype=jnp.float32)
        return {'x': x, 'gate_W': gate_W, 'value_W': value_W, 'gamma': gamma, 'beta': beta}
    _L1_attn_in = _L1_attn_setup()

    def _L1_ffn_setup():
        import jax, jax.numpy as jnp
        import numpy as np
        DIM = 128

        def _reference_tuple_inner(x, W_r, W_k, W_v, mu_r, mu_k):
            B, T, C = x.shape
            x_prev = jnp.concatenate([jnp.zeros((B, 1, C), x.dtype), x[:, :-1, :]], axis=1)
            xr = mu_r * x + (1.0 - mu_r) * x_prev
            xk = mu_k * x + (1.0 - mu_k) * x_prev
            r = jax.nn.sigmoid(jnp.einsum('btc,dc->btd', xr, W_r))
            k = jnp.einsum('btc,dc->btd', xk, W_k)
            k_act = jnp.square(jax.nn.relu(k))
            out = r * jnp.einsum('btc,dc->btd', k_act, W_v)
            new_state = x[:, -1, :]
            return (out, new_state)
        key = jax.random.key(seed)
        ks = jax.random.split(key, 6)
        B, T, C = (8, 256, DIM)
        x = jax.random.normal(ks[0], (B, T, C), dtype=jnp.float32)
        s = 1.0 / np.sqrt(C)
        W_r = jax.random.uniform(ks[1], (C, C), jnp.float32, -s, s)
        W_k = jax.random.uniform(ks[2], (C, C), jnp.float32, -s, s)
        W_v = jax.random.uniform(ks[3], (C, C), jnp.float32, -s, s)
        mu_r = jax.random.uniform(ks[4], (C,), jnp.float32)
        mu_k = jax.random.uniform(ks[5], (C,), jnp.float32)
        return {'x': x, 'W_r': W_r, 'W_k': W_k, 'W_v': W_v, 'mu_r': mu_r, 'mu_k': mu_k}
    _L1_ffn_in = _L1_ffn_setup()
    _d = {'L0_attn_x': _L0_attn_in['x'], 'L0_attn_W_dq': _L0_attn_in['W_dq'], 'L0_attn_W_uq': _L0_attn_in['W_uq'], 'L0_attn_W_dkv': _L0_attn_in['W_dkv'], 'L0_attn_W_uk': _L0_attn_in['W_uk'], 'L0_attn_W_uv': _L0_attn_in['W_uv'], 'L0_attn_W_o': _L0_attn_in['W_o'], 'L0_ffn_norm_weight': _L0_ffn_in['norm_weight'], 'L0_ffn_router_weight': _L0_ffn_in['router_weight'], 'L0_ffn_gate_up_weight': _L0_ffn_in['gate_up_weight'], 'L0_ffn_down_weight': _L0_ffn_in['down_weight'], 'L0_ffn_residual_alpha': _L0_ffn_in['residual_alpha'], 'L1_attn_gate_W': _L1_attn_in['gate_W'], 'L1_attn_value_W': _L1_attn_in['value_W'], 'L1_attn_gamma': _L1_attn_in['gamma'], 'L1_attn_beta': _L1_attn_in['beta'], 'L1_ffn_W_r': _L1_ffn_in['W_r'], 'L1_ffn_W_k': _L1_ffn_in['W_k'], 'L1_ffn_W_v': _L1_ffn_in['W_v'], 'L1_ffn_mu_r': _L1_ffn_in['mu_r'], 'L1_ffn_mu_k': _L1_ffn_in['mu_k']}
    _x0 = _d['L0_attn_x']
    _d['L0_attn_x'] = jax.random.normal(jax.random.fold_in(jax.random.key(seed), 1), (8, 256, 128), dtype=_x0.dtype)
    del _x0
    return _d

def reference(L0_attn_x, L0_attn_W_dq, L0_attn_W_uq, L0_attn_W_dkv, L0_attn_W_uk, L0_attn_W_uv, L0_attn_W_o, L0_ffn_norm_weight, L0_ffn_router_weight, L0_ffn_gate_up_weight, L0_ffn_down_weight, L0_ffn_residual_alpha, L1_attn_gate_W, L1_attn_value_W, L1_attn_gamma, L1_attn_beta, L1_ffn_W_r, L1_ffn_W_k, L1_ffn_W_v, L1_ffn_mu_r, L1_ffn_mu_k):

    def _L0_attn_ref(x, W_dq, W_uq, W_dkv, W_uk, W_uv, W_o):
        import math
        import jax, jax.numpy as jnp
        import numpy as np
        D_MODEL = 128
        N_HEADS = 16
        D_K = D_MODEL // N_HEADS
        D_C = 32
        B, S = (2, 256)
        Bx, Sx, _ = x.shape
        c_q = x @ W_dq
        Q = (c_q @ W_uq).reshape(Bx, Sx, N_HEADS, D_K)
        c_kv = x @ W_dkv
        K = (c_kv @ W_uk).reshape(Bx, Sx, N_HEADS, D_K)
        V = (c_kv @ W_uv).reshape(Bx, Sx, N_HEADS, D_K)
        scores = jnp.einsum('bqhd,bkhd->bhqk', Q, K) / math.sqrt(D_K)
        causal = jnp.tril(jnp.ones((Sx, Sx), dtype=bool))
        scores = jnp.where(causal, scores, -jnp.inf)
        attn = jax.nn.softmax(scores, axis=-1)
        out = jnp.einsum('bhqk,bkhd->bqhd', attn, V).reshape(Bx, Sx, N_HEADS * D_K)
        return out @ W_o

    def _L0_ffn_ref(x, norm_weight, router_weight, gate_up_weight, down_weight, residual_alpha):
        import jax, jax.numpy as jnp
        import numpy as np
        DIM = 128
        HID = 352
        E = 8
        TOP_K = 2
        EPS = 1e-06

        def _rmsnorm(x, w):
            var = jnp.mean(jnp.square(x), axis=-1, keepdims=True)
            return x * jax.lax.rsqrt(var + EPS) * w
        normed = _rmsnorm(x, norm_weight)
        logits = jnp.einsum('bsd,ed->bse', normed, router_weight)
        probs = jax.nn.softmax(logits, axis=-1)
        topk_w, topk_idx = jax.lax.top_k(probs, TOP_K)
        topk_w = topk_w / jnp.sum(topk_w, axis=-1, keepdims=True)
        combine = jnp.sum(jax.nn.one_hot(topk_idx, E, dtype=normed.dtype) * topk_w[..., None], axis=-2)
        moe_out = jnp.zeros_like(x)
        for e in range(E):
            gu = jnp.einsum('bsd,hd->bsh', normed, gate_up_weight[e])
            gate, up = (gu[..., :HID], gu[..., HID:])
            hidden = jax.nn.silu(gate) * up
            out_e = jnp.einsum('bsh,dh->bsd', hidden, down_weight[e])
            moe_out = moe_out + combine[..., e, None] * out_e
        alpha = jnp.clip(residual_alpha, -0.5, 2.0)
        return x + alpha * moe_out

    def _L1_attn_ref(x, gate_W, value_W, gamma, beta):
        import jax, jax.numpy as jnp
        import numpy as np
        SHIFTS = (-32, -16, -4, -1, 1, 4, 16, 32)
        LN_EPS = 1e-05
        B, L, D = x.shape
        n = len(SHIFTS) + 1
        v = jnp.einsum('bld,ed->ble', x, value_W)
        stacked = jnp.stack([v] + [jnp.roll(v, -s, axis=1) for s in SHIFTS], axis=2)
        gates = jax.nn.sigmoid(jnp.einsum('bld,ed->ble', x, gate_W))
        gates = gates.reshape(B, L, n, D)
        out = jnp.sum(stacked * gates, axis=2)
        mu = jnp.mean(out, axis=-1, keepdims=True)
        var = jnp.mean(jnp.square(out - mu), axis=-1, keepdims=True)
        return (out - mu) * jax.lax.rsqrt(var + LN_EPS) * gamma + beta

    def _L1_ffn_ref(x, W_r, W_k, W_v, mu_r, mu_k):
        import jax, jax.numpy as jnp
        import numpy as np
        DIM = 128

        def _reference_tuple_inner(x, W_r, W_k, W_v, mu_r, mu_k):
            B, T, C = x.shape
            x_prev = jnp.concatenate([jnp.zeros((B, 1, C), x.dtype), x[:, :-1, :]], axis=1)
            xr = mu_r * x + (1.0 - mu_r) * x_prev
            xk = mu_k * x + (1.0 - mu_k) * x_prev
            r = jax.nn.sigmoid(jnp.einsum('btc,dc->btd', xr, W_r))
            k = jnp.einsum('btc,dc->btd', xk, W_k)
            k_act = jnp.square(jax.nn.relu(k))
            out = r * jnp.einsum('btc,dc->btd', k_act, W_v)
            new_state = x[:, -1, :]
            return (out, new_state)
        return _reference_tuple_inner(x, W_r, W_k, W_v, mu_r, mu_k)[0]
    x = L0_attn_x
    x = x + 0.5 * _L0_ffn_ref(_layernorm(x, axis=-1), L0_ffn_norm_weight, L0_ffn_router_weight, L0_ffn_gate_up_weight, L0_ffn_down_weight, L0_ffn_residual_alpha)
    x = x + _L0_attn_ref(_layernorm(x, axis=-1), L0_attn_W_dq, L0_attn_W_uq, L0_attn_W_dkv, L0_attn_W_uk, L0_attn_W_uv, L0_attn_W_o)
    x = x + 0.5 * _L0_ffn_ref(_layernorm(x, axis=-1), L0_ffn_norm_weight, L0_ffn_router_weight, L0_ffn_gate_up_weight, L0_ffn_down_weight, L0_ffn_residual_alpha)
    x = x + 0.5 * _L1_ffn_ref(_layernorm(x, axis=-1), L1_ffn_W_r, L1_ffn_W_k, L1_ffn_W_v, L1_ffn_mu_r, L1_ffn_mu_k)
    x = x + _L1_attn_ref(_layernorm(x, axis=-1), L1_attn_gate_W, L1_attn_value_W, L1_attn_gamma, L1_attn_beta)
    x = x + 0.5 * _L1_ffn_ref(_layernorm(x, axis=-1), L1_ffn_W_r, L1_ffn_W_k, L1_ffn_W_v, L1_ffn_mu_r, L1_ffn_mu_k)
    return x

_drawn_inputs = setup_inputs


def setup_inputs(seed=0):
    import zlib

    import numpy as np

    out = dict(_drawn_inputs(seed))
    spreads = {'L0_ffn_norm_weight': (1.0, 0.6), 'L1_attn_gamma': (1.0, 0.2), 'L1_attn_beta': (0.0, 0.1)}
    factors = {'L0_attn_W_dq': 8.0,
     'L0_attn_W_uq': 8.0,
     'L0_attn_W_uk': 8.0,
     'L0_ffn_router_weight': 8.0,
     'L0_ffn_gate_up_weight': 8.0,
     'L0_ffn_down_weight': 8.0,
     'L1_ffn_W_r': 7.21,
     'L1_ffn_mu_r': 8.0,
     'L1_ffn_mu_k': 2.667}
    for name, (base, spread) in spreads.items():
        noise = np.random.default_rng([zlib.crc32(name.encode()), seed]).standard_normal(out[name].shape)
        drawn = base * np.exp(spread * noise) if base else spread * noise
        out[name] = jnp.asarray(drawn.astype(out[name].dtype))
    for name, factor in factors.items():
        out[name] = (out[name] * factor).astype(out[name].dtype)
    return out
```

```python
import concourse.bass as bass
from concourse import mybir
from contextlib import ExitStack

FP32 = mybir.dt.float32
F32R = mybir.dt.float32r
BF16 = mybir.dt.bfloat16
ALU = mybir.AluOpType
ACT = mybir.ActivationFunctionType
AX = mybir.AxisListType

P = 128
D = 128
BATCH, SEQ = 8, 256
TOKENS = BATCH * SEQ
TILES = TOKENS // P
CHUNK = 512
CT = CHUNK // P
CHUNKS = TOKENS // CHUNK

EXPERTS, HID = 8, 352
PARTS = [(0, 128), (128, 128), (256, 96)]
STEPS = EXPERTS * len(PARTS)
LOW0 = 32
NEG_BIG = -3.0e38
MASKED = -1.0e30
LAG = 3

GU0 = 0
DN0 = GU0 + EXPERTS * 2 * HID
ROUTER0 = DN0 + EXPERTS * 3 * D
R0 = ROUTER0 + P
K0, V0, VALUE0 = R0 + D, R0 + 2 * D, R0 + 3 * D
GATES0 = VALUE0 + D
WO0 = GATES0 + 9 * D
CQ0 = WO0 + D
CKV0 = CQ0 + 96
WCOLS = CKV0 + 96

HEADS, DK, DC = 16, 8, 32
SLOTS = 4
GROUPS = HEADS // SLOTS
PAIRS = HEADS // 2
BT = SEQ // P
UQ0, UK0, UV0 = 0, GROUPS * P, 2 * GROUPS * P
UCOLS = UV0 + HEADS * DK
MAX_ROW = 24

SHIFTS = (0, -32, -16, -4, -1, 1, 4, 16, 32)
PAD = 32

NORM_W, ALPHA, Q_SIGN, Q_LOW, K_SIGN, K_LOW, K_ONES, MU_R, MU_K = range(9)


def nth(per, c, i):
    return c * per + (i + 1)


def wait_reuse(eng, sem, value):
    if not isinstance(value, int) or value > 0:
        eng.wait_ge(sem, value)


class Chunks:

    def __init__(self, start):
        self.first, self.last = start, start + CHUNKS - 1

    def each(self, eng, body):
        body(self.first)
        with eng.Fori(self.first + 1, self.last) as c:
            body(c)
        body(self.last)

    def is_first(self, c):
        return isinstance(c, int) and c == self.first

    def is_last(self, c):
        return isinstance(c, int) and c == self.last

    def tokens(self, c):
        return bass.ds((c - self.first) * CHUNK, CHUNK)

    def tiles(self, c):
        return bass.ds((c - self.first) * CT, CT)

    def tile(self, c, t):
        return bass.ds((c - self.first) * CT + t, 1)


class Shared:
    pass


class Chain:

    def __init__(self, eng, sem, per, c):
        self.eng, self.sem, self.per, self.c, self.n = eng, sem, per, c, 0

    def link(self, ins):
        ins.then_inc(self.sem, 1)
        self.n += 1
        self.eng.wait_ge(self.sem, self.c * self.per + self.n)

    def end(self):
        assert self.n == self.per, (self.n, self.per)


def hold(eng, S, sem, value):
    eng.wait_ge(sem, value)
    eng.sem_inc(S.held, 1)


def setup(nc, S, dram):
    with ExitStack() as ctx:
        def sb(n, shape, dt=FP32):
            return ctx.enter_context(nc.sbuf_tensor(n, shape, dt))

        def sem(name):
            return S.sems.enter_context(nc.semaphore(name))

        stage = sb("stage", [P, WCOLS])
        up_stage = sb("up_stage", [96, UCOLS])
        sel_stage, mask_stage = sb("sel_stage", [P, EXPERTS * P]), sb("mask_stage", [P, 6 * P])

        cuts = list(range(0, WCOLS, 704))
        pieces = list(zip(cuts, cuts[1:] + [WCOLS]))
        x_in = [sem(f"x_in{c}") for c in range(CHUNKS)]
        w_in = [sem(f"w_in{n}") for n in range(len(pieces))]
        small_in, late_in = sem("small_in"), sem("late_in")
        hi_done, al = sem("hi_done"), sem("al")
        block = ctx.enter_context(nc.Block())
        xv = dram["x"].rearrange("(c t p) d -> c p t d", p=P, t=CT)

        @block.sync
        def _(sp):
            for c in range(CHUNKS):
                sp.dma_start(S.x[:, c * CT:(c + 1) * CT, :], xv[c]).then_inc(x_in[c], 16)
            for n in range(0, len(pieces), 2):
                a, b = pieces[n]
                sp.dma_start(stage[:, a:b], dram["weights"][:, a:b]).then_inc(w_in[n], 16)
            for dst, src in ((S.gamma, dram["gamma"]), (S.beta, dram["beta"]), (up_stage, dram["up"]), (mask_stage, dram["mask"])):
                sp.dma_start(dst[:, :], src).then_inc(late_in, 16)

        @block.scalar
        def _(act):
            for dst, src in ((S.vec, dram["vec"]), (S.ident, dram["ident"]), (S.rev, dram["rev"]), (sel_stage, dram["sel"])):
                act.dma_start(dst[:, :], src).then_inc(small_in, 16)
            for n in range(1, len(pieces), 2):
                a, b = pieces[n]
                act.dma_start(stage[:, a:b], dram["weights"][:, a:b]).then_inc(w_in[n], 16)
            for n, (a, b) in enumerate(pieces):
                act.wait_ge(w_in[n], 16)
                act.activation(S.whi[:, a:b], stage[:, a:b], ACT.Copy).then_inc(hi_done, 1)
            act.wait_ge(small_in, 64)
            act.activation(S.sel[:, :], sel_stage[:, :], ACT.Copy)
            act.activation(S.ident_bf[:, :], S.ident[:, :], ACT.Copy)
            act.wait_ge(late_in, 64)
            act.activation(S.up[:, :], up_stage[:, :], ACT.Copy).then_inc(hi_done, 1)
            act.activation(S.mask[:, :], mask_stage[:, :], ACT.Copy)

        @block.vector
        def _(dve):
            dve.memset(S.combp[:, :, :], 0.0)
            dve.wait_ge(small_in, 64)
            dve.tensor_scalar(S.half_alpha[:, :], S.vec[:, ALPHA:ALPHA + 1], -0.5, 2.0, ALU.max, ALU.min).then_inc(al, 1)
            dve.wait_ge(al, 1)
            dve.tensor_scalar(S.half_alpha[:, :], S.half_alpha[:, :], 0.5, None, ALU.mult)
            dve.tensor_scalar(S.one_minus_mu[:, :], S.vec[:, MU_R:MU_K + 1], -1.0, 1.0, ALU.mult, ALU.add)
            for n, (a, b) in enumerate(pieces):
                dve.wait_ge(hi_done, n + 1)
                dve.tensor_tensor(S.wlo[:, a:b], stage[:, a:b], S.whi[:, a:b].bitcast(FP32), ALU.subtract)
            dve.wait_ge(hi_done, len(pieces) + 1)
            dve.tensor_tensor(S.up[64:96, :], up_stage[64:96, :], S.up[64:96, :].bitcast(FP32), ALU.subtract)

        @block.gpsimd
        def _(pool):
            for tile, value in ((S.minus_half, -0.5), (S.eps_ln, 1e-5), (S.eps_rms, 1e-6)):
                pool.memset(tile[:, :], value)
            for c in range(CHUNKS):
                pool.wait_ge(x_in[c], 16)


def moe(nc, S, name, sems, start):
    with ExitStack() as ctx:
        def sb(n, shape, dt=FP32):
            return ctx.enter_context(nc.sbuf_tensor(f"{name}_{n}", shape, dt))

        def sem(n):
            if n not in sems:
                sems[n] = S.sems.enter_context(nc.semaphore(f"{name}_{n}"))
            return sems[n]

        norm_hi, norm_lo = sb("norm_hi", [P, TOKENS], F32R), sb("norm_lo", [P, TOKENS], F32R)
        comb_t = sb("comb_t", [P, TOKENS], F32R)
        nr = sb("nr", [P, CT, D])
        xn = sb("xn", [P, CT, D])
        st, mv = sb("st", [P, CT, 6]), sb("mv", [P, CT, 2])
        rstd, rms, tmp = (sb(n, [P, CT]) for n in ("rstd", "rms", "tmp"))
        silu = [sb(f"silu{i}", [P, CHUNK]) for i in range(2)]
        hid = [sb(f"hid{i}", [P, CHUNK]) for i in range(3)]
        hid_hi = [sb(f"hid_hi{i}", [P, CHUNK], F32R) for i in range(4)]
        hid_lo = [sb(f"hid_lo{i}", [P, CHUNK], F32R) for i in range(4)]
        cb = [sb(f"cb{i}", [P, CHUNK]) for i in range(2)]
        scaled = [sb(f"scaled{i}", [P, CHUNK]) for i in range(2)]
        acc = sb("acc", [P, CHUNK])
        lgt = sb("lgt", [P, CHUNK])
        lg, lg2, one1, one2, eq = (sb(n, [P, CT, EXPERTS]) for n in ("lg", "lg2", "one1", "one2", "eq"))
        top1, top2, key1, key2, diff, tanh, w1, w2 = (
            sb(n, [P, CT, 1]) for n in ("top1", "top2", "key1", "key2", "diff", "tanh", "w1", "w2"))

        gate_ps, up_ps, out_ps = S.bank[0:2], S.bank[2:4], S.bank[4:6]
        bc_ps, misc_ps = S.bank[6], S.bank[7]

        nr_done, base_done, xt_done = sem("nr_done"), sem("base_done"), sem("xt_done")
        nhi_done, nlo_done, lg_done = sem("nhi_done"), sem("nlo_done"), sem("lg_done")
        diff_done, tanh_done, comb_done = sem("diff_done"), sem("tanh_done"), sem("comb_done")
        ct_done, cte_done, bc_done, cb_done = sem("ct_done"), sem("cte_done"), sem("bc_done"), sem("cb_done")
        gate_done, up_done, down_done = sem("gate_done"), sem("up_done"), sem("down_done")
        silu_done, hid_done, hi_done, lo_done = sem("silu_done"), sem("hid_done"), sem("hi_done"), sem("lo_done")
        scaled_done, acc_done, fin_done, x_done = sem("scaled_done"), sem("acc_done"), sem("fin_done"), sem("x_done")
        route_order, comb_order, st_done, mv_done, rstd_order = sem("route_order"), sem("comb_order"), sem("st_done"), sem("mv_done"), sem("rstd_order")
        lgt_done, lge_done, xn_done, rstd_done = sem("lgt_done"), sem("lge_done"), sem("xn_done"), sem("rstd_done")
        chunks = Chunks(start)
        block = ctx.enter_context(nc.Block())

        def wgu(half, e, row, n):
            a = GU0 + e * 2 * HID + row
            return half[:, a:a + n]

        def wdn(half, e, p, n):
            a = DN0 + (e * 3 + p) * D
            return half[0:n, a:a + D]

        @block.tensor
        def _(pe):
            def transposes(c):
                pe.wait_ge(nr_done, nth(CT, c, CT - 1))
                wait_reuse(pe, x_done, c - 1)
                for t in range(CT):
                    mm = pe.transpose(misc_ps[:, t * P:(t + 1) * P], nr[:, t, :], S.ident[:, :])
                mm.then_inc(xt_done, 1)

            def logits(c):
                pe.wait_ge(nlo_done, nth(1, c, 0))
                tok = chunks.tokens(c)
                router = slice(ROUTER0, ROUTER0 + P)
                three(pe, misc_ps[:, :], S.whi[:, router], S.wlo[:, router], norm_hi[:, tok], norm_lo[:, tok])\
                    .then_inc(lgt_done, 1)

            def logit_transposes(c):
                pe.wait_ge(lge_done, nth(1, c, 0))
                for t in range(CT):
                    mm = pe.transpose(misc_ps[:, t * P:(t + 1) * P], lgt[:, t * P:(t + 1) * P], S.ident[:, :])
                mm.then_inc(lg_done, 1)

            def comb_transposes(c):
                pe.wait_ge(comb_done, nth(1, c, 0))
                for t in range(CT):
                    mm = pe.transpose(misc_ps[0:P, t * P:(t + 1) * P], S.combp[:, t, :], S.ident[:, :])
                mm.then_inc(ct_done, 1)

            def up_and_gate(c, j):
                e, p = divmod(j, 3)
                row, n = PARTS[p]
                tok = chunks.tokens(c)
                hi, lo = norm_hi[:, tok], norm_lo[:, tok]
                wait_reuse(pe, silu_done, nth(STEPS, c, j - 2))
                three(pe, gate_ps[j % 2][0:n, :], wgu(S.whi, e, row, n), wgu(S.wlo, e, row, n), hi, lo)\
                    .then_inc(gate_done, 1)
                wait_reuse(pe, hid_done, nth(STEPS, c, j - 2))
                three(pe, up_ps[j % 2][0:n, :], wgu(S.whi, e, HID + row, n), wgu(S.wlo, e, HID + row, n), hi, lo)\
                    .then_inc(up_done, 1)

            def down(c, j):
                e, p = divmod(j, 3)
                n = PARTS[p][1]
                out = out_ps[e % 2][:, :]
                if p == 0:
                    wait_reuse(pe, scaled_done, nth(EXPERTS, c, e - 2))
                pe.wait_ge(lo_done, nth(STEPS, c, j))
                hi, lo = hid_hi[j % 4][0:n, :], hid_lo[j % 4][0:n, :]
                pe.matmul(out, wdn(S.whi, e, p, n), hi, start=(p == 0), stop=False)
                pe.matmul(out, wdn(S.whi, e, p, n), lo, start=False, stop=False)
                pe.matmul(out, wdn(S.wlo, e, p, n), hi, start=False, stop=(p == 2)).then_inc(down_done, 1)

            def broadcast(c, e):
                pe.wait_ge(cte_done, nth(1, c, 0))
                wait_reuse(pe, cb_done, nth(EXPERTS, c, e - 1))
                pe.matmul(bc_ps[:, :], S.sel[:, e * P:(e + 1) * P], comb_t[:, chunks.tokens(c)],
                          start=True, stop=True).then_inc(bc_done, 1)

            def result(c):
                pe.wait_ge(acc_done, nth(EXPERTS - 1, c, EXPERTS - 2))
                for t in range(CT):
                    mm = pe.transpose(misc_ps[:, t * P:(t + 1) * P], acc[:, t * P:(t + 1) * P], S.ident[:, :])
                mm.then_inc(fin_done, 1)

            def body(c):
                for j in range(STEPS):
                    if j % 3 == 0:
                        broadcast(c, j // 3)
                    up_and_gate(c, j)
                    if j >= LAG:
                        down(c, j - LAG)
                    elif not chunks.is_first(c):
                        down(c - 1, STEPS + j - LAG)
                    if j == 7 and not chunks.is_first(c):
                        result(c - 1)
                    if not chunks.is_last(c):
                        if j == 9:
                            transposes(c + 1)
                        if j == 12:
                            logits(c + 1)
                        if j == 14:
                            logit_transposes(c + 1)
                        if j == 20:
                            comb_transposes(c + 1)

            transposes(chunks.first)
            logits(chunks.first)
            logit_transposes(chunks.first)
            comb_transposes(chunks.first)
            chunks.each(pe, body)
            for j in range(STEPS - LAG, STEPS):
                down(chunks.last, j)
            result(chunks.last)

        @block.scalar
        def _(act):
            def split_norm(c):
                act.wait_ge(xt_done, nth(1, c, 0))
                act.activation(norm_hi[:, chunks.tokens(c)], misc_ps[:, :], ACT.Copy,
                               scale=S.vec[:, NORM_W:NORM_W + 1]).then_inc(nhi_done, 1)

            def keep_logits(c):
                act.wait_ge(lgt_done, nth(1, c, 0))
                act.activation(lgt[:, :], misc_ps[:, :], ACT.Copy).then_inc(lge_done, 1)

            def weights_tanh(c):
                act.wait_ge(diff_done, nth(1, c, 0))
                act.activation(tanh[:, :, 0], diff[:, :, 0], ACT.Tanh, scale=0.5).then_inc(tanh_done, 1)

            def keep_comb(c):
                act.wait_ge(ct_done, nth(1, c, 0))
                act.activation(comb_t[:, chunks.tokens(c)], misc_ps[0:P, :], ACT.Copy)\
                    .then_inc(cte_done, 1)

            def gate(c, j):
                n = PARTS[j % 3][1]
                act.wait_ge(gate_done, nth(STEPS, c, j))
                wait_reuse(act, hid_done, nth(STEPS, c, j - 2))
                act.activation(silu[j % 2][0:n, :], gate_ps[j % 2][0:n, :], ACT.Silu).then_inc(silu_done, 1)

            def high(c, j):
                n = PARTS[j % 3][1]
                act.wait_ge(hid_done, nth(STEPS, c, j))
                wait_reuse(act, down_done, nth(STEPS, c, j - 4))
                act.activation(hid_hi[j % 4][0:n, :], hid[j % 3][0:n, :], ACT.Copy).then_inc(hi_done, 1)

            def keep_broadcast(c, e):
                act.wait_ge(bc_done, nth(EXPERTS, c, e))
                wait_reuse(act, scaled_done, nth(EXPERTS, c, e - 2))
                act.activation(cb[e % 2][:, :], bc_ps[:, :], ACT.Copy).then_inc(cb_done, 1)

            def body(c):
                for j in range(STEPS):
                    gate(c, j)
                    if j > 0:
                        high(c, j - 1)
                    elif not chunks.is_first(c):
                        high(c - 1, STEPS - 1)
                    if j % 3 == 1:
                        keep_broadcast(c, j // 3)
                    if not chunks.is_last(c):
                        if j == 10:
                            split_norm(c + 1)
                        if j == 12:
                            keep_logits(c + 1)
                        if j == 17:
                            weights_tanh(c + 1)
                        if j == 20:
                            keep_comb(c + 1)

            split_norm(chunks.first)
            keep_logits(chunks.first)
            weights_tanh(chunks.first)
            keep_comb(chunks.first)
            chunks.each(act, body)
            high(chunks.last, STEPS - 1)

        @block.vector
        def _(dve):
            def statistics(c):
                for t in range(CT):
                    dve.bn_stats(st[:, t, :], S.x[:, chunks.tile(c, t), :]).then_inc(st_done, 1)
                hold(dve, S, st_done, nth(CT, c, CT - 1))
                for t in range(CT):
                    dve.bn_aggr(mv[:, t, :], st[:, t, :]).then_inc(mv_done, 1)

            def apply_norm(c):
                dve.wait_ge(rstd_done, nth(1, c, 0))
                for t in range(CT):
                    dve.tensor_scalar(xn[:, t, :], S.x[:, chunks.tile(c, t), :], mv[:, t, 0:1], rstd[:, t:t + 1],
                                      ALU.subtract, ALU.mult).then_inc(xn_done, 1)
                dve.wait_ge(xn_done, nth(CT, c, CT - 1))
                wait_reuse(dve, xt_done, c)
                for t in range(CT):
                    dve.tensor_scalar(nr[:, t, :], xn[:, t, :], rms[:, t:t + 1], None, ALU.mult).then_inc(nr_done, 1)
                x = S.x[:, chunks.tiles(c), :]
                dve.scalar_tensor_tensor(x, xn[:, :, :], 0.5, x, ALU.mult, ALU.add).then_inc(base_done, 1)

            def low_norm(c):
                dve.wait_ge(nhi_done, nth(1, c, 0))
                tok = chunks.tokens(c)
                dve.scalar_tensor_tensor(norm_lo[:, tok], misc_ps[:, :], S.vec[:, NORM_W:NORM_W + 1],
                                         norm_hi[:, tok].bitcast(FP32), ALU.mult, ALU.subtract).then_inc(nlo_done, 1)

            def all8(a):
                return a[:, :, :].to_broadcast([P, CT, EXPERTS])

            def route(c):
                ch = Chain(dve, route_order, 12, c)
                dve.wait_ge(lg_done, nth(1, c, 0))
                ch.link(dve.tensor_copy(lg[:, :, :], misc_ps[:, :].rearrange("p (t e) -> p t e", t=CT)[:, :, 0:EXPERTS]))
                for logit, top, key, one in ((lg, top1, key1, one1), (lg2, top2, key2, one2)):
                    ch.link(dve.reduce_max(top[:, :, 0], logit[:, :, :], axis=AX.X))
                    ch.link(dve.tensor_tensor(eq[:, :, :], logit[:, :, :], all8(top), ALU.is_equal))
                    ch.link(dve.tensor_tensor(eq[:, :, :], eq[:, :, :], S.rev3, ALU.mult))
                    ch.link(dve.reduce_max(key[:, :, 0], eq[:, :, :], axis=AX.X))
                    ch.link(dve.tensor_tensor(one[:, :, :], eq[:, :, :], all8(key), ALU.is_equal))
                    if logit is lg:
                        ch.link(dve.scalar_tensor_tensor(lg2[:, :, :], one1[:, :, :], NEG_BIG, lg[:, :, :],
                                                         ALU.mult, ALU.add))
                dve.tensor_tensor(diff[:, :, :], top2[:, :, :], top1[:, :, :], ALU.subtract).then_inc(diff_done, 1)
                ch.end()

            def combine(c):
                ch = Chain(dve, comb_order, 6, c)
                dve.wait_ge(tanh_done, nth(1, c, 0))
                ch.link(dve.tensor_scalar(w2[:, :, :], tanh[:, :, :], 0.5, 0.5, ALU.mult, ALU.add))
                ch.link(dve.tensor_scalar(w1[:, :, :], tanh[:, :, :], -0.5, 0.5, ALU.mult, ALU.add))
                ch.link(dve.tensor_tensor(one1[:, :, :], one1[:, :, :], all8(w1), ALU.mult))
                ch.link(dve.tensor_tensor(one2[:, :, :], one2[:, :, :], all8(w2), ALU.mult))
                ch.link(dve.tensor_tensor(lg[:, :, :], one1[:, :, :], one2[:, :, :], ALU.add))
                if not chunks.is_first(c):
                    dve.wait_ge(ct_done, c)
                ch.link(dve.tensor_copy(S.combp[:, :, 0:EXPERTS].bitcast(F32R), lg[:, :, :]))
                ch.end()
                dve.tensor_tensor(S.combp[:, :, LOW0:LOW0 + EXPERTS], lg[:, :, :], S.combp[:, :, 0:EXPERTS], ALU.subtract)\
                    .then_inc(comb_done, 1)

            def hidden(c, j):
                n = PARTS[j % 3][1]
                dve.wait_ge(up_done, nth(STEPS, c, j))
                dve.wait_ge(silu_done, nth(STEPS, c, j))
                wait_reuse(dve, lo_done, nth(STEPS, c, j - 3))
                dve.tensor_tensor(hid[j % 3][0:n, :], up_ps[j % 2][0:n, :], silu[j % 2][0:n, :], ALU.mult)\
                    .then_inc(hid_done, 1)

            def low(c, j):
                n = PARTS[j % 3][1]
                dve.wait_ge(hi_done, nth(STEPS, c, j))
                dve.tensor_tensor(hid_lo[j % 4][0:n, :], hid[j % 3][0:n, :], hid_hi[j % 4][0:n, :].bitcast(FP32),
                                  ALU.subtract).then_inc(lo_done, 1)

            def scale(c, e):
                dve.wait_ge(down_done, nth(STEPS, c, 3 * e + 2))
                dve.wait_ge(cb_done, nth(EXPERTS, c, e))
                wait_reuse(dve, acc_done, nth(EXPERTS - 1, c, {0: -2, 1: -1, 2: 0}.get(e, max(0, e - 3))))
                dve.tensor_tensor(scaled[e % 2][:, :], out_ps[e % 2][:, :], cb[e % 2][:, :], ALU.mult)\
                    .then_inc(scaled_done, 1)

            def update(c):
                dve.wait_ge(fin_done, nth(1, c, 0))
                dve.wait_ge(base_done, nth(1, c, 0))
                x = S.x[:, chunks.tiles(c), :]
                dve.scalar_tensor_tensor(x, misc_ps[:, :].rearrange("p (t d) -> p t d", d=D), S.half_alpha[:, 0:1], x,
                                         ALU.mult, ALU.add).then_inc(x_done, 1)

            def body(c):
                for j in range(STEPS):
                    hidden(c, j)
                    if j > 0:
                        low(c, j - 1)
                    elif not chunks.is_first(c):
                        low(c - 1, STEPS - 1)
                    if j % 3 == 0:
                        e = j // 3 - 2
                        if e >= 0:
                            scale(c, e)
                        elif not chunks.is_first(c):
                            scale(c - 1, EXPERTS + e)
                    if j == 8 and not chunks.is_first(c):
                        update(c - 1)
                    if not chunks.is_last(c):
                        if j == 1:
                            statistics(c + 1)
                        if j == 6:
                            apply_norm(c + 1)
                        if j == 10:
                            low_norm(c + 1)
                        if j == 15:
                            route(c + 1)
                        if j == 18:
                            combine(c + 1)

            statistics(chunks.first)
            apply_norm(chunks.first)
            low_norm(chunks.first)
            route(chunks.first)
            combine(chunks.first)
            chunks.each(dve, body)
            low(chunks.last, STEPS - 1)
            scale(chunks.last, EXPERTS - 2)
            scale(chunks.last, EXPERTS - 1)
            update(chunks.last)

        @block.gpsimd
        def _(pool):
            def rstds(c):
                ch = Chain(pool, rstd_order, 5, c)
                var, half = mv[:, :, 1], S.minus_half[:, 0:CT]
                pool.wait_ge(mv_done, nth(CT, c, CT - 1))
                ch.link(pool.tensor_tensor(tmp[:, :], var, S.eps_ln[:, 0:CT], ALU.add))
                ch.link(pool.tensor_tensor(rstd[:, :], tmp[:, :], half, ALU.pow))
                ch.link(pool.tensor_tensor(tmp[:, :], var, rstd[:, :], ALU.mult))
                ch.link(pool.tensor_tensor(tmp[:, :], tmp[:, :], rstd[:, :], ALU.mult))
                ch.link(pool.tensor_tensor(tmp[:, :], tmp[:, :], S.eps_rms[:, 0:CT], ALU.add))
                pool.tensor_tensor(rms[:, :], tmp[:, :], half, ALU.pow).then_inc(rstd_done, 1)
                ch.end()

            def total(c, e):
                pool.wait_ge(scaled_done, nth(EXPERTS, c, e))
                if e == 1:
                    wait_reuse(pool, fin_done, c)
                else:
                    pool.wait_ge(acc_done, nth(EXPERTS - 1, c, e - 2))
                pool.tensor_tensor(acc[:, :], scaled[0][:, :] if e == 1 else acc[:, :], scaled[e % 2][:, :], ALU.add)\
                    .then_inc(acc_done, 1)

            def body(c):
                if not chunks.is_last(c):
                    rstds(c + 1)
                for e in range(1, EXPERTS):
                    total(c, e)

            rstds(chunks.first)
            chunks.each(pool, body)


def three(pe, out, whi, wlo, hi, lo):
    pe.matmul(out, whi, hi, start=True, stop=False)
    pe.matmul(out, whi, lo, start=False, stop=False)
    return pe.matmul(out, wlo, hi, start=False, stop=True)


def columns(S, a, n=D):
    return S.whi[:, a:a + n], S.wlo[:, a:a + n]


def attention(nc, S, name):
    with ExitStack() as ctx:
        def sb(n, shape, dt=FP32):
            return ctx.enter_context(nc.sbuf_tensor(f"{name}_{n}", shape, dt))

        def sem(n):
            return S.sems.enter_context(nc.semaphore(f"{name}_{n}"))

        st, mv = sb("st", [P, BT, 6]), sb("mv", [P, BT, 2])
        rstd, tmp = sb("rstd", [P, BT]), sb("tmp", [P, BT])
        xn = sb("xn", [P, BT, D])
        t_hi, t_lo = sb("t_hi", [P, SEQ], F32R), sb("t_lo", [P, SEQ], F32R)
        low_rank = sb("low_rank", [96, 2 * SEQ], F32R)
        q_part, k_part = sb("q_part", [P, SEQ], F32R), sb("k_part", [P, SEQ], F32R)
        q_st, k_st, q_max = (sb(n, [P, GROUPS, SEQ], F32R) for n in ("q_st", "k_st", "q_max"))
        block_max = sb("block_max", [P, HEADS, 3])
        max_rows = sb("max_rows", [P, BT, HEADS, 32])
        probs = [sb(f"probs{i}", [P, 2, 3, P]) for i in range(3)]
        values = sb("values", [P, BT, HEADS, 32])
        heads_t = sb("heads_t", [P, 2, 2, SEQ])
        rsum, heads = sb("rsum", [P, BT, HEADS, 1]), sb("heads", [P, BT, HEADS, DK])
        h_hi, h_lo = sb("h_hi", [P, SEQ], F32R), sb("h_lo", [P, SEQ], F32R)

        def two_banks(i):
            return S.psum[:, i * 512:(i + 2) * 512].rearrange("p (s c) -> p s c", s=2)

        score_t_ps, score_ps = [two_banks(0), two_banks(2)], two_banks(4)
        head_ps, misc_ps = S.bank[6], S.bank[7]
        split_ps, att_ps = S.bank[0:2], S.bank[2]
        val_ps = xt_ps = S.bank[3]
        rank_ps = S.bank[4]

        names = ("both st mv rstd eps xn t thi tlo c chi clo vmm v qk tqk kq s max mhi mneg mt q2 sc exp pv ot ott rs at att "
                 "ahi alo wo x set").split()
        N = {n: sem(n) for n in names}
        block = ctx.enter_context(nc.Block())
        inv_sqrt = float(DK) ** -0.5

        def slot(j):
            return slice(32 * j, 32 * j + 32)

        def over_batches(eng, body):
            body(-1)
            body(0)
            with eng.Fori(1, BATCH - 2) as b:
                body(b)
            body(BATCH - 2)
            body(BATCH - 1)

        def has(b):
            return not isinstance(b, int) or 0 <= b < BATCH

        @block.tensor
        def _(pe):
            def transposes(b):
                pe.wait_ge(N["xn"], nth(BT, b, BT - 1))
                wait_reuse(pe, N["v"], b)
                for t in range(BT):
                    mm = pe.transpose(xt_ps[:, t * P:(t + 1) * P], xn[:, t, :], S.ident[:, :])
                mm.then_inc(N["t"], 1)

            def ranks(b):
                pe.wait_ge(N["tlo"], nth(1, b, 0))
                wait_reuse(pe, N["q2"], GROUPS * (b - 1))
                three(pe, rank_ps[0:96, 0:SEQ], *columns(S, CQ0, 96), t_hi[:, :], t_lo[:, :])
                three(pe, rank_ps[0:96, SEQ:], *columns(S, CKV0, 96), t_hi[:, :], t_lo[:, :]).then_inc(N["c"], 1)

            def value(b):
                pe.wait_ge(N["clo"], nth(1, b, 0))
                wait_reuse(pe, N["exp"], PAIRS * b)
                for t in range(BT):
                    mm = pe.matmul(val_ps[:, t * P:(t + 1) * P], low_rank[:, SEQ + t * P:SEQ + (t + 1) * P],
                                   S.up[:, UV0:UCOLS], start=True, stop=True)
                mm.then_inc(N["vmm"], 1)

            def project(b, g):
                pe.wait_ge(N["clo"], nth(1, b, 0))
                wait_reuse(pe, N["kq"], nth(GROUPS, b, g - 1))
                if g == 0:
                    wait_reuse(pe, N["x"], nth(1, b - 2, 0))
                pe.matmul(misc_ps[:, 0:SEQ], S.up[:, UQ0 + g * P:UQ0 + (g + 1) * P], low_rank[:, 0:SEQ],
                          start=True, stop=True)
                pe.matmul(misc_ps[:, SEQ:], S.up[:, UK0 + g * P:UK0 + (g + 1) * P], low_rank[:, SEQ:],
                          start=True, stop=True).then_inc(N["qk"], 1)

            def scores(b, u):
                g, pair = u // 2, (2 * (u % 2), 2 * (u % 2) + 1)
                pe.wait_ge(N["kq"], nth(GROUPS, b, g))
                wait_reuse(pe, N["max"], nth(PAIRS, b, u - 1))
                for s in range(2):
                    pe.matmul(score_ps[:, s, 0:3 * P], S.ident_bf[:, :], S.mask[:, 0:3 * P], start=True, stop=False)
                for s, j in enumerate(pair):
                    pe.matmul(score_ps[:, s, 0:SEQ], q_st[slot(j), g, P:SEQ], k_st[slot(j), g, :], start=False, stop=False)
                for s, j in enumerate(pair):
                    mm = pe.matmul(score_ps[:, s, SEQ:SEQ + P], q_st[slot(j), g, 0:P], k_st[slot(j), g, 0:P],
                                   start=False, stop=True)
                mm.then_inc(N["s"], 1)

            def max_transposes(b):
                pe.wait_ge(N["mneg"], nth(1, b, 0))
                for g in range(GROUPS):
                    for t in range(BT):
                        at = (g % 2) * SEQ + t * P
                        mm = pe.transpose(score_ps[:, g // 2, at:at + P],
                                          max_rows[:, t, g * SLOTS:(g + 1) * SLOTS, :], S.ident[:, :])
                mm.then_inc(N["mt"], 1)

            def scores_t(b, u):
                g, pair = u // 2, (2 * (u % 2), 2 * (u % 2) + 1)
                pe.wait_ge(N["q2"], nth(GROUPS, b, g))
                wait_reuse(pe, N["exp"], nth(PAIRS, b, u - 2))
                if u == 0:
                    wait_reuse(pe, N["at"], nth(BT, b - 1, BT - 1))
                if u == 1:
                    pe.wait_ge(N["v"], nth(1, b, 0))
                    wait_reuse(pe, N["alo"], nth(1, b - 1, 0))
                    if has(b + 1):
                        pe.wait_ge(N["tlo"], nth(1, b + 1, 0))
                out = score_t_ps[u % 2]
                for s in range(2):
                    pe.matmul(out[:, s, 0:3 * P], S.ident_bf[:, :], S.mask[:, 3 * P:], start=True, stop=False)
                for s, j in enumerate(pair):
                    pe.matmul(out[:, s, 0:SEQ], k_st[slot(j), g, 0:P], q_max[slot(j), g, :], start=False, stop=False)
                for s, j in enumerate(pair):
                    mm = pe.matmul(out[:, s, SEQ:SEQ + P], k_st[slot(j), g, P:SEQ], q_max[slot(j), g, P:SEQ],
                                   start=False, stop=True)
                mm.then_inc(N["sc"], 1)

            def weigh(b, u):
                g, pair = u // 2, (2 * (u % 2), 2 * (u % 2) + 1)
                pe.wait_ge(N["exp"], nth(PAIRS, b, u))
                if u == 0:
                    pe.wait_ge(N["v"], nth(1, b, 0))
                if u % 4 == 0:
                    wait_reuse(pe, N["ot"], nth(2, b, u // 4 - 1))
                at = (g % 2) * SEQ
                for s, j in enumerate(pair):
                    pe.matmul(head_ps[slot(j), at:at + SEQ], values[:, 0, g * SLOTS + j, :], probs[u % 3][:, s, 0:2, :],
                              start=True, stop=False)
                for s, j in enumerate(pair):
                    mm = pe.matmul(head_ps[slot(j), at + P:at + SEQ], values[:, 1, g * SLOTS + j, :],
                                   probs[u % 3][:, s, 2, :], start=False, stop=True)
                mm.then_inc(N["pv"], 1)

            def head_transposes(b):
                pe.wait_ge(N["ot"], nth(2, b, 1))
                for t in range(BT):
                    for g in range(GROUPS):
                        mm = pe.transpose(split_ps[t][:, g * P:(g + 1) * P],
                                          heads_t[:, g // 2, g % 2, t * P:(t + 1) * P], S.ident[:, :])
                mm.then_inc(N["ott"], 1)

            def back_transposes(b):
                pe.wait_ge(N["at"], nth(BT, b, BT - 1))
                for t in range(BT):
                    mm = pe.transpose(att_ps[:, t * P:(t + 1) * P], heads[:, t, :, :], S.ident[:, :])
                mm.then_inc(N["att"], 1)

            def output(b):
                pe.wait_ge(N["alo"], nth(1, b, 0))
                if has(b + 1):
                    pe.wait_ge(N["kq"], nth(GROUPS, b + 1, GROUPS - 1))
                hi, lo = columns(S, WO0)
                for t in range(BT):
                    mm = three(pe, misc_ps[:, t * P:(t + 1) * P], h_hi[:, t * P:(t + 1) * P],
                               h_lo[:, t * P:(t + 1) * P], hi, lo)
                mm.then_inc(N["wo"], 1)

            def body(b):
                for u in range(PAIRS):
                    if has(b + 1) and u % 2 == 0:
                        project(b + 1, u // 2)
                    if has(b):
                        scores_t(b, u)
                        if u > 0:
                            weigh(b, u - 1)
                    if has(b + 1) and u > 0:
                        scores(b + 1, u - 1)
                if has(b):
                    weigh(b, PAIRS - 1)
                if has(b + 1):
                    scores(b + 1, PAIRS - 1)
                if has(b + 1):
                    max_transposes(b + 1)
                if has(b):
                    head_transposes(b)
                if has(b + 1):
                    value(b + 1)
                if has(b + 2):
                    transposes(b + 2)
                if has(b):
                    back_transposes(b)
                if has(b + 2):
                    ranks(b + 2)
                if has(b):
                    output(b)

            transposes(0)
            ranks(0)
            over_batches(pe, body)

        @block.scalar
        def _(act):
            def split(b):
                act.wait_ge(N["t"], nth(1, b, 0))
                wait_reuse(act, N["c"], b)
                act.activation(t_hi[:, :], xt_ps[:, 0:SEQ], ACT.Copy).then_inc(N["thi"], 1)

            def split_ranks(b):
                act.wait_ge(N["c"], nth(1, b, 0))
                wait_reuse(act, N["vmm"], b)
                act.activation(low_rank[:, :], rank_ps[0:96, :], ACT.Copy).then_inc(N["chi"], 1)

            def keep_value(b):
                act.wait_ge(N["vmm"], nth(1, b, 0))
                wait_reuse(act, N["pv"], PAIRS * b)
                act.activation(values[:, :, :, 0:DK],
                               val_ps[:, 0:SEQ].rearrange("p (t h d) -> p t h d", t=BT, h=HEADS), ACT.Copy)\
                    .then_inc(N["v"], 1)

            def parts(b, g):
                act.wait_ge(N["qk"], nth(GROUPS, b, g))
                wait_reuse(act, N["kq"], nth(GROUPS, b, g - 1))
                act.activation(q_part[:, :], misc_ps[:, 0:SEQ], ACT.Identity, scale=S.vec[:, Q_SIGN:Q_SIGN + 1])\
                    .then_inc(N["tqk"], 1)
                act.activation(k_part[:, :], misc_ps[:, SEQ:], ACT.Identity, scale=S.vec[:, K_SIGN:K_SIGN + 1],
                               bias=S.vec[:, K_ONES:K_ONES + 1]).then_inc(N["tqk"], 1)

            def exps(b, u):
                act.wait_ge(N["sc"], nth(PAIRS, b, u))
                wait_reuse(act, N["pv"], nth(PAIRS, b, u - 3))
                act.activation(probs[u % 3][:, :, :, :].rearrange("p s k q -> p s (k q)"),
                               score_t_ps[u % 2][:, :, 0:3 * P], ACT.Exp, scale=inv_sqrt).then_inc(N["exp"], 1)

            def keep_heads(b, i):
                act.wait_ge(N["pv"], nth(PAIRS, b, 4 * i + 3))
                wait_reuse(act, N["ott"], b)
                act.activation(heads_t[:, i, :, :].rearrange("p g q -> p (g q)"), head_ps, ACT.Copy).then_inc(N["ot"], 1)

            def split_heads(b):
                act.wait_ge(N["att"], nth(1, b, 0))
                wait_reuse(act, N["wo"], b)
                act.activation(h_hi[:, :], att_ps[:, 0:SEQ], ACT.Copy).then_inc(N["ahi"], 1)

            def body(b):
                for u in range(PAIRS):
                    if has(b + 1) and u % 2 == 0:
                        parts(b + 1, u // 2)
                    if has(b):
                        exps(b, u)
                        if u == 5:
                            keep_heads(b, 0)
                if has(b):
                    keep_heads(b, 1)
                if has(b + 1):
                    keep_value(b + 1)
                if has(b + 2):
                    split(b + 2)
                if has(b):
                    split_heads(b)
                if has(b + 2):
                    split_ranks(b + 2)

            act.wait_ge(N["set"], 2)
            split(0)
            split_ranks(0)
            over_batches(act, body)

        @block.vector
        def _(dve):
            def statistics(b):
                for t in range(BT):
                    dve.bn_stats(st[:, t, :], S.x[:, bass.ds(b * BT + t, 1), :]).then_inc(N["st"], 1)
                hold(dve, S, N["st"], nth(BT, b, BT - 1))
                for t in range(BT):
                    dve.bn_aggr(mv[:, t, :], st[:, t, :]).then_inc(N["mv"], 1)

            def apply_norm(b):
                dve.wait_ge(N["rstd"], nth(1, b, 0))
                wait_reuse(dve, N["t"], b)
                for t in range(BT):
                    dve.tensor_scalar(xn[:, t, :], S.x[:, bass.ds(b * BT + t, 1), :], mv[:, t, 0:1], rstd[:, t:t + 1],
                                      ALU.subtract, ALU.mult).then_inc(N["xn"], 1)

            def low(b):
                dve.wait_ge(N["thi"], nth(1, b, 0))
                dve.tensor_tensor(t_lo[:, :], xt_ps[:, 0:SEQ], t_hi[:, :].bitcast(FP32), ALU.subtract).then_inc(N["tlo"], 1)

            def low_ranks(b):
                dve.wait_ge(N["chi"], nth(1, b, 0))
                dve.tensor_tensor(low_rank[DC:2 * DC, :], rank_ps[DC:2 * DC, :], low_rank[DC:2 * DC, :].bitcast(FP32),
                                  ALU.subtract).then_inc(N["clo"], 1)

            def stack(b, g):
                dve.wait_ge(N["tqk"], nth(2 * GROUPS, b, 2 * g + 1))
                wait_reuse(dve, N["sc"], nth(PAIRS, b - 1, 2 * g + 1))
                dve.scalar_tensor_tensor(q_st[:, g, :], misc_ps[:, 0:SEQ], S.vec[:, Q_LOW:Q_LOW + 1],
                                         q_part[:, :].bitcast(FP32), ALU.mult, ALU.add)
                dve.scalar_tensor_tensor(k_st[:, g, :], misc_ps[:, SEQ:], S.vec[:, K_LOW:K_LOW + 1],
                                         k_part[:, :].bitcast(FP32), ALU.mult, ALU.add).then_inc(N["kq"], 1)

            def maxima(b, u):
                dve.wait_ge(N["s"], nth(PAIRS, b, u))
                if u == 0:
                    wait_reuse(dve, N["mneg"], b)
                dve.reduce_max(block_max[:, 2 * u:2 * u + 2, :],
                               score_ps[:, :, 0:3 * P].rearrange("p s (k q) -> p s k q", q=P), axis=AX.X, negate=True)\
                    .then_inc(N["max"], 1)

            def split_maxima(b):
                dve.wait_ge(N["max"], nth(PAIRS, b, PAIRS - 1))
                wait_reuse(dve, N["mt"], b)
                dve.tensor_tensor(block_max[:, :, 1], block_max[:, :, 0], block_max[:, :, 1], ALU.min).then_inc(N["both"], 1)
                dve.wait_ge(N["both"], nth(1, b, 0))
                hi = max_rows[:, :, :, MAX_ROW]
                both = block_max[:, :, 2:0:-1].rearrange("p h t -> p t h")
                dve.tensor_copy(hi.bitcast(F32R), both).then_inc(N["mhi"], 1)
                dve.wait_ge(N["mhi"], nth(1, b, 0))
                dve.tensor_tensor(max_rows[:, :, :, MAX_ROW + 1], both, hi, ALU.subtract).then_inc(N["mneg"], 1)

            def add_maxima(b):
                dve.wait_ge(N["mt"], nth(1, b, 0))
                for g in range(GROUPS):
                    at = (g % 2) * SEQ
                    dve.tensor_tensor(q_max[:, g, :], score_ps[:, g // 2, at:at + SEQ], q_st[:, g, :].bitcast(FP32), ALU.add)\
                        .then_inc(N["q2"], 1)

            def divide(b):
                dve.wait_ge(N["ott"], nth(1, b, 0))
                wait_reuse(dve, N["att"], b)
                for t in range(BT):
                    out = split_ps[t].rearrange("p (h c) -> p h c", h=HEADS)
                    dve.reciprocal(rsum[:, t, :, :], out[:, :, DK:DK + 1]).then_inc(N["rs"], 1)
                for t in range(BT):
                    out = split_ps[t].rearrange("p (h c) -> p h c", h=HEADS)
                    dve.wait_ge(N["rs"], nth(BT, b, t))
                    dve.tensor_tensor(heads[:, t, :, :], out[:, :, 0:DK], rsum[:, t, :, :].to_broadcast([P, HEADS, DK]),
                                      ALU.mult).then_inc(N["at"], 1)

            def low_heads(b):
                dve.wait_ge(N["ahi"], nth(1, b, 0))
                dve.tensor_tensor(h_lo[:, :], att_ps[:, 0:SEQ], h_hi[:, :].bitcast(FP32), ALU.subtract).then_inc(N["alo"], 1)

            def update(b):
                dve.wait_ge(N["wo"], nth(1, b, 0))
                x = S.x[:, bass.ds(b * BT, BT), :]
                dve.tensor_tensor(x, misc_ps[:, 0:SEQ].rearrange("p (t d) -> p t d", d=D), x, ALU.add).then_inc(N["x"], 1)

            def body(b):
                for u in range(PAIRS):
                    if has(b + 1):
                        if u % 2 == 1:
                            stack(b + 1, u // 2)
                        if u > 0:
                            maxima(b + 1, u - 1)
                    if u == 2 and has(b + 2):
                        statistics(b + 2)
                    if u == 6 and has(b + 2):
                        apply_norm(b + 2)
                if has(b + 1):
                    maxima(b + 1, PAIRS - 1)
                if has(b + 1):
                    split_maxima(b + 1)
                    add_maxima(b + 1)
                if has(b):
                    divide(b)
                if has(b + 2):
                    low(b + 2)
                if has(b):
                    low_heads(b)
                if has(b + 2):
                    low_ranks(b + 2)
                if has(b):
                    update(b)

            dve.memset(max_rows[:, :, :, :], 0.0)
            statistics(0)
            apply_norm(0)
            low(0)
            low_ranks(0)
            over_batches(dve, body)

        @block.gpsimd
        def _(pool):
            def power(b):
                pool.wait_ge(N["mv"], nth(BT, b, BT - 1))
                pool.tensor_tensor(tmp[:, :], mv[:, :, 1], S.eps_ln[:, 0:BT], ALU.add).then_inc(N["eps"], 1)
                pool.wait_ge(N["eps"], nth(1, b, 0))
                pool.tensor_tensor(rstd[:, :], tmp[:, :], S.minus_half[:, 0:BT], ALU.pow).then_inc(N["rstd"], 1)

            def body(b):
                if has(b + 2):
                    power(b + 2)

            pool.memset(values[:, :, :, :], 0.0).then_inc(N["set"], 1)
            pool.wait_ge(N["set"], 1)
            pool.memset(values[:, :, :, DK:DK + 1], 1.0).then_inc(N["set"], 1)
            power(0)
            over_batches(pool, body)


def rolls(nc, S, name, sems, start):
    with ExitStack() as ctx:
        def sb(n, shape, dt=FP32):
            return ctx.enter_context(nc.sbuf_tensor(f"{name}_{n}", shape, dt))

        def sem(n):
            if n not in sems:
                sems[n] = S.sems.enter_context(nc.semaphore(f"{name}_{n}"))
            return sems[n]

        NG = len(SHIFTS)
        xn = sb("xn", [P, CT, D])
        t_hi, t_lo = sb("t_hi", [P, CHUNK], F32R), sb("t_lo", [P, CHUNK], F32R)
        value = [sb(f"value{i}", [P, 2, SEQ + 2 * PAD]) for i in range(1)][0]
        gate = [sb(f"gate{i}", [P, CHUNK]) for i in range(3)]
        prod = [sb(f"prod{i}", [P, CHUNK]) for i in range(3)]
        acc = sb("acc", [P, CHUNK])
        st, mv = sb("st", [P, CT, 6]), sb("mv", [P, CT, 2])
        st2, mv2 = sb("st2", [P, CT, 6]), sb("mv2", [P, CT, 2])
        rstd, tmp, rstd2, tmp2 = (sb(n, [P, CT]) for n in ("rstd", "tmp", "rstd2", "tmp2"))
        on = sb("on", [P, CT, D])
        xt_ps, val_ps, sum_ps = S.bank[0], S.bank[1], S.bank[2]
        gate_ps = S.bank[3:6]

        st_done, mv_done, rstd_done, xn_done = sem("st_done"), sem("mv_done"), sem("rstd_done"), sem("xn_done")
        xt_done, hi_done, lo_done, val_done = sem("xt_done"), sem("hi_done"), sem("lo_done"), sem("val_done")
        vpad_done, gmm_done, gate_done, prod_done = sem("vpad_done"), sem("gmm_done"), sem("gate_done"), sem("prod_done")
        acc_done, sum_done, st2_done, mv2_done = sem("acc_done"), sem("sum_done"), sem("st2_done"), sem("mv2_done")
        rstd2_done, on_done, og_done, ob_done = sem("rstd2_done"), sem("on_done"), sem("og_done"), sem("ob_done")
        x_done, eps_done, eps2_done = sem("x_done"), sem("eps_done"), sem("eps2_done")
        chunks = Chunks(start)
        block = ctx.enter_context(nc.Block())

        @block.tensor
        def _(pe):
            def front(c):
                pe.wait_ge(xn_done, nth(CT, c, CT - 1))
                wait_reuse(pe, lo_done, c)
                for t in range(CT):
                    mm = pe.transpose(xt_ps[:, t * P:(t + 1) * P], xn[:, t, :], S.ident[:, :])
                mm.then_inc(xt_done, 1)

            def products(c):
                pe.wait_ge(lo_done, nth(1, c, 0))
                wait_reuse(pe, vpad_done, 3 * c)
                three(pe, val_ps[:, :], *columns(S, VALUE0), t_hi[:, :], t_lo[:, :]).then_inc(val_done, 1)
                for n in range(NG):
                    wait_reuse(pe, gate_done, nth(NG, c, n - 3))
                    three(pe, gate_ps[n % 3][:, :], *columns(S, GATES0 + n * D), t_hi[:, :], t_lo[:, :])\
                        .then_inc(gmm_done, 1)
                    if n == 1 and not chunks.is_first(c):
                        total(c - 1)

            def total(c):
                pe.wait_ge(acc_done, nth(NG - 1, c, NG - 2))
                wait_reuse(pe, on_done, nth(CT, c, -1))
                for t in range(CT):
                    mm = pe.transpose(sum_ps[:, t * P:(t + 1) * P], acc[:, t * P:(t + 1) * P], S.ident[:, :])
                mm.then_inc(sum_done, 1)

            def body(c):
                products(c)
                if not chunks.is_last(c):
                    front(c + 1)

            front(chunks.first)
            chunks.each(pe, body)
            total(chunks.last)

        @block.scalar
        def _(act):
            def front(c):
                act.wait_ge(xt_done, nth(1, c, 0))
                wait_reuse(act, gmm_done, NG * c)
                act.activation(t_hi[:, :], xt_ps[:, :], ACT.Copy).then_inc(hi_done, 1)

            def keep_value(c):
                act.wait_ge(val_done, nth(1, c, 0))
                wait_reuse(act, prod_done, NG * c)
                v = val_ps[:, :].rearrange("p (b s) -> p b s", b=2)
                act.activation(value[:, :, PAD:PAD + SEQ], v, ACT.Copy).then_inc(vpad_done, 1)
                act.activation(value[:, :, 0:PAD], v[:, :, SEQ - PAD:SEQ], ACT.Copy).then_inc(vpad_done, 1)
                act.activation(value[:, :, PAD + SEQ:], v[:, :, 0:PAD], ACT.Copy).then_inc(vpad_done, 1)

            def gates(c):
                for n in range(NG):
                    act.wait_ge(gmm_done, nth(NG, c, n))
                    wait_reuse(act, prod_done, nth(NG, c, n - 3))
                    act.activation(gate[n % 3][:, :], gate_ps[n % 3][:, :], ACT.Sigmoid).then_inc(gate_done, 1)

            def body(c):
                keep_value(c)
                gates(c)
                if not chunks.is_last(c):
                    front(c + 1)

            front(chunks.first)
            chunks.each(act, body)

        @block.vector
        def _(dve):
            def statistics(c):
                for t in range(CT):
                    dve.bn_stats(st[:, t, :], S.x[:, chunks.tile(c, t), :]).then_inc(st_done, 1)
                hold(dve, S, st_done, nth(CT, c, CT - 1))
                for t in range(CT):
                    dve.bn_aggr(mv[:, t, :], st[:, t, :]).then_inc(mv_done, 1)

            def apply_norm(c):
                dve.wait_ge(rstd_done, nth(1, c, 0))
                wait_reuse(dve, xt_done, c)
                for t in range(CT):
                    dve.tensor_scalar(xn[:, t, :], S.x[:, chunks.tile(c, t), :], mv[:, t, 0:1], rstd[:, t:t + 1],
                                      ALU.subtract, ALU.mult).then_inc(xn_done, 1)

            def low(c):
                dve.wait_ge(hi_done, nth(1, c, 0))
                dve.tensor_tensor(t_lo[:, :], xt_ps[:, :], t_hi[:, :].bitcast(FP32), ALU.subtract).then_inc(lo_done, 1)

            def roll(c, n):
                if n == 0:
                    dve.wait_ge(vpad_done, nth(3, c, 2))
                dve.wait_ge(gate_done, nth(NG, c, n))
                wait_reuse(dve, acc_done, nth(NG - 1, c, {0: -3, 1: -2, 2: -1}.get(n, max(0, n - 4))))
                at = PAD + SHIFTS[n]
                dve.tensor_tensor(prod[n % 3][:, :].rearrange("p (b s) -> p b s", b=2),
                                  gate[n % 3][:, :].rearrange("p (b s) -> p b s", b=2),
                                  value[:, :, at:at + SEQ], ALU.mult).then_inc(prod_done, 1)

            def sum_statistics(c):
                hold(dve, S, sum_done, nth(1, c, 0))
                for t in range(CT):
                    dve.bn_stats(st2[:, t, :], sum_ps[:, t * P:(t + 1) * P]).then_inc(st2_done, 1)
                hold(dve, S, st2_done, nth(CT, c, CT - 1))
                for t in range(CT):
                    dve.bn_aggr(mv2[:, t, :], st2[:, t, :]).then_inc(mv2_done, 1)

            def finish(c):
                dve.wait_ge(rstd2_done, nth(1, c, 0))
                wait_reuse(dve, x_done, c)
                for t in range(CT):
                    dve.tensor_scalar(on[:, t, :], sum_ps[:, t * P:(t + 1) * P], mv2[:, t, 0:1], rstd2[:, t:t + 1],
                                      ALU.subtract, ALU.mult).then_inc(on_done, 1)
                dve.wait_ge(on_done, nth(CT, c, CT - 1))
                dve.tensor_tensor(on[:, :, :], on[:, :, :], S.gamma[:, :].unsqueeze(1).to_broadcast([P, CT, D]),
                                  ALU.mult).then_inc(og_done, 1)

            def update(c):
                dve.wait_ge(ob_done, nth(1, c, 0))
                x = S.x[:, chunks.tiles(c), :]
                dve.tensor_tensor(x, x, on[:, :, :], ALU.add).then_inc(x_done, 1)

            def body(c):
                if not chunks.is_last(c):
                    statistics(c + 1)
                roll(c, 0)
                roll(c, 1)
                if not chunks.is_first(c):
                    sum_statistics(c - 1)
                roll(c, 2)
                roll(c, 3)
                if not chunks.is_last(c):
                    apply_norm(c + 1)
                if not chunks.is_first(c):
                    finish(c - 1)
                roll(c, 4)
                roll(c, 5)
                if not chunks.is_last(c):
                    pass
                roll(c, 6)
                if not chunks.is_first(c):
                    update(c - 1)
                roll(c, 7)
                roll(c, 8)
                if not chunks.is_last(c):
                    low(c + 1)

            statistics(chunks.first)
            apply_norm(chunks.first)
            low(chunks.first)
            chunks.each(dve, body)
            sum_statistics(chunks.last)
            finish(chunks.last)
            update(chunks.last)

        @block.gpsimd
        def _(pool):
            def power(c, mv, ready, tmp, eps_done, out, done):
                pool.wait_ge(ready, nth(CT, c, CT - 1))
                pool.tensor_tensor(tmp[:, :], mv[:, :, 1], S.eps_ln[:, 0:CT], ALU.add).then_inc(eps_done, 1)
                pool.wait_ge(eps_done, nth(1, c, 0))
                pool.tensor_tensor(out[:, :], tmp[:, :], S.minus_half[:, 0:CT], ALU.pow).then_inc(done, 1)

            def add(c, n):
                pool.wait_ge(prod_done, nth(NG, c, n))
                if n == 1:
                    wait_reuse(pool, sum_done, c)
                else:
                    pool.wait_ge(acc_done, nth(NG - 1, c, n - 2))
                pool.tensor_tensor(acc[:, :], prod[0][:, :] if n == 1 else acc[:, :], prod[n % 3][:, :], ALU.add)\
                    .then_inc(acc_done, 1)

            def add_beta(c):
                pool.wait_ge(og_done, nth(1, c, 0))
                pool.tensor_tensor(on[:, :, :], on[:, :, :], S.beta[:, :].unsqueeze(1).to_broadcast([P, CT, D]),
                                   ALU.add).then_inc(ob_done, 1)

            def body(c):
                if not chunks.is_last(c):
                    power(c + 1, mv, mv_done, tmp, eps_done, rstd, rstd_done)
                add(c, 1)
                if not chunks.is_first(c):
                    power(c - 1, mv2, mv2_done, tmp2, eps2_done, rstd2, rstd2_done)
                add(c, 2)
                add(c, 3)
                if not chunks.is_first(c):
                    add_beta(c - 1)
                for n in range(4, NG):
                    add(c, n)

            power(chunks.first, mv, mv_done, tmp, eps_done, rstd, rstd_done)
            chunks.each(pool, body)
            power(chunks.last, mv2, mv2_done, tmp2, eps2_done, rstd2, rstd2_done)
            add_beta(chunks.last)


def mix(nc, S, name, sems, start):
    with ExitStack() as ctx:
        def sb(n, shape, dt=FP32):
            return ctx.enter_context(nc.sbuf_tensor(f"{name}_{n}", shape, dt))

        def sem(n):
            if n not in sems:
                sems[n] = S.sems.enter_context(nc.semaphore(f"{name}_{n}"))
            return sems[n]

        xn = sb("xn", [P, CT, D])
        st, mv = sb("st", [P, CT, 6]), sb("mv", [P, CT, 2])
        rstd, tmp = sb("rstd", [P, CT]), sb("tmp", [P, CT])
        xt = sb("xt", [P, 2, SEQ + 1])
        now = [sb(f"now{i}", [P, CHUNK]) for i in range(2)]
        mixed = [sb(f"mixed{i}", [P, CHUNK]) for i in range(2)]
        m_hi = [sb(f"m_hi{i}", [P, CHUNK], F32R) for i in range(2)]
        m_lo = [sb(f"m_lo{i}", [P, CHUNK], F32R) for i in range(2)]
        recept, relu, key = sb("recept", [P, CHUNK]), sb("relu", [P, CHUNK]), sb("key", [P, CHUNK])
        key_hi, key_lo = sb("key_hi", [P, CHUNK], F32R), sb("key_lo", [P, CHUNK], F32R)
        out = sb("out", [P, CHUNK])
        xt_ps, r_ps, k_ps, v_ps, o_ps = S.bank[0:5]

        st_done, mv_done, rstd_done, xn_done = sem("st_done"), sem("mv_done"), sem("rstd_done"), sem("xn_done")
        eps_done, xt_done, keep_done, now_done = sem("eps_done"), sem("xt_done"), sem("keep_done"), sem("now_done")
        mixed_done, mhi_done, mlo_done, rk_done = sem("mixed_done"), sem("mhi_done"), sem("mlo_done"), sem("rk_done")
        sig_done, relu_done, key_done, khi_done = sem("sig_done"), sem("relu_done"), sem("key_done"), sem("khi_done")
        klo_done, v_done, out_done, o_done, x_done = sem("klo_done"), sem("v_done"), sem("out_done"), sem("o_done"), sem("x_done")
        zero_done = sem("zero_done")
        chunks = Chunks(start)
        block = ctx.enter_context(nc.Block())
        before, after = xt[:, :, 0:SEQ], xt[:, :, 1:SEQ + 1]

        def by_batch(a):
            return a[:, :].rearrange("p (b s) -> p b s", b=2)

        @block.tensor
        def _(pe):
            def front(c):
                pe.wait_ge(xn_done, nth(CT, c, CT - 1))
                wait_reuse(pe, keep_done, c)
                for t in range(CT):
                    mm = pe.transpose(xt_ps[:, t * P:(t + 1) * P], xn[:, t, :], S.ident[:, :])
                mm.then_inc(xt_done, 1)

            def r_and_k(c):
                pe.wait_ge(mlo_done, nth(2, c, 1))
                wait_reuse(pe, sig_done, c)
                three(pe, r_ps[:, :], *columns(S, R0), m_hi[0][:, :], m_lo[0][:, :]).then_inc(rk_done, 1)
                wait_reuse(pe, key_done, c)
                three(pe, k_ps[:, :], *columns(S, K0), m_hi[1][:, :], m_lo[1][:, :]).then_inc(rk_done, 1)

            def v(c):
                pe.wait_ge(klo_done, nth(1, c, 0))
                wait_reuse(pe, out_done, c)
                three(pe, v_ps[:, :], *columns(S, V0), key_hi[:, :], key_lo[:, :]).then_inc(v_done, 1)

            def back(c):
                pe.wait_ge(out_done, nth(1, c, 0))
                wait_reuse(pe, x_done, c)
                for t in range(CT):
                    mm = pe.transpose(o_ps[:, t * P:(t + 1) * P], out[:, t * P:(t + 1) * P], S.ident[:, :])
                mm.then_inc(o_done, 1)

            def body(c):
                r_and_k(c)
                if not chunks.is_last(c):
                    front(c + 1)
                v(c)
                back(c)

            front(chunks.first)
            chunks.each(pe, body)

        @block.scalar
        def _(act):
            def front(c):
                act.wait_ge(xt_done, nth(1, c, 0))
                wait_reuse(act, mixed_done, 2 * c)
                act.activation(after, by_batch(xt_ps), ACT.Copy).then_inc(keep_done, 1)
                act.wait_ge(keep_done, nth(1, c, 0))
                for i in range(2):
                    act.activation(by_batch(now[i]), after, ACT.Copy, scale=S.vec[:, MU_R + i:MU_R + i + 1])\
                        .then_inc(now_done, 1)

            def high(c):
                for i in range(2):
                    act.wait_ge(mixed_done, nth(2, c, i))
                    wait_reuse(act, rk_done, 2 * c)
                    act.activation(m_hi[i][:, :], mixed[i][:, :], ACT.Copy).then_inc(mhi_done, 1)

            def gates(c):
                act.wait_ge(rk_done, nth(2, c, 0))
                wait_reuse(act, out_done, c)
                act.activation(recept[:, :], r_ps[:, :], ACT.Sigmoid).then_inc(sig_done, 1)
                act.wait_ge(rk_done, nth(2, c, 1))
                wait_reuse(act, key_done, c)
                act.activation(relu[:, :], k_ps[:, :], ACT.Relu).then_inc(relu_done, 1)

            def key_high(c):
                act.wait_ge(key_done, nth(1, c, 0))
                wait_reuse(act, v_done, c)
                act.activation(key_hi[:, :], key[:, :], ACT.Copy).then_inc(khi_done, 1)

            def body(c):
                gates(c)
                if not chunks.is_last(c):
                    front(c + 1)
                key_high(c)
                if not chunks.is_last(c):
                    high(c + 1)

            front(chunks.first)
            high(chunks.first)
            chunks.each(act, body)

        @block.vector
        def _(dve):
            def statistics(c):
                for t in range(CT):
                    dve.bn_stats(st[:, t, :], S.x[:, chunks.tile(c, t), :]).then_inc(st_done, 1)
                hold(dve, S, st_done, nth(CT, c, CT - 1))
                for t in range(CT):
                    dve.bn_aggr(mv[:, t, :], st[:, t, :]).then_inc(mv_done, 1)

            def apply_norm(c):
                dve.wait_ge(rstd_done, nth(1, c, 0))
                wait_reuse(dve, xt_done, c)
                for t in range(CT):
                    dve.tensor_scalar(xn[:, t, :], S.x[:, chunks.tile(c, t), :], mv[:, t, 0:1], rstd[:, t:t + 1],
                                      ALU.subtract, ALU.mult).then_inc(xn_done, 1)

            def mixes(c):
                for i in range(2):
                    dve.wait_ge(now_done, nth(2, c, i))
                    wait_reuse(dve, mlo_done, 2 * c)
                    dve.scalar_tensor_tensor(by_batch(mixed[i]), before, S.one_minus_mu[:, i:i + 1], by_batch(now[i]),
                                             ALU.mult, ALU.add).then_inc(mixed_done, 1)

            def low(c):
                for i in range(2):
                    dve.wait_ge(mhi_done, nth(2, c, i))
                    dve.tensor_tensor(m_lo[i][:, :], mixed[i][:, :], m_hi[i][:, :].bitcast(FP32), ALU.subtract)\
                        .then_inc(mlo_done, 1)

            def square(c):
                dve.wait_ge(relu_done, nth(1, c, 0))
                wait_reuse(dve, klo_done, c)
                dve.tensor_tensor(key[:, :], k_ps[:, :], relu[:, :], ALU.mult).then_inc(key_done, 1)

            def key_low(c):
                dve.wait_ge(khi_done, nth(1, c, 0))
                dve.tensor_tensor(key_lo[:, :], key[:, :], key_hi[:, :].bitcast(FP32), ALU.subtract).then_inc(klo_done, 1)

            def output(c):
                dve.wait_ge(v_done, nth(1, c, 0))
                dve.wait_ge(sig_done, nth(1, c, 0))
                wait_reuse(dve, o_done, c)
                dve.tensor_tensor(out[:, :], v_ps[:, :], recept[:, :], ALU.mult).then_inc(out_done, 1)

            def update(c):
                dve.wait_ge(o_done, nth(1, c, 0))
                x = S.x[:, chunks.tiles(c), :]
                dve.scalar_tensor_tensor(x, o_ps[:, :].rearrange("p (t d) -> p t d", d=D), 0.5, x, ALU.mult, ALU.add)\
                    .then_inc(x_done, 1)

            def body(c):
                if not chunks.is_last(c):
                    statistics(c + 1)
                square(c)
                if not chunks.is_last(c):
                    apply_norm(c + 1)
                key_low(c)
                if not chunks.is_last(c):
                    mixes(c + 1)
                output(c)
                if not chunks.is_last(c):
                    low(c + 1)
                update(c)

            dve.memset(xt[:, :, 0:1], 0.0).then_inc(zero_done, 1)
            dve.wait_ge(zero_done, start // CHUNKS + 1)
            statistics(chunks.first)
            apply_norm(chunks.first)
            mixes(chunks.first)
            low(chunks.first)
            chunks.each(dve, body)

        @block.gpsimd
        def _(pool):
            def power(c):
                pool.wait_ge(mv_done, nth(CT, c, CT - 1))
                pool.tensor_tensor(tmp[:, :], mv[:, :, 1], S.eps_ln[:, 0:CT], ALU.add).then_inc(eps_done, 1)
                pool.wait_ge(eps_done, nth(1, c, 0))
                pool.tensor_tensor(rstd[:, :], tmp[:, :], S.minus_half[:, 0:CT], ALU.pow).then_inc(rstd_done, 1)

            power(chunks.first)
            chunks.each(pool, lambda c: None if chunks.is_last(c) else power(c + 1))


def store(nc, S, dram):
    with ExitStack() as ctx:
        out_done = ctx.enter_context(nc.semaphore("out_done"))
        block = ctx.enter_context(nc.Block())

        @block.sync
        def _(sp):
            sp.dma_start(dram["out"].rearrange("(t p) d -> p t d", p=P), S.x[:, :, :]).then_inc(out_done, 16)
            sp.wait_ge(out_done, 16)


def macaron(nc, dram):
    with ExitStack() as ctx:
        def sb(n, shape, dt=FP32):
            return ctx.enter_context(nc.sbuf_tensor(n, shape, dt))

        S = Shared()
        S.sems = ctx
        S.x = sb("x", [P, TILES, D])
        S.whi, S.wlo = sb("whi", [P, WCOLS], F32R), sb("wlo", [P, WCOLS], F32R)
        S.sel = sb("sel", [P, EXPERTS * P], F32R)
        S.ident = sb("ident", [P, P])
        S.rev = sb("rev", [P, CT * EXPERTS])
        S.rev3 = S.rev[:, :].rearrange("p (t e) -> p t e", e=EXPERTS)
        S.vec, S.half_alpha, S.one_minus_mu = sb("vec", [P, 9]), sb("half_alpha", [P, 1]), sb("one_minus_mu", [P, 2])
        S.gamma, S.beta = sb("gamma", [P, D]), sb("beta", [P, D])
        S.ident_bf, S.mask = sb("ident_bf", [P, P], BF16), sb("mask", [P, 6 * P], BF16)
        S.up = sb("up", [96, UCOLS], F32R)
        S.combp = sb("combp", [P, CT, P])
        S.minus_half, S.eps_ln, S.eps_rms = (sb(n, [P, CT]) for n in ("minus_half", "eps_ln", "eps_rms"))
        S.held = ctx.enter_context(nc.semaphore("held"))
        S.psum = ctx.enter_context(nc.psum_tensor("psum", [P, 8 * 512], FP32))
        S.bank = [S.psum[:, i * 512:(i + 1) * 512] for i in range(8)]
        setup(nc, S, dram)
        moe_sems, mix_sems = {}, {}
        moe(nc, S, "moe1", moe_sems, 0)
        attention(nc, S, "attn")
        moe(nc, S, "moe2", moe_sems, CHUNKS)
        mix(nc, S, "mix1", mix_sems, 0)
        rolls(nc, S, "rolls", {}, 0)
        mix(nc, S, "mix2", mix_sems, CHUNKS)
        store(nc, S, dram)


def kernel(**inputs):
    import numpy as np
    import concourse.bacc as bacc
    from concourse.bass_utils import run_bass_kernel_spmd

    def grab(n):
        return np.asarray(inputs[n])

    f = np.float32
    gate_up = grab("L0_ffn_gate_up_weight").transpose(2, 0, 1).reshape(D, EXPERTS * 2 * HID)
    down = np.zeros((EXPERTS, 3 * P, D), f)
    down[:, :HID, :] = grab("L0_ffn_down_weight").transpose(0, 2, 1)
    down = down.reshape(EXPERTS, 3, P, D).transpose(2, 0, 1, 3).reshape(P, EXPERTS * 3 * D)
    sel = np.zeros((P, EXPERTS, P), f)
    for e in range(EXPERTS):
        sel[e, e, :] = 1.0
        sel[LOW0 + e, e, :] = 1.0
    weights = [gate_up, down, grab("L0_ffn_router_weight").T, np.zeros((D, P - EXPERTS), f)]
    weights += [grab(f"L1_ffn_W_{n}").T for n in "rkv"]
    weights += [grab("L1_attn_value_W").T, grab("L1_attn_gate_W").T, grab("L0_attn_W_o")]
    weights += [grab("L0_attn_W_dq")] * 3 + [grab("L0_attn_W_dkv")] * 3
    up = np.zeros((DC, UCOLS), f)
    for n, at in (("uq", UQ0), ("uk", UK0)):
        v = up[:, at:at + GROUPS * P].reshape(DC, HEADS, 32)
        w = grab(f"L0_attn_W_{n}").reshape(DC, HEADS, DK)
        for r in range(3):
            v[:, :, r * DK:(r + 1) * DK] = w
    up[:, UV0:] = grab("L0_attn_W_uv")
    row = np.arange(P) % 32 // DK
    one = np.ones(P, f)
    vec = [grab("L0_ffn_norm_weight"), np.broadcast_to(grab("L0_ffn_residual_alpha"), (P,)),
           np.array([1, 1, -1, 0], f)[row], np.array([0, 0, 1, 0], f)[row],
           np.array([1, -1, 1, 0], f)[row], np.array([0, 1, 0, 0], f)[row],
           np.isin(np.arange(P) % 32, (MAX_ROW, MAX_ROW + 1)).astype(f),
           grab("L1_ffn_mu_r"), grab("L1_ffn_mu_k")]
    later = np.where(np.arange(P)[None, :] > np.arange(P)[:, None], f(MASKED), f(0))
    none = np.zeros((P, P), f)
    arrays = {
        "x": grab("L0_attn_x").reshape(TOKENS, D),
        "weights": np.concatenate(weights, axis=1),
        "up": np.concatenate([up] * 3, axis=0),
        "vec": np.stack(vec, axis=1),
        "gamma": np.broadcast_to(grab("L1_attn_gamma"), (P, D)),
        "beta": np.broadcast_to(grab("L1_attn_beta"), (P, D)),
        "mask": np.concatenate([none, later, later, later.T, none, later.T], axis=1),
        "sel": sel.reshape(P, EXPERTS * P),
        "ident": np.eye(P, dtype=f),
        "rev": np.broadcast_to(np.tile(np.arange(EXPERTS, 0, -1, dtype=f), CT), (P, CT * EXPERTS)),
    }
    nc = bacc.Bacc("TRN2", target_bir_lowering=False, num_devices=1)
    dram, sent = {}, {}
    for n, a in arrays.items():
        a = np.ascontiguousarray(a)
        sent[f"in_{n}"] = a
        dram[n] = nc.dram_tensor(f"in_{n}", a.shape, mybir.dt.from_np(a.dtype), kind="ExternalInput").ap()
    dram["out"] = nc.dram_tensor("out_x", (TOKENS, D), FP32, kind="ExternalOutput").ap()
    macaron(nc, dram)
    r = run_bass_kernel_spmd(nc, [sent], core_ids=[0])
    return r.results[0]["out_x"].reshape(BATCH, SEQ, D)
```

```python
import concourse.bass as bass
from concourse import mybir
from contextlib import ExitStack

FP32 = mybir.dt.float32
F32R = mybir.dt.float32r
BF16 = mybir.dt.bfloat16
ALU = mybir.AluOpType
ACT = mybir.ActivationFunctionType
AX = mybir.AxisListType

P = 128
D = 128
BATCH, SEQ = 8, 256
TOKENS = BATCH * SEQ
TILES = TOKENS // P
CHUNK = 512
CT = CHUNK // P
CHUNKS = TOKENS // CHUNK

EXPERTS, HID = 8, 352
PARTS = [(0, 128), (128, 128), (256, 96)]
STEPS = EXPERTS * len(PARTS)
LOW0 = 32
NEG_BIG = -3.0e38
MASKED = -1.0e30
LAG = 3

GU0 = 0
DN0 = GU0 + EXPERTS * 2 * HID
ROUTER0 = DN0 + EXPERTS * 3 * D
R0 = ROUTER0 + P
K0, V0, VALUE0 = R0 + D, R0 + 2 * D, R0 + 3 * D
GATES0 = VALUE0 + D
WO0 = GATES0 + 9 * D
CQ0 = WO0 + D
CKV0 = CQ0 + 96
WCOLS = CKV0 + 96

HEADS, DK, DC = 16, 8, 32
SLOTS = 4
GROUPS = HEADS // SLOTS
PAIRS = HEADS // 2
BT = SEQ // P
UQ0, UK0, UV0 = 0, GROUPS * P, 2 * GROUPS * P
UCOLS = UV0 + HEADS * DK
BEHIND = 3
MAX_ROW = 24

SHIFTS = (0, -32, -16, -4, -1, 1, 4, 16, 32)
PAD = 32

NORM_W, ALPHA, Q_SIGN, Q_LOW, K_SIGN, K_LOW, K_ONES, MU_R, MU_K = range(9)


def nth(per, c, i):
    return c * per + (i + 1)


def wait_reuse(eng, sem, value):
    if not isinstance(value, int) or value > 0:
        eng.wait_ge(sem, value)


class Chunks:

    def __init__(self, start):
        self.first, self.last = start, start + CHUNKS - 1

    def each(self, eng, body):
        body(self.first)
        with eng.Fori(self.first + 1, self.last) as c:
            body(c)
        body(self.last)

    def is_first(self, c):
        return isinstance(c, int) and c == self.first

    def is_last(self, c):
        return isinstance(c, int) and c == self.last

    def tokens(self, c):
        return bass.ds((c - self.first) * CHUNK, CHUNK)

    def tiles(self, c):
        return bass.ds((c - self.first) * CT, CT)

    def tile(self, c, t):
        return bass.ds((c - self.first) * CT + t, 1)


class Shared:
    pass


class Chain:

    def __init__(self, eng, sem, per, c):
        self.eng, self.sem, self.per, self.c, self.n = eng, sem, per, c, 0

    def link(self, ins):
        ins.then_inc(self.sem, 1)
        self.n += 1
        self.eng.wait_ge(self.sem, self.c * self.per + self.n)

    def end(self):
        assert self.n == self.per, (self.n, self.per)


def hold(eng, S, sem, value):
    eng.wait_ge(sem, value)
    eng.sem_inc(S.held, 1)


def setup(nc, S, dram):
    with ExitStack() as ctx:
        def sb(n, shape, dt=FP32):
            return ctx.enter_context(nc.sbuf_tensor(n, shape, dt))

        def sem(name):
            return S.sems.enter_context(nc.semaphore(name))

        stage = sb("stage", [P, WCOLS])
        up_stage = sb("up_stage", [96, UCOLS])
        sel_stage, mask_stage = sb("sel_stage", [P, EXPERTS * P]), sb("mask_stage", [P, 6 * P])

        cuts = list(range(0, WCOLS, 704))
        pieces = list(zip(cuts, cuts[1:] + [WCOLS]))
        x_in = [sem(f"x_in{c}") for c in range(CHUNKS)]
        w_in = [sem(f"w_in{n}") for n in range(len(pieces))]
        small_in, late_in = sem("small_in"), sem("late_in")
        hi_done, al, mu_done, fold_done = sem("hi_done"), sem("al"), sem("mu_done"), sem("fold_done")
        block = ctx.enter_context(nc.Block())
        xv = dram["x"].rearrange("(c t p) d -> c p t d", p=P, t=CT)

        def folded(n):
            w, shift = divmod(n, 2)
            mu = S.vec[:, MU_R + w:MU_R + w + 1] if shift == 0 else S.one_minus_mu[:, w:w + 1]
            return stage[:, R0 + w * D:R0 + (w + 1) * D], mu

        @block.sync
        def _(sp):
            for c in range(CHUNKS):
                sp.dma_start(S.x[:, c * CT:(c + 1) * CT, :], xv[c]).then_inc(x_in[c], 16)
            for n in range(0, len(pieces), 2):
                a, b = pieces[n]
                sp.dma_start(stage[:, a:b], dram["weights"][:, a:b]).then_inc(w_in[n], 16)
            for dst, src in ((S.gamma, dram["gamma"]), (S.beta, dram["beta"]), (up_stage, dram["up"]), (mask_stage, dram["mask"])):
                sp.dma_start(dst[:, :], src).then_inc(late_in, 16)

        @block.scalar
        def _(act):
            for dst, src in ((S.vec, dram["vec"]), (S.ident, dram["ident"]), (S.rev, dram["rev"]), (sel_stage, dram["sel"])):
                act.dma_start(dst[:, :], src).then_inc(small_in, 16)
            for n in range(1, len(pieces), 2):
                a, b = pieces[n]
                act.dma_start(stage[:, a:b], dram["weights"][:, a:b]).then_inc(w_in[n], 16)
            for n, (a, b) in enumerate(pieces):
                act.wait_ge(w_in[n], 16)
                act.activation(S.whi[:, a:b], stage[:, a:b], ACT.Copy).then_inc(hi_done, 1)
            act.wait_ge(small_in, 64)
            act.activation(S.sel[:, :], sel_stage[:, :], ACT.Copy)
            act.wait_ge(mu_done, 1)
            for n in range(4):
                mm = act.activation(S.fold_hi[:, n * D:(n + 1) * D], folded(n)[0], ACT.Copy, scale=folded(n)[1])
            mm.then_inc(fold_done, 1)
            act.activation(S.ident_bf[:, :], S.ident[:, :], ACT.Copy)
            act.wait_ge(late_in, 64)
            act.activation(S.up[:, :], up_stage[:, :], ACT.Copy).then_inc(hi_done, 1)
            act.activation(S.mask[:, :], mask_stage[:, :], ACT.Copy)

        @block.vector
        def _(dve):
            dve.memset(S.combp[:, :, :], 0.0)
            dve.wait_ge(small_in, 64)
            dve.tensor_scalar(S.half_alpha[:, :], S.vec[:, ALPHA:ALPHA + 1], -0.5, 2.0, ALU.max, ALU.min).then_inc(al, 1)
            dve.wait_ge(al, 1)
            dve.tensor_scalar(S.half_alpha[:, :], S.half_alpha[:, :], 0.5, None, ALU.mult)
            dve.tensor_scalar(S.one_minus_mu[:, :], S.vec[:, MU_R:MU_K + 1], -1.0, 1.0, ALU.mult, ALU.add).then_inc(mu_done, 1)
            for n, (a, b) in enumerate(pieces):
                dve.wait_ge(hi_done, n + 1)
                dve.tensor_tensor(S.wlo[:, a:b], stage[:, a:b], S.whi[:, a:b].bitcast(FP32), ALU.subtract)
            dve.wait_ge(fold_done, 1)
            for n in range(4):
                w, mu = folded(n)
                at = slice(n * D, (n + 1) * D)
                dve.scalar_tensor_tensor(S.fold_lo[:, at], w, mu, S.fold_hi[:, at].bitcast(FP32), ALU.mult, ALU.subtract)
            dve.wait_ge(hi_done, len(pieces) + 1)
            dve.tensor_tensor(S.up[64:96, :], up_stage[64:96, :], S.up[64:96, :].bitcast(FP32), ALU.subtract)

        @block.gpsimd
        def _(pool):
            for tile, value in ((S.minus_half, -0.5), (S.eps_ln, 1e-5), (S.eps_rms, 1e-6)):
                pool.memset(tile[:, :], value)
            for c in range(CHUNKS):
                pool.wait_ge(x_in[c], 16)


def moe(nc, S, name, sems, start):
    with ExitStack() as ctx:
        def sb(n, shape, dt=FP32):
            return ctx.enter_context(nc.sbuf_tensor(f"{name}_{n}", shape, dt))

        def sem(n):
            if n not in sems:
                sems[n] = S.sems.enter_context(nc.semaphore(f"{name}_{n}"))
            return sems[n]

        norm_hi, norm_lo = sb("norm_hi", [P, TOKENS], F32R), sb("norm_lo", [P, TOKENS], F32R)
        comb_t = sb("comb_t", [P, TOKENS], F32R)
        nr = sb("nr", [P, CT, D])
        xn = sb("xn", [P, CT, D])
        st, mv = sb("st", [P, CT, 6]), sb("mv", [P, CT, 2])
        rstd, rms, tmp = (sb(n, [P, CT]) for n in ("rstd", "rms", "tmp"))
        silu = [sb(f"silu{i}", [P, CHUNK]) for i in range(2)]
        hid = [sb(f"hid{i}", [P, CHUNK]) for i in range(3)]
        hid_hi = [sb(f"hid_hi{i}", [P, CHUNK], F32R) for i in range(4)]
        hid_lo = [sb(f"hid_lo{i}", [P, CHUNK], F32R) for i in range(4)]
        cb = [sb(f"cb{i}", [P, CHUNK]) for i in range(2)]
        scaled = [sb(f"scaled{i}", [P, CHUNK]) for i in range(2)]
        acc = sb("acc", [P, CHUNK])
        lgt = sb("lgt", [P, CHUNK])
        lg, lg2, one1, one2, eq = (sb(n, [P, CT, EXPERTS]) for n in ("lg", "lg2", "one1", "one2", "eq"))
        top1, top2, key1, key2, diff, tanh, w1, w2 = (
            sb(n, [P, CT, 1]) for n in ("top1", "top2", "key1", "key2", "diff", "tanh", "w1", "w2"))

        gate_ps, up_ps, out_ps = S.bank[0:2], S.bank[2:4], S.bank[4:6]
        bc_ps, misc_ps = S.bank[6], S.bank[7]

        nr_done, base_done, xt_done = sem("nr_done"), sem("base_done"), sem("xt_done")
        nhi_done, nlo_done, lg_done = sem("nhi_done"), sem("nlo_done"), sem("lg_done")
        diff_done, tanh_done, comb_done = sem("diff_done"), sem("tanh_done"), sem("comb_done")
        ct_done, cte_done, bc_done, cb_done = sem("ct_done"), sem("cte_done"), sem("bc_done"), sem("cb_done")
        gate_done, up_done, down_done = sem("gate_done"), sem("up_done"), sem("down_done")
        silu_done, hid_done, hi_done, lo_done = sem("silu_done"), sem("hid_done"), sem("hi_done"), sem("lo_done")
        scaled_done, acc_done, fin_done, x_done = sem("scaled_done"), sem("acc_done"), sem("fin_done"), sem("x_done")
        route_order, comb_order, st_done, mv_done, rstd_order = sem("route_order"), sem("comb_order"), sem("st_done"), sem("mv_done"), sem("rstd_order")
        lgt_done, lge_done, xn_done, rstd_done = sem("lgt_done"), sem("lge_done"), sem("xn_done"), sem("rstd_done")
        chunks = Chunks(start)
        block = ctx.enter_context(nc.Block())

        def wgu(half, e, row, n):
            a = GU0 + e * 2 * HID + row
            return half[:, a:a + n]

        def wdn(half, e, p, n):
            a = DN0 + (e * 3 + p) * D
            return half[0:n, a:a + D]

        @block.tensor
        def _(pe):
            def transposes(c):
                pe.wait_ge(nr_done, nth(CT, c, CT - 1))
                wait_reuse(pe, x_done, c - 1)
                for t in range(CT):
                    mm = pe.transpose(misc_ps[:, t * P:(t + 1) * P], nr[:, t, :], S.ident[:, :])
                mm.then_inc(xt_done, 1)

            def logits(c):
                pe.wait_ge(nlo_done, nth(1, c, 0))
                tok = chunks.tokens(c)
                router = slice(ROUTER0, ROUTER0 + P)
                three(pe, misc_ps[:, :], S.whi[:, router], S.wlo[:, router], norm_hi[:, tok], norm_lo[:, tok])\
                    .then_inc(lgt_done, 1)

            def logit_transposes(c):
                pe.wait_ge(lge_done, nth(1, c, 0))
                for t in range(CT):
                    mm = pe.transpose(misc_ps[:, t * P:(t + 1) * P], lgt[:, t * P:(t + 1) * P], S.ident[:, :])
                mm.then_inc(lg_done, 1)

            def comb_transposes(c):
                pe.wait_ge(comb_done, nth(1, c, 0))
                for t in range(CT):
                    mm = pe.transpose(misc_ps[0:P, t * P:(t + 1) * P], S.combp[:, t, :], S.ident[:, :])
                mm.then_inc(ct_done, 1)

            def up_and_gate(c, j):
                e, p = divmod(j, 3)
                row, n = PARTS[p]
                tok = chunks.tokens(c)
                hi, lo = norm_hi[:, tok], norm_lo[:, tok]
                wait_reuse(pe, silu_done, nth(STEPS, c, j - 2))
                three(pe, gate_ps[j % 2][0:n, :], wgu(S.whi, e, row, n), wgu(S.wlo, e, row, n), hi, lo)\
                    .then_inc(gate_done, 1)
                wait_reuse(pe, hid_done, nth(STEPS, c, j - 2))
                three(pe, up_ps[j % 2][0:n, :], wgu(S.whi, e, HID + row, n), wgu(S.wlo, e, HID + row, n), hi, lo)\
                    .then_inc(up_done, 1)

            def down(c, j):
                e, p = divmod(j, 3)
                n = PARTS[p][1]
                out = out_ps[e % 2][:, :]
                if p == 0:
                    wait_reuse(pe, scaled_done, nth(EXPERTS, c, e - 2))
                pe.wait_ge(lo_done, nth(STEPS, c, j))
                hi, lo = hid_hi[j % 4][0:n, :], hid_lo[j % 4][0:n, :]
                pe.matmul(out, wdn(S.whi, e, p, n), hi, start=(p == 0), stop=False)
                pe.matmul(out, wdn(S.whi, e, p, n), lo, start=False, stop=False)
                pe.matmul(out, wdn(S.wlo, e, p, n), hi, start=False, stop=(p == 2)).then_inc(down_done, 1)

            def broadcast(c, e):
                pe.wait_ge(cte_done, nth(1, c, 0))
                wait_reuse(pe, cb_done, nth(EXPERTS, c, e - 1))
                pe.matmul(bc_ps[:, :], S.sel[:, e * P:(e + 1) * P], comb_t[:, chunks.tokens(c)],
                          start=True, stop=True).then_inc(bc_done, 1)

            def result(c):
                pe.wait_ge(acc_done, nth(EXPERTS - 1, c, EXPERTS - 2))
                for t in range(CT):
                    mm = pe.transpose(misc_ps[:, t * P:(t + 1) * P], acc[:, t * P:(t + 1) * P], S.ident[:, :])
                mm.then_inc(fin_done, 1)

            def body(c):
                for j in range(STEPS):
                    if j % 3 == 0:
                        broadcast(c, j // 3)
                    up_and_gate(c, j)
                    if j >= LAG:
                        down(c, j - LAG)
                    elif not chunks.is_first(c):
                        down(c - 1, STEPS + j - LAG)
                    if j == 7 and not chunks.is_first(c):
                        result(c - 1)
                    if not chunks.is_last(c):
                        if j == 9:
                            transposes(c + 1)
                        if j == 12:
                            logits(c + 1)
                        if j == 14:
                            logit_transposes(c + 1)
                        if j == 20:
                            comb_transposes(c + 1)

            transposes(chunks.first)
            logits(chunks.first)
            logit_transposes(chunks.first)
            comb_transposes(chunks.first)
            chunks.each(pe, body)
            for j in range(STEPS - LAG, STEPS):
                down(chunks.last, j)
            result(chunks.last)

        @block.scalar
        def _(act):
            def split_norm(c):
                act.wait_ge(xt_done, nth(1, c, 0))
                act.activation(norm_hi[:, chunks.tokens(c)], misc_ps[:, :], ACT.Copy,
                               scale=S.vec[:, NORM_W:NORM_W + 1]).then_inc(nhi_done, 1)

            def keep_logits(c):
                act.wait_ge(lgt_done, nth(1, c, 0))
                act.activation(lgt[:, :], misc_ps[:, :], ACT.Copy).then_inc(lge_done, 1)

            def weights_tanh(c):
                act.wait_ge(diff_done, nth(1, c, 0))
                act.activation(tanh[:, :, 0], diff[:, :, 0], ACT.Tanh, scale=0.5).then_inc(tanh_done, 1)

            def keep_comb(c):
                act.wait_ge(ct_done, nth(1, c, 0))
                act.activation(comb_t[:, chunks.tokens(c)], misc_ps[0:P, :], ACT.Copy)\
                    .then_inc(cte_done, 1)

            def gate(c, j):
                n = PARTS[j % 3][1]
                act.wait_ge(gate_done, nth(STEPS, c, j))
                wait_reuse(act, hid_done, nth(STEPS, c, j - 2))
                act.activation(silu[j % 2][0:n, :], gate_ps[j % 2][0:n, :], ACT.Silu).then_inc(silu_done, 1)

            def high(c, j):
                n = PARTS[j % 3][1]
                act.wait_ge(hid_done, nth(STEPS, c, j))
                wait_reuse(act, down_done, nth(STEPS, c, j - 4))
                act.activation(hid_hi[j % 4][0:n, :], hid[j % 3][0:n, :], ACT.Copy).then_inc(hi_done, 1)

            def keep_broadcast(c, e):
                act.wait_ge(bc_done, nth(EXPERTS, c, e))
                wait_reuse(act, scaled_done, nth(EXPERTS, c, e - 2))
                act.activation(cb[e % 2][:, :], bc_ps[:, :], ACT.Copy).then_inc(cb_done, 1)

            def body(c):
                for j in range(STEPS):
                    gate(c, j)
                    if j > 0:
                        high(c, j - 1)
                    elif not chunks.is_first(c):
                        high(c - 1, STEPS - 1)
                    if j % 3 == 1:
                        keep_broadcast(c, j // 3)
                    if not chunks.is_last(c):
                        if j == 10:
                            split_norm(c + 1)
                        if j == 12:
                            keep_logits(c + 1)
                        if j == 17:
                            weights_tanh(c + 1)
                        if j == 20:
                            keep_comb(c + 1)

            split_norm(chunks.first)
            keep_logits(chunks.first)
            weights_tanh(chunks.first)
            keep_comb(chunks.first)
            chunks.each(act, body)
            high(chunks.last, STEPS - 1)

        @block.vector
        def _(dve):
            def statistics(c):
                for t in range(CT):
                    dve.bn_stats(st[:, t, :], S.x[:, chunks.tile(c, t), :]).then_inc(st_done, 1)
                hold(dve, S, st_done, nth(CT, c, CT - 1))
                for t in range(CT):
                    dve.bn_aggr(mv[:, t, :], st[:, t, :]).then_inc(mv_done, 1)

            def apply_norm(c):
                dve.wait_ge(rstd_done, nth(1, c, 0))
                for t in range(CT):
                    dve.tensor_scalar(xn[:, t, :], S.x[:, chunks.tile(c, t), :], mv[:, t, 0:1], rstd[:, t:t + 1],
                                      ALU.subtract, ALU.mult).then_inc(xn_done, 1)
                dve.wait_ge(xn_done, nth(CT, c, CT - 1))
                wait_reuse(dve, xt_done, c)
                for t in range(CT):
                    dve.tensor_scalar(nr[:, t, :], xn[:, t, :], rms[:, t:t + 1], None, ALU.mult).then_inc(nr_done, 1)
                x = S.x[:, chunks.tiles(c), :]
                dve.scalar_tensor_tensor(x, xn[:, :, :], 0.5, x, ALU.mult, ALU.add).then_inc(base_done, 1)

            def low_norm(c):
                dve.wait_ge(nhi_done, nth(1, c, 0))
                tok = chunks.tokens(c)
                dve.scalar_tensor_tensor(norm_lo[:, tok], misc_ps[:, :], S.vec[:, NORM_W:NORM_W + 1],
                                         norm_hi[:, tok].bitcast(FP32), ALU.mult, ALU.subtract).then_inc(nlo_done, 1)

            def all8(a):
                return a[:, :, :].to_broadcast([P, CT, EXPERTS])

            def route(c):
                ch = Chain(dve, route_order, 12, c)
                dve.wait_ge(lg_done, nth(1, c, 0))
                ch.link(dve.tensor_copy(lg[:, :, :], misc_ps[:, :].rearrange("p (t e) -> p t e", t=CT)[:, :, 0:EXPERTS]))
                for logit, top, key, one in ((lg, top1, key1, one1), (lg2, top2, key2, one2)):
                    ch.link(dve.reduce_max(top[:, :, 0], logit[:, :, :], axis=AX.X))
                    ch.link(dve.tensor_tensor(eq[:, :, :], logit[:, :, :], all8(top), ALU.is_equal))
                    ch.link(dve.tensor_tensor(eq[:, :, :], eq[:, :, :], S.rev3, ALU.mult))
                    ch.link(dve.reduce_max(key[:, :, 0], eq[:, :, :], axis=AX.X))
                    ch.link(dve.tensor_tensor(one[:, :, :], eq[:, :, :], all8(key), ALU.is_equal))
                    if logit is lg:
                        ch.link(dve.scalar_tensor_tensor(lg2[:, :, :], one1[:, :, :], NEG_BIG, lg[:, :, :],
                                                         ALU.mult, ALU.add))
                dve.tensor_tensor(diff[:, :, :], top2[:, :, :], top1[:, :, :], ALU.subtract).then_inc(diff_done, 1)
                ch.end()

            def combine(c):
                ch = Chain(dve, comb_order, 6, c)
                dve.wait_ge(tanh_done, nth(1, c, 0))
                ch.link(dve.tensor_scalar(w2[:, :, :], tanh[:, :, :], 0.5, 0.5, ALU.mult, ALU.add))
                ch.link(dve.tensor_scalar(w1[:, :, :], tanh[:, :, :], -0.5, 0.5, ALU.mult, ALU.add))
                ch.link(dve.tensor_tensor(one1[:, :, :], one1[:, :, :], all8(w1), ALU.mult))
                ch.link(dve.tensor_tensor(one2[:, :, :], one2[:, :, :], all8(w2), ALU.mult))
                ch.link(dve.tensor_tensor(lg[:, :, :], one1[:, :, :], one2[:, :, :], ALU.add))
                if not chunks.is_first(c):
                    dve.wait_ge(ct_done, c)
                ch.link(dve.tensor_copy(S.combp[:, :, 0:EXPERTS].bitcast(F32R), lg[:, :, :]))
                ch.end()
                dve.tensor_tensor(S.combp[:, :, LOW0:LOW0 + EXPERTS], lg[:, :, :], S.combp[:, :, 0:EXPERTS], ALU.subtract)\
                    .then_inc(comb_done, 1)

            def hidden(c, j):
                n = PARTS[j % 3][1]
                dve.wait_ge(up_done, nth(STEPS, c, j))
                dve.wait_ge(silu_done, nth(STEPS, c, j))
                wait_reuse(dve, lo_done, nth(STEPS, c, j - 3))
                dve.tensor_tensor(hid[j % 3][0:n, :], up_ps[j % 2][0:n, :], silu[j % 2][0:n, :], ALU.mult)\
                    .then_inc(hid_done, 1)

            def low(c, j):
                n = PARTS[j % 3][1]
                dve.wait_ge(hi_done, nth(STEPS, c, j))
                dve.tensor_tensor(hid_lo[j % 4][0:n, :], hid[j % 3][0:n, :], hid_hi[j % 4][0:n, :].bitcast(FP32),
                                  ALU.subtract).then_inc(lo_done, 1)

            def scale(c, e):
                dve.wait_ge(down_done, nth(STEPS, c, 3 * e + 2))
                dve.wait_ge(cb_done, nth(EXPERTS, c, e))
                wait_reuse(dve, acc_done, nth(EXPERTS - 1, c, {0: -2, 1: -1, 2: 0}.get(e, max(0, e - 3))))
                dve.tensor_tensor(scaled[e % 2][:, :], out_ps[e % 2][:, :], cb[e % 2][:, :], ALU.mult)\
                    .then_inc(scaled_done, 1)

            def update(c):
                dve.wait_ge(fin_done, nth(1, c, 0))
                dve.wait_ge(base_done, nth(1, c, 0))
                x = S.x[:, chunks.tiles(c), :]
                dve.scalar_tensor_tensor(x, misc_ps[:, :].rearrange("p (t d) -> p t d", d=D), S.half_alpha[:, 0:1], x,
                                         ALU.mult, ALU.add).then_inc(x_done, 1)

            def body(c):
                for j in range(STEPS):
                    hidden(c, j)
                    if j > 0:
                        low(c, j - 1)
                    elif not chunks.is_first(c):
                        low(c - 1, STEPS - 1)
                    if j % 3 == 0:
                        e = j // 3 - 2
                        if e >= 0:
                            scale(c, e)
                        elif not chunks.is_first(c):
                            scale(c - 1, EXPERTS + e)
                    if j == 8 and not chunks.is_first(c):
                        update(c - 1)
                    if not chunks.is_last(c):
                        if j == 1:
                            statistics(c + 1)
                        if j == 6:
                            apply_norm(c + 1)
                        if j == 10:
                            low_norm(c + 1)
                        if j == 15:
                            route(c + 1)
                        if j == 18:
                            combine(c + 1)

            statistics(chunks.first)
            apply_norm(chunks.first)
            low_norm(chunks.first)
            route(chunks.first)
            combine(chunks.first)
            chunks.each(dve, body)
            low(chunks.last, STEPS - 1)
            scale(chunks.last, EXPERTS - 2)
            scale(chunks.last, EXPERTS - 1)
            update(chunks.last)

        @block.gpsimd
        def _(pool):
            def rstds(c):
                ch = Chain(pool, rstd_order, 5, c)
                var, half = mv[:, :, 1], S.minus_half[:, 0:CT]
                pool.wait_ge(mv_done, nth(CT, c, CT - 1))
                ch.link(pool.tensor_tensor(tmp[:, :], var, S.eps_ln[:, 0:CT], ALU.add))
                ch.link(pool.tensor_tensor(rstd[:, :], tmp[:, :], half, ALU.pow))
                ch.link(pool.tensor_tensor(tmp[:, :], var, rstd[:, :], ALU.mult))
                ch.link(pool.tensor_tensor(tmp[:, :], tmp[:, :], rstd[:, :], ALU.mult))
                ch.link(pool.tensor_tensor(tmp[:, :], tmp[:, :], S.eps_rms[:, 0:CT], ALU.add))
                pool.tensor_tensor(rms[:, :], tmp[:, :], half, ALU.pow).then_inc(rstd_done, 1)
                ch.end()

            def total(c, e):
                pool.wait_ge(scaled_done, nth(EXPERTS, c, e))
                if e == 1:
                    wait_reuse(pool, fin_done, c)
                else:
                    pool.wait_ge(acc_done, nth(EXPERTS - 1, c, e - 2))
                pool.tensor_tensor(acc[:, :], scaled[0][:, :] if e == 1 else acc[:, :], scaled[e % 2][:, :], ALU.add)\
                    .then_inc(acc_done, 1)

            def body(c):
                if not chunks.is_last(c):
                    rstds(c + 1)
                for e in range(1, EXPERTS):
                    total(c, e)

            rstds(chunks.first)
            chunks.each(pool, body)


def three(pe, out, whi, wlo, hi, lo):
    pe.matmul(out, whi, hi, start=True, stop=False)
    pe.matmul(out, whi, lo, start=False, stop=False)
    return pe.matmul(out, wlo, hi, start=False, stop=True)


def columns(S, a, n=D):
    return S.whi[:, a:a + n], S.wlo[:, a:a + n]


def attention(nc, S, name):
    with ExitStack() as ctx:
        def sb(n, shape, dt=FP32):
            return ctx.enter_context(nc.sbuf_tensor(f"{name}_{n}", shape, dt))

        st, mv = sb("st", [P, BT, 6]), sb("mv", [P, BT, 2])
        rstd, tmp = sb("rstd", [P, BT]), sb("tmp", [P, BT])
        xn = sb("xn", [P, BT, D])
        t_x, t_hi, t_lo = sb("t_x", [P, SEQ]), sb("t_hi", [P, SEQ], F32R), sb("t_lo", [P, SEQ], F32R)
        low_rank = sb("low_rank", [96, 2 * SEQ], F32R)
        q_part, k_part = sb("q_part", [P, SEQ], F32R), sb("k_part", [P, SEQ], F32R)
        q_st, k_st = sb("q_st", [P, GROUPS, SEQ], F32R), sb("k_st", [P, SEQ], F32R)
        k_head = sb("k_head", [P, GROUPS, SLOTS, SEQ], F32R)
        q_max = sb("q_max", [P, GROUPS, SEQ], F32R)
        block_max = sb("block_max", [P, HEADS, 3])
        max_rows = sb("max_rows", [P, BT, HEADS, 32])
        probs = [sb(f"probs{i}", [P, 2, 3 * P]) for i in range(4)]
        value_in = sb("value_in", [P, BT, HEADS, DK])
        values = sb("values", [P, BT, HEADS, 32])
        heads_t = [sb(f"heads_t{i}", [P, BT, P]) for i in range(2)]
        rsum, heads = sb("rsum", [P, BT, HEADS, 1]), sb("heads", [P, BT, HEADS, DK])
        h_hi, h_lo = sb("h_hi", [P, SEQ], F32R), sb("h_lo", [P, SEQ], F32R)

        def two_banks(i):
            a = S.psum[:, i * 512:(i + 2) * 512].rearrange("p (s c) -> p s c", s=2)
            return a[:, :, 0:3 * P], a[:, :, 3 * P:]

        score_t_ps, extra_t_ps = zip(two_banks(0), two_banks(2))
        score_ps, extra_ps = two_banks(4)
        head_ps = rank_ps = S.bank[6]
        qk_ps = S.bank[7]

        names = ("st mv eps rstd xn t thi tx tlo c chi clo vmm vs v qk tqk kq ka kp s max both mhi mneg mt q2 sc exp pv ot ott rs "
                 "at att ahi alo wo x set").split()
        N = {n: S.sems.enter_context(nc.semaphore(f"{name}_{n}")) for n in names}
        block = ctx.enter_context(nc.Block())
        later, earlier = S.mask[:, 0:3 * P], S.mask[:, 3 * P:]
        inv_sqrt = float(DK) ** -0.5

        def slot(j):
            return slice(32 * j, 32 * j + 32)

        def pair(u):
            return u // 2, (2 * (u % 2), 2 * (u % 2) + 1)

        def has(b):
            return not isinstance(b, int) or 0 <= b < BATCH

        def behind(b, u):
            return (b + 1, u - BEHIND) if u >= BEHIND else (b, u - BEHIND + PAIRS)

        def weighed(b, u):
            return (b, (u - 3) // 2) if u >= 3 else (b - 1, GROUPS - 1)

        def shifted(b, u):
            return (b + 1, 0) if u == 6 else (b, u // 2 + 1)

        def over_batches(eng, body):
            for b in range(-2, 1):
                body(b)
            with eng.Fori(1, BATCH - 2) as b:
                body(b)
            for b in range(BATCH - 2, BATCH + 1):
                body(b)

        @block.tensor
        def _(pe):
            def transposes(b):
                pe.wait_ge(N["xn"], nth(BT, b, BT - 1))
                for t in range(BT):
                    mm = pe.transpose(extra_t_ps[0][:, t, :], xn[:, t, :], S.ident[:, :])
                mm.then_inc(N["t"], 1)

            def ranks(b):
                pe.wait_ge(N["tlo"], nth(1, b, 0))
                wait_reuse(pe, N["at"], nth(GROUPS, b - 2, 1))
                three(pe, rank_ps[0:96, 0:SEQ], *columns(S, CQ0, 96), t_hi[:, :], t_lo[:, :])
                three(pe, rank_ps[0:96, SEQ:], *columns(S, CKV0, 96), t_hi[:, :], t_lo[:, :]).then_inc(N["c"], 1)

            def value(b):
                pe.wait_ge(N["clo"], nth(1, b, 0))
                for t in range(BT):
                    mm = pe.matmul(extra_t_ps[0][:, t, :], low_rank[:, SEQ + t * P:SEQ + (t + 1) * P],
                                   S.up[:, UV0:UCOLS], start=True, stop=True)
                mm.then_inc(N["vmm"], 1)

            def project(b, g):
                pe.wait_ge(N["clo"], nth(1, b, 0))
                wait_reuse(pe, N["kq"], nth(GROUPS, b, g - 1))
                pe.matmul(qk_ps[:, 0:SEQ], S.up[:, UQ0 + g * P:UQ0 + (g + 1) * P], low_rank[:, 0:SEQ],
                          start=True, stop=True)
                pe.matmul(qk_ps[:, SEQ:], S.up[:, UK0 + g * P:UK0 + (g + 1) * P], low_rank[:, SEQ:],
                          start=True, stop=True).then_inc(N["qk"], 1)

            def scores(b, u):
                g, js = pair(u)
                pe.wait_ge(N["ka"], nth(GROUPS, b, g))
                pe.wait_ge(N["kp"], nth(2 * GROUPS, b, 2 * g + 1))
                for s in range(2):
                    pe.matmul(score_ps[:, s, :], S.ident_bf[:, :], later, start=True, stop=False)
                for s, j in enumerate(js):
                    pe.matmul(score_ps[:, s, 0:SEQ], q_st[:, g, P:SEQ], k_head[:, g, j, :], start=False, stop=False)
                for s, j in enumerate(js):
                    mm = pe.matmul(score_ps[:, s, SEQ:], q_st[:, g, 0:P], k_head[:, g, j, 0:P],
                                   start=False, stop=True)
                mm.then_inc(N["s"], 1)

            def max_transposes(b, g):
                pe.wait_ge(N["mneg"], nth(GROUPS, b, g))
                for i in range(BT):
                    mm = pe.transpose(extra_ps[:, i, :], max_rows[:, 1 - i, g * SLOTS:(g + 1) * SLOTS, :], S.ident[:, :])
                mm.then_inc(N["mt"], 1)

            def scores_t(b, u):
                g, js = pair(u)
                pe.wait_ge(N["q2"], nth(GROUPS, b, g))
                out = score_t_ps[u % 2]
                for s in range(2):
                    pe.matmul(out[:, s, :], S.ident_bf[:, :], earlier, start=True, stop=False)
                for s, j in enumerate(js):
                    pe.matmul(out[:, s, 0:SEQ], k_head[:, g, j, 0:P], q_max[:, g, :], start=False, stop=False)
                for s, j in enumerate(js):
                    mm = pe.matmul(out[:, s, SEQ:], k_head[:, g, j, P:SEQ], q_max[:, g, 0:P], start=False, stop=True)
                mm.then_inc(N["sc"], 1)

            def weigh(b, g):
                pe.wait_ge(N["exp"], nth(PAIRS, b, 2 * g + 1))
                pe.wait_ge(N["v"], nth(1, b, 0))
                out = extra_t_ps[1]

                def product(i, t, at, start, stop):
                    for j in range(SLOTS):
                        p = probs[(2 * g + j // 2) % 4]
                        mm = pe.matmul(out[slot(j), i, :], values[:, t, g * SLOTS + j, :], p[:, j % 2, at:at + P],
                                       start=start, stop=stop)
                    return mm

                product(0, 0, 0, True, False)
                product(0, 1, 2 * P, False, True)
                product(1, 0, P, True, True).then_inc(N["pv"], 1)

            def head_transposes(b, g):
                pe.wait_ge(N["ot"], nth(GROUPS, b, g))
                wait_reuse(pe, N["at"], nth(GROUPS, b, g - 1))
                for t in range(BT):
                    mm = pe.transpose(head_ps[:, t * P:(t + 1) * P], heads_t[g % 2][:, 1 - t, :], S.ident[:, :])
                mm.then_inc(N["ott"], 1)

            def back_transposes(b):
                pe.wait_ge(N["at"], nth(GROUPS, b, GROUPS - 1))
                for t in range(BT):
                    mm = pe.transpose(extra_ps[:, t, :], heads[:, t, :, :], S.ident[:, :])
                mm.then_inc(N["att"], 1)

            def output(b):
                pe.wait_ge(N["alo"], nth(1, b, 0))
                hi, lo = columns(S, WO0)
                for t in range(BT):
                    tok = slice(t * P, (t + 1) * P)
                    mm = three(pe, extra_ps[:, t, :], h_hi[:, tok], h_lo[:, tok], hi, lo)
                mm.then_inc(N["wo"], 1)

            def score_t_banks_read(b, u):
                before = (b, u - 2) if u >= 2 else (b - 1, u - 2 + PAIRS)
                if has(before[0]):
                    wait_reuse(pe, N["exp"], nth(PAIRS, *before))
                if u % 2 == 1:
                    wb, wg = weighed(*before)
                    if has(wb):
                        wait_reuse(pe, N["ot"], nth(GROUPS, wb, wg))
                elif u == 4 and has(b + 1):
                    pe.wait_ge(N["vs"], nth(1, b + 1, 0))
                elif u == 6 and has(b + 2):
                    pe.wait_ge(N["tx"], nth(1, b + 2, 0))

            def score_banks_read(b, u):
                sb, su = behind(b, u - 1) if u > 0 else behind(b - 1, PAIRS - 1)
                if has(sb):
                    wait_reuse(pe, N["max"], nth(PAIRS, sb, su))
                if u % 2 == 1:
                    mb, mg = shifted(b, u - 1)
                    if has(mb):
                        wait_reuse(pe, N["q2"], nth(GROUPS, mb, mg))
                elif u in (4, 6) and has(b - 1):
                    pe.wait_ge(N["alo"] if u == 4 else N["x"], nth(1, b - 1, 0))

            def body(b):
                for u in range(PAIRS):
                    score_t_banks_read(b, u)
                    if u == 2 and has(b + 1):
                        value(b + 1)
                    if u == 4 and has(b + 2):
                        transposes(b + 2)
                    if u % 2 == 1 and has(weighed(b, u)[0]):
                        weigh(*weighed(b, u))
                    if has(b):
                        scores_t(b, u)
                    if u % 2 == 0:
                        done = weighed(b, u - 1) if u > 0 else weighed(b - 1, PAIRS - 1)
                        if has(done[0]):
                            if u == 0 and has(b + 1):
                                pe.wait_ge(N["clo"], nth(1, b + 1, 0))
                            head_transposes(*done)
                    if u == 7 and has(b + 2):
                        ranks(b + 2)
                    score_banks_read(b, u)
                    if u % 2 == 0 and has(shifted(b, u)[0]):
                        max_transposes(*shifted(b, u))
                    if u == 3 and has(b - 1):
                        back_transposes(b - 1)
                    if u == 5 and has(b - 1):
                        output(b - 1)
                    if has(behind(b, u)[0]):
                        scores(*behind(b, u))
                    if u % 2 == 0 and has(b + 1):
                        project(b + 1, u // 2)

            over_batches(pe, body)

        @block.scalar
        def _(act):
            def keep_tokens(b):
                act.wait_ge(N["t"], nth(1, b, 0))
                wait_reuse(act, N["c"], b)
                act.activation(t_hi[:, :].rearrange("p (t q) -> p t q", t=BT), extra_t_ps[0], ACT.Copy).then_inc(N["thi"], 1)
                wait_reuse(act, N["tlo"], b)
                act.activation(t_x[:, :].rearrange("p (t q) -> p t q", t=BT), extra_t_ps[0], ACT.Copy).then_inc(N["tx"], 1)

            def split_ranks(b):
                act.wait_ge(N["c"], nth(1, b, 0))
                wait_reuse(act, N["vmm"], b)
                wait_reuse(act, N["qk"], GROUPS * b)
                act.activation(low_rank[:, :], rank_ps[0:96, :], ACT.Copy).then_inc(N["chi"], 1)

            def keep_value(b):
                act.wait_ge(N["vmm"], nth(1, b, 0))
                wait_reuse(act, N["v"], b)
                act.activation(value_in[:, :, :, :].rearrange("p t h d -> p t (h d)"), extra_t_ps[0], ACT.Copy)\
                    .then_inc(N["vs"], 1)

            def parts(b, g):
                act.wait_ge(N["qk"], nth(GROUPS, b, g))
                wait_reuse(act, N["kq"], nth(GROUPS, b, g - 1))
                act.activation(q_part[:, :], qk_ps[:, 0:SEQ], ACT.Identity, scale=S.vec[:, Q_SIGN:Q_SIGN + 1])\
                    .then_inc(N["tqk"], 1)
                act.activation(k_part[:, :], qk_ps[:, SEQ:], ACT.Identity, scale=S.vec[:, K_SIGN:K_SIGN + 1],
                               bias=S.vec[:, K_ONES:K_ONES + 1]).then_inc(N["tqk"], 1)

            def exps(b, u):
                act.wait_ge(N["sc"], nth(PAIRS, b, u))
                wait_reuse(act, N["pv"], nth(GROUPS, b, u // 2 - 2))
                act.activation(probs[u % 4][:, :, :], score_t_ps[u % 2], ACT.Exp, scale=inv_sqrt).then_inc(N["exp"], 1)

            def place_keys(b, g):
                act.wait_ge(N["kq"], nth(GROUPS, b, g))
                if has(b - 1):
                    act.wait_ge(N["sc"], nth(PAIRS, b - 1, 2 * g + 1))
                for j in (0, 1):
                    mm = act.activation(k_head[slot(j), g, j, :], k_st[slot(j), :].bitcast(FP32), ACT.Copy)
                mm.then_inc(N["ka"], 1)

            def keep_heads(b, g):
                act.wait_ge(N["pv"], nth(GROUPS, b, g))
                wait_reuse(act, N["ott"], nth(GROUPS, b, g - 2))
                act.activation(heads_t[g % 2][:, :, :], extra_t_ps[1], ACT.Copy).then_inc(N["ot"], 1)

            def body(b):
                for u in range(PAIRS):
                    if u % 2 == 1 and has(weighed(b, u)[0]):
                        if has(b):
                            act.wait_ge(N["sc"], nth(PAIRS, b, u))
                        keep_heads(*weighed(b, u))
                    if has(b):
                        exps(b, u)
                    if u == 2 and has(b + 1):
                        keep_value(b + 1)
                    if u == 4 and has(b + 2):
                        keep_tokens(b + 2)
                    if u % 2 == 0 and has(b + 1):
                        parts(b + 1, u // 2)
                    if u % 2 == 1 and has(b + 1):
                        place_keys(b + 1, u // 2)
                    if u == 7 and has(b + 2):
                        split_ranks(b + 2)

            over_batches(act, body)

        @block.vector
        def _(dve):
            def statistics(b):
                for t in range(BT):
                    dve.bn_stats(st[:, t, :], S.x[:, bass.ds(b * BT + t, 1), :]).then_inc(N["st"], 1)
                hold(dve, S, N["st"], nth(BT, b, BT - 1))
                for t in range(BT):
                    dve.bn_aggr(mv[:, t, :], st[:, t, :]).then_inc(N["mv"], 1)

            def apply_norm(b):
                dve.wait_ge(N["rstd"], nth(1, b, 0))
                wait_reuse(dve, N["t"], b)
                for t in range(BT):
                    dve.tensor_scalar(xn[:, t, :], S.x[:, bass.ds(b * BT + t, 1), :], mv[:, t, 0:1], rstd[:, t:t + 1],
                                      ALU.subtract, ALU.mult).then_inc(N["xn"], 1)

            def low_ranks(b):
                dve.wait_ge(N["chi"], nth(1, b, 0))
                dve.tensor_tensor(low_rank[DC:2 * DC, :], rank_ps[DC:2 * DC, :], low_rank[DC:2 * DC, :].bitcast(FP32),
                                  ALU.subtract).then_inc(N["clo"], 1)

            def stack(b, g):
                dve.wait_ge(N["tqk"], nth(2 * GROUPS, b, 2 * g + 1))
                wait_reuse(dve, N["q2"], nth(GROUPS, b - 1, g))
                wait_reuse(dve, N["ka"], nth(GROUPS, b, g - 1))
                wait_reuse(dve, N["kp"], nth(2 * GROUPS, b, 2 * g - 1))
                dve.scalar_tensor_tensor(q_st[:, g, :], qk_ps[:, 0:SEQ], S.vec[:, Q_LOW:Q_LOW + 1],
                                         q_part[:, :].bitcast(FP32), ALU.mult, ALU.add)
                dve.scalar_tensor_tensor(k_st[:, :], qk_ps[:, SEQ:], S.vec[:, K_LOW:K_LOW + 1],
                                         k_part[:, :].bitcast(FP32), ALU.mult, ALU.add).then_inc(N["kq"], 1)

            def maxima(b, u):
                dve.wait_ge(N["s"], nth(PAIRS, b, u))
                wait_reuse(dve, N["mneg"], nth(GROUPS, b - 1, u // 2))
                dve.reduce_max(block_max[:, 2 * u:2 * u + 2, :], score_ps.rearrange("p s (k q) -> p s k q", q=P),
                               axis=AX.X, negate=True).then_inc(N["max"], 1)

            def split_maxima(b, g):
                h = slice(g * SLOTS, (g + 1) * SLOTS)
                dve.wait_ge(N["max"], nth(PAIRS, b, 2 * g + 1))
                wait_reuse(dve, N["mt"], nth(GROUPS, b - 1, g))
                dve.tensor_tensor(block_max[:, h, 1], block_max[:, h, 0], block_max[:, h, 1], ALU.min).then_inc(N["both"], 1)
                dve.wait_ge(N["both"], nth(GROUPS, b, g))
                hi = max_rows[:, :, h, MAX_ROW]
                both = block_max[:, h, 2:0:-1].rearrange("p h t -> p t h")
                dve.tensor_copy(hi.bitcast(F32R), both).then_inc(N["mhi"], 1)
                dve.wait_ge(N["mhi"], nth(GROUPS, b, g))
                dve.tensor_tensor(max_rows[:, :, h, MAX_ROW + 1], both, hi, ALU.subtract).then_inc(N["mneg"], 1)

            def add_maxima(b, g):
                dve.wait_ge(N["mt"], nth(GROUPS, b, g))
                for i in range(BT):
                    q = slice((1 - i) * P, (2 - i) * P)
                    mm = dve.tensor_tensor(q_max[:, g, i * P:(i + 1) * P], extra_ps[:, i, :], q_st[:, g, q].bitcast(FP32), ALU.add)
                mm.then_inc(N["q2"], 1)

            def divide(b, g):
                h = slice(g * SLOTS, (g + 1) * SLOTS)
                out = head_ps[:, 0:SEQ].rearrange("p (t h c) -> p t h c", t=BT, h=SLOTS)
                dve.wait_ge(N["ott"], nth(GROUPS, b, g))
                wait_reuse(dve, N["at"], nth(GROUPS, b, g - 1))
                dve.reciprocal(rsum[:, :, h, :], out[:, :, :, DK:DK + 1]).then_inc(N["rs"], 1)
                dve.wait_ge(N["rs"], nth(GROUPS, b, g))
                if g == 0:
                    wait_reuse(dve, N["att"], b)
                for t in range(BT):
                    mm = dve.tensor_tensor(heads[:, t, h, :], out[:, t, :, 0:DK],
                                           rsum[:, t, h, :].to_broadcast([P, SLOTS, DK]), ALU.mult)
                mm.then_inc(N["at"], 1)

            def split_heads(b):
                dve.wait_ge(N["att"], nth(1, b, 0))
                hi, lo = (a[:, :].rearrange("p (t q) -> p t q", t=BT) for a in (h_hi, h_lo))
                dve.tensor_copy(hi, extra_ps).then_inc(N["ahi"], 1)
                dve.wait_ge(N["ahi"], nth(1, b, 0))
                dve.tensor_tensor(lo, extra_ps, hi.bitcast(FP32), ALU.subtract).then_inc(N["alo"], 1)

            def update(b):
                dve.wait_ge(N["wo"], nth(1, b, 0))
                x = S.x[:, bass.ds(b * BT, BT), :]
                dve.tensor_tensor(x, extra_ps, x, ALU.add).then_inc(N["x"], 1)

            def body(b):
                for u in range(PAIRS):
                    sb, su = behind(b, u)
                    if u == 0 and has(b + 2):
                        statistics(b + 2)
                    if u % 2 == 1 and has(b + 1):
                        stack(b + 1, u // 2)
                    if u % 2 == 0:
                        done = weighed(b, u - 1) if u > 0 else weighed(b - 1, PAIRS - 1)
                        if has(done[0]):
                            divide(*done)
                    if u == 3 and has(b + 2):
                        apply_norm(b + 2)
                    if has(sb):
                        dve.wait_ge(N["s"], nth(PAIRS, sb, su))
                    if u % 2 == 0 and has(shifted(b, u)[0]):
                        add_maxima(*shifted(b, u))
                    if u == 3 and has(b - 1):
                        split_heads(b - 1)
                    if u == 5 and has(b - 1):
                        update(b - 1)
                    if has(sb):
                        maxima(sb, su)
                        if su % 2 == 1:
                            split_maxima(sb, su // 2)
                    if u == 7 and has(b + 2):
                        low_ranks(b + 2)

            dve.memset(max_rows[:, :, :, :], 0.0)
            over_batches(dve, body)

        @block.gpsimd
        def _(pool):
            def power(b):
                pool.wait_ge(N["mv"], nth(BT, b, BT - 1))
                pool.tensor_tensor(tmp[:, :], mv[:, :, 1], S.eps_ln[:, 0:BT], ALU.add).then_inc(N["eps"], 1)
                pool.wait_ge(N["eps"], nth(1, b, 0))
                pool.tensor_tensor(rstd[:, :], tmp[:, :], S.minus_half[:, 0:BT], ALU.pow).then_inc(N["rstd"], 1)
                hold(pool, S, N["rstd"], nth(1, b, 0))

            def place_values(b):
                hold(pool, S, N["vs"], nth(1, b, 0))
                if has(b - 1):
                    hold(pool, S, N["pv"], nth(GROUPS, b - 1, GROUPS - 1))
                pool.tensor_copy(values[:, :, :, 0:DK], value_in[:, :, :, :]).then_inc(N["v"], 1)
                hold(pool, S, N["v"], nth(1, b, 0))

            def place_keys(b, g):
                hold(pool, S, N["kq"], nth(GROUPS, b, g))
                if has(b - 1):
                    hold(pool, S, N["sc"], nth(PAIRS, b - 1, 2 * g + 1))
                for i, j in enumerate((2, 3)):
                    pool.tensor_copy(k_head[slot(j), g, j, :], k_st[slot(j), :]).then_inc(N["kp"], 1)
                    hold(pool, S, N["kp"], nth(2 * GROUPS, b, 2 * g + i))

            def low(b):
                pool.wait_ge(N["tx"], nth(1, b, 0))
                wait_reuse(pool, N["c"], b)
                pool.tensor_tensor(t_lo[:, :], t_x[:, :], t_hi[:, :].bitcast(FP32), ALU.subtract).then_inc(N["tlo"], 1)
                hold(pool, S, N["tlo"], nth(1, b, 0))

            def body(b):
                if has(b + 2):
                    power(b + 2)
                if has(b):
                    place_values(b)
                for g in range(GROUPS):
                    if has(b + 1):
                        place_keys(b + 1, g)
                    if g == 1 and has(b + 2):
                        low(b + 2)

            pool.memset(k_head[:, :, :, :].bitcast(FP32), 0.0)
            pool.memset(values[:, :, :, :], 0.0).then_inc(N["set"], 1)
            pool.wait_ge(N["set"], 1)
            pool.memset(values[:, :, :, DK:DK + 1], 1.0).then_inc(N["set"], 1)
            pool.wait_ge(N["set"], 2)
            over_batches(pool, body)


def rolls(nc, S, name, sems, start):
    with ExitStack() as ctx:
        def sb(n, shape, dt=FP32):
            return ctx.enter_context(nc.sbuf_tensor(f"{name}_{n}", shape, dt))

        def sem(n):
            if n not in sems:
                sems[n] = S.sems.enter_context(nc.semaphore(f"{name}_{n}"))
            return sems[n]

        NG = len(SHIFTS)
        xn = sb("xn", [P, CT, D])
        t_hi, t_lo = sb("t_hi", [P, CHUNK], F32R), sb("t_lo", [P, CHUNK], F32R)
        value = [sb(f"value{i}", [P, 2, SEQ + 2 * PAD]) for i in range(1)][0]
        gate = [sb(f"gate{i}", [P, CHUNK]) for i in range(3)]
        prod = [sb(f"prod{i}", [P, CHUNK]) for i in range(3)]
        acc = sb("acc", [P, CHUNK])
        st, mv = sb("st", [P, CT, 6]), sb("mv", [P, CT, 2])
        st2, mv2 = sb("st2", [P, CT, 6]), sb("mv2", [P, CT, 2])
        rstd, tmp, rstd2, tmp2 = (sb(n, [P, CT]) for n in ("rstd", "tmp", "rstd2", "tmp2"))
        on = sb("on", [P, CT, D])
        xt_ps, val_ps, sum_ps = S.bank[0], S.bank[1], S.bank[2]
        gate_ps = S.bank[3:6]

        st_done, mv_done, rstd_done, xn_done = sem("st_done"), sem("mv_done"), sem("rstd_done"), sem("xn_done")
        xt_done, hi_done, lo_done, val_done = sem("xt_done"), sem("hi_done"), sem("lo_done"), sem("val_done")
        vpad_done, gmm_done, gate_done, prod_done = sem("vpad_done"), sem("gmm_done"), sem("gate_done"), sem("prod_done")
        acc_done, sum_done, st2_done, mv2_done = sem("acc_done"), sem("sum_done"), sem("st2_done"), sem("mv2_done")
        rstd2_done, on_done, og_done, ob_done = sem("rstd2_done"), sem("on_done"), sem("og_done"), sem("ob_done")
        x_done, eps_done, eps2_done = sem("x_done"), sem("eps_done"), sem("eps2_done")
        chunks = Chunks(start)
        block = ctx.enter_context(nc.Block())

        @block.tensor
        def _(pe):
            def front(c):
                pe.wait_ge(xn_done, nth(CT, c, CT - 1))
                wait_reuse(pe, lo_done, c)
                for t in range(CT):
                    mm = pe.transpose(xt_ps[:, t * P:(t + 1) * P], xn[:, t, :], S.ident[:, :])
                mm.then_inc(xt_done, 1)

            def products(c):
                pe.wait_ge(lo_done, nth(1, c, 0))
                wait_reuse(pe, vpad_done, 3 * c)
                three(pe, val_ps[:, :], *columns(S, VALUE0), t_hi[:, :], t_lo[:, :]).then_inc(val_done, 1)
                for n in range(NG):
                    wait_reuse(pe, gate_done, nth(NG, c, n - 3))
                    three(pe, gate_ps[n % 3][:, :], *columns(S, GATES0 + n * D), t_hi[:, :], t_lo[:, :])\
                        .then_inc(gmm_done, 1)
                    if n == 1 and not chunks.is_first(c):
                        total(c - 1)

            def total(c):
                pe.wait_ge(acc_done, nth(NG - 1, c, NG - 2))
                wait_reuse(pe, on_done, nth(CT, c, -1))
                for t in range(CT):
                    mm = pe.transpose(sum_ps[:, t * P:(t + 1) * P], acc[:, t * P:(t + 1) * P], S.ident[:, :])
                mm.then_inc(sum_done, 1)

            def body(c):
                products(c)
                if not chunks.is_last(c):
                    front(c + 1)

            front(chunks.first)
            chunks.each(pe, body)
            total(chunks.last)

        @block.scalar
        def _(act):
            def front(c):
                act.wait_ge(xt_done, nth(1, c, 0))
                wait_reuse(act, gmm_done, NG * c)
                act.activation(t_hi[:, :], xt_ps[:, :], ACT.Copy).then_inc(hi_done, 1)

            def keep_value(c):
                act.wait_ge(val_done, nth(1, c, 0))
                wait_reuse(act, prod_done, NG * c)
                v = val_ps[:, :].rearrange("p (b s) -> p b s", b=2)
                act.activation(value[:, :, PAD:PAD + SEQ], v, ACT.Copy).then_inc(vpad_done, 1)
                act.activation(value[:, :, 0:PAD], v[:, :, SEQ - PAD:SEQ], ACT.Copy).then_inc(vpad_done, 1)
                act.activation(value[:, :, PAD + SEQ:], v[:, :, 0:PAD], ACT.Copy).then_inc(vpad_done, 1)

            def gates(c):
                for n in range(NG):
                    act.wait_ge(gmm_done, nth(NG, c, n))
                    wait_reuse(act, prod_done, nth(NG, c, n - 3))
                    act.activation(gate[n % 3][:, :], gate_ps[n % 3][:, :], ACT.Sigmoid).then_inc(gate_done, 1)

            def body(c):
                keep_value(c)
                gates(c)
                if not chunks.is_last(c):
                    front(c + 1)

            front(chunks.first)
            chunks.each(act, body)

        @block.vector
        def _(dve):
            def statistics(c):
                for t in range(CT):
                    dve.bn_stats(st[:, t, :], S.x[:, chunks.tile(c, t), :]).then_inc(st_done, 1)
                hold(dve, S, st_done, nth(CT, c, CT - 1))
                for t in range(CT):
                    dve.bn_aggr(mv[:, t, :], st[:, t, :]).then_inc(mv_done, 1)

            def apply_norm(c):
                dve.wait_ge(rstd_done, nth(1, c, 0))
                wait_reuse(dve, xt_done, c)
                for t in range(CT):
                    dve.tensor_scalar(xn[:, t, :], S.x[:, chunks.tile(c, t), :], mv[:, t, 0:1], rstd[:, t:t + 1],
                                      ALU.subtract, ALU.mult).then_inc(xn_done, 1)

            def low(c):
                dve.wait_ge(hi_done, nth(1, c, 0))
                dve.tensor_tensor(t_lo[:, :], xt_ps[:, :], t_hi[:, :].bitcast(FP32), ALU.subtract).then_inc(lo_done, 1)

            def roll(c, n):
                if n == 0:
                    dve.wait_ge(vpad_done, nth(3, c, 2))
                dve.wait_ge(gate_done, nth(NG, c, n))
                wait_reuse(dve, acc_done, nth(NG - 1, c, {0: -3, 1: -2, 2: -1}.get(n, max(0, n - 4))))
                at = PAD + SHIFTS[n]
                dve.tensor_tensor(prod[n % 3][:, :].rearrange("p (b s) -> p b s", b=2),
                                  gate[n % 3][:, :].rearrange("p (b s) -> p b s", b=2),
                                  value[:, :, at:at + SEQ], ALU.mult).then_inc(prod_done, 1)

            def sum_statistics(c):
                hold(dve, S, sum_done, nth(1, c, 0))
                for t in range(CT):
                    dve.bn_stats(st2[:, t, :], sum_ps[:, t * P:(t + 1) * P]).then_inc(st2_done, 1)
                hold(dve, S, st2_done, nth(CT, c, CT - 1))
                for t in range(CT):
                    dve.bn_aggr(mv2[:, t, :], st2[:, t, :]).then_inc(mv2_done, 1)

            def finish(c):
                dve.wait_ge(rstd2_done, nth(1, c, 0))
                wait_reuse(dve, x_done, c)
                for t in range(CT):
                    dve.tensor_scalar(on[:, t, :], sum_ps[:, t * P:(t + 1) * P], mv2[:, t, 0:1], rstd2[:, t:t + 1],
                                      ALU.subtract, ALU.mult).then_inc(on_done, 1)
                dve.wait_ge(on_done, nth(CT, c, CT - 1))
                dve.tensor_tensor(on[:, :, :], on[:, :, :], S.gamma[:, :].unsqueeze(1).to_broadcast([P, CT, D]),
                                  ALU.mult).then_inc(og_done, 1)

            def update(c):
                dve.wait_ge(ob_done, nth(1, c, 0))
                x = S.x[:, chunks.tiles(c), :]
                dve.tensor_tensor(x, x, on[:, :, :], ALU.add).then_inc(x_done, 1)

            def body(c):
                if not chunks.is_last(c):
                    statistics(c + 1)
                roll(c, 0)
                roll(c, 1)
                if not chunks.is_first(c):
                    sum_statistics(c - 1)
                roll(c, 2)
                roll(c, 3)
                if not chunks.is_last(c):
                    apply_norm(c + 1)
                if not chunks.is_first(c):
                    finish(c - 1)
                roll(c, 4)
                roll(c, 5)
                if not chunks.is_last(c):
                    pass
                roll(c, 6)
                if not chunks.is_first(c):
                    update(c - 1)
                roll(c, 7)
                roll(c, 8)
                if not chunks.is_last(c):
                    low(c + 1)

            statistics(chunks.first)
            apply_norm(chunks.first)
            low(chunks.first)
            chunks.each(dve, body)
            sum_statistics(chunks.last)
            finish(chunks.last)
            update(chunks.last)

        @block.gpsimd
        def _(pool):
            def power(c, mv, ready, tmp, eps_done, out, done):
                pool.wait_ge(ready, nth(CT, c, CT - 1))
                pool.tensor_tensor(tmp[:, :], mv[:, :, 1], S.eps_ln[:, 0:CT], ALU.add).then_inc(eps_done, 1)
                pool.wait_ge(eps_done, nth(1, c, 0))
                pool.tensor_tensor(out[:, :], tmp[:, :], S.minus_half[:, 0:CT], ALU.pow).then_inc(done, 1)

            def add(c, n):
                pool.wait_ge(prod_done, nth(NG, c, n))
                if n == 1:
                    wait_reuse(pool, sum_done, c)
                else:
                    pool.wait_ge(acc_done, nth(NG - 1, c, n - 2))
                pool.tensor_tensor(acc[:, :], prod[0][:, :] if n == 1 else acc[:, :], prod[n % 3][:, :], ALU.add)\
                    .then_inc(acc_done, 1)

            def add_beta(c):
                pool.wait_ge(og_done, nth(1, c, 0))
                pool.tensor_tensor(on[:, :, :], on[:, :, :], S.beta[:, :].unsqueeze(1).to_broadcast([P, CT, D]),
                                   ALU.add).then_inc(ob_done, 1)

            def body(c):
                if not chunks.is_last(c):
                    power(c + 1, mv, mv_done, tmp, eps_done, rstd, rstd_done)
                add(c, 1)
                if not chunks.is_first(c):
                    power(c - 1, mv2, mv2_done, tmp2, eps2_done, rstd2, rstd2_done)
                add(c, 2)
                add(c, 3)
                if not chunks.is_first(c):
                    add_beta(c - 1)
                for n in range(4, NG):
                    add(c, n)

            power(chunks.first, mv, mv_done, tmp, eps_done, rstd, rstd_done)
            chunks.each(pool, body)
            power(chunks.last, mv2, mv2_done, tmp2, eps2_done, rstd2, rstd2_done)
            add_beta(chunks.last)


def mix(nc, S, name, sems, start):
    with ExitStack() as ctx:
        def sb(n, shape, dt=FP32):
            return ctx.enter_context(nc.sbuf_tensor(f"{name}_{n}", shape, dt))

        def sem(n):
            if n not in sems:
                sems[n] = S.sems.enter_context(nc.semaphore(f"{name}_{n}"))
            return sems[n]

        xn = sb("xn", [P, TILES, D])
        st, mv = sb("st", [P, TILES, 6]), sb("mv", [P, TILES, 2])
        rstd, tmp = sb("rstd", [P, TILES]), sb("tmp", [P, TILES])
        xt = sb("xt", [P, CHUNK])
        x_hi = sb("x_hi", [P, BATCH, SEQ + 1], F32R)
        x_lo = sb("x_lo", [P, BATCH, SEQ + 1], F32R)
        recept, relu, key = (sb(n, [P, CHUNK]) for n in ("recept", "relu", "key"))
        key_hi, key_lo = sb("key_hi", [P, CHUNK], F32R), sb("key_lo", [P, CHUNK], F32R)
        out = sb("out", [P, CHUNK])
        r_ps, k_ps, v_ps, o_ps = S.bank[0:4]
        xt_ps = S.bank[4:6]

        st_done, mv_done, rstd_done, xn_done = sem("st_done"), sem("mv_done"), sem("rstd_done"), sem("xn_done")
        eps_done, xt_done, xhi_done, keep_done = sem("eps_done"), sem("xt_done"), sem("xhi_done"), sem("keep_done")
        xlo_done, k_done, r_done, sig_done = sem("xlo_done"), sem("k_done"), sem("r_done"), sem("sig_done")
        key_done, khi_done, klo_done, v_done = sem("key_done"), sem("khi_done"), sem("klo_done"), sem("v_done")
        out_done, o_done, x_done, zero_done = sem("out_done"), sem("o_done"), sem("x_done"), sem("zero_done")
        relu_done = sem("relu_done")
        chunks = Chunks(start)
        block = ctx.enter_context(nc.Block())
        last = chunks.last

        def halves(c, shift):
            b = bass.ds((c - start) * 2, 2)
            return x_hi[:, b, 1 - shift:1 - shift + SEQ], x_lo[:, b, 1 - shift:1 - shift + SEQ]

        def tiles(c):
            return range((c - start) * CT, (c - start + 1) * CT)

        def by_batch(a):
            return a[:, :].rearrange("p (b s) -> p b s", b=2)

        @block.tensor
        def _(pe):
            def front(c):
                pe.wait_ge(xn_done, nth(CT, c, CT - 1))
                wait_reuse(pe, keep_done, c - 1)
                for n, t in enumerate(tiles(c)):
                    mm = pe.transpose(xt_ps[c % 2][:, n * P:(n + 1) * P], xn[:, t, :], S.ident[:, :])
                mm.then_inc(xt_done, 1)

            def mixed(c, out, w):
                for shift in range(2):
                    hi, lo = halves(c, shift)
                    whi, wlo = (a[:, (2 * w + shift) * D:(2 * w + shift + 1) * D] for a in (S.fold_hi, S.fold_lo))
                    pe.matmul(out, whi, hi, start=(shift == 0), stop=False)
                    pe.matmul(out, whi, lo, start=False, stop=False)
                    mm = pe.matmul(out, wlo, hi, start=False, stop=(shift == 1))
                return mm

            def keys_and_gates(c):
                pe.wait_ge(xlo_done, nth(1, c, 0))
                wait_reuse(pe, relu_done, c)
                mixed(c, k_ps[:, :], 1).then_inc(k_done, 1)
                wait_reuse(pe, sig_done, c)
                mixed(c, r_ps[:, :], 0).then_inc(r_done, 1)

            def v(c):
                pe.wait_ge(klo_done, nth(1, c, 0))
                wait_reuse(pe, out_done, c)
                three(pe, v_ps[:, :], *columns(S, V0), key_hi[:, :], key_lo[:, :]).then_inc(v_done, 1)

            def back(c):
                pe.wait_ge(out_done, nth(1, c, 0))
                wait_reuse(pe, x_done, c)
                for t in range(CT):
                    mm = pe.transpose(o_ps[:, t * P:(t + 1) * P], out[:, t * P:(t + 1) * P], S.ident[:, :])
                mm.then_inc(o_done, 1)

            front(start)
            front(start + 1)
            keys_and_gates(start)
            for c in range(start + 2, last + 1):
                front(c)
            with pe.Fori(start + 1, last + 1) as c:
                keys_and_gates(c)
                v(c - 1)
                back(c - 1)
            v(last)
            back(last)

        @block.scalar
        def _(act):
            def front(c):
                act.wait_ge(xt_done, nth(1, c, 0))
                act.activation(halves(c, 0)[0], by_batch(xt_ps[c % 2]), ACT.Copy).then_inc(xhi_done, 1)
                wait_reuse(act, xlo_done, c)
                act.activation(xt[:, :], xt_ps[c % 2][:, :], ACT.Copy).then_inc(keep_done, 1)

            def gate(c):
                act.wait_ge(r_done, nth(1, c, 0))
                wait_reuse(act, out_done, c)
                act.activation(recept[:, :], r_ps[:, :], ACT.Sigmoid).then_inc(sig_done, 1)

            def key_high(c):
                act.wait_ge(k_done, nth(1, c, 0))
                wait_reuse(act, key_done, c)
                wait_reuse(act, khi_done, c)
                act.activation(relu[:, :], k_ps[:, :], ACT.Relu).then_inc(relu_done, 1)
                act.wait_ge(relu_done, nth(1, c, 0))
                wait_reuse(act, v_done, c)
                act.activation(key_hi[:, :], relu[:, :], ACT.Square).then_inc(khi_done, 1)

            act.wait_ge(zero_done, start // CHUNKS + 1)
            front(start)
            front(start + 1)
            key_high(start)
            gate(start)
            for c in range(start + 2, last + 1):
                front(c)
            with act.Fori(start + 1, last + 1) as c:
                key_high(c)
                gate(c)

        @block.vector
        def _(dve):
            def statistics(c):
                for t in tiles(c):
                    dve.bn_stats(st[:, t, :], S.x[:, t, :]).then_inc(st_done, 1)
                dve.wait_ge(st_done, nth(CT, c, CT - 1))
                for t in tiles(c):
                    dve.bn_aggr(mv[:, t, :], st[:, t, :]).then_inc(mv_done, 1)

            def apply_norm(c):
                dve.wait_ge(rstd_done, nth(1, c, 0))
                for t in tiles(c):
                    dve.tensor_scalar(xn[:, t, :], S.x[:, t, :], mv[:, t, 0:1], rstd[:, t:t + 1], ALU.subtract, ALU.mult)\
                        .then_inc(xn_done, 1)

            def square(c):
                dve.wait_ge(relu_done, nth(1, c, 0))
                wait_reuse(dve, klo_done, c)
                dve.tensor_tensor(key[:, :], relu[:, :], relu[:, :], ALU.mult).then_inc(key_done, 1)

            def key_low(c):
                dve.wait_ge(khi_done, nth(1, c, 0))
                dve.wait_ge(key_done, nth(1, c, 0))
                dve.tensor_tensor(key_lo[:, :], key[:, :], key_hi[:, :].bitcast(FP32), ALU.subtract).then_inc(klo_done, 1)

            def output(c):
                dve.wait_ge(v_done, nth(1, c, 0))
                dve.wait_ge(sig_done, nth(1, c, 0))
                wait_reuse(dve, o_done, c)
                dve.tensor_tensor(out[:, :], v_ps[:, :], recept[:, :], ALU.mult).then_inc(out_done, 1)

            def update(c):
                dve.wait_ge(o_done, nth(1, c, 0))
                x = S.x[:, chunks.tiles(c), :]
                dve.scalar_tensor_tensor(x, o_ps[:, :].rearrange("p (t d) -> p t d", d=D), 0.5, x, ALU.mult, ALU.add)\
                    .then_inc(x_done, 1)

            for a in (x_hi, x_lo):
                mm = dve.memset(a[:, :, 0:1].bitcast(FP32), 0.0)
            mm.then_inc(zero_done, 1)
            statistics(start)
            for c in range(start, last):
                statistics(c + 1)
                apply_norm(c)
            apply_norm(last)
            square(start)
            key_low(start)
            with dve.Fori(start + 1, last + 1) as c:
                square(c)
                output(c - 1)
                key_low(c)
                update(c - 1)
            output(last)
            update(last)

        @block.gpsimd
        def _(pool):
            def power(c):
                t = slice(tiles(c)[0], tiles(c)[-1] + 1)
                pool.wait_ge(mv_done, nth(CT, c, CT - 1))
                pool.tensor_tensor(tmp[:, t], mv[:, t, 1], S.eps_ln[:, 0:CT], ALU.add).then_inc(eps_done, 1)
                pool.wait_ge(eps_done, nth(1, c, 0))
                pool.tensor_tensor(rstd[:, t], tmp[:, t], S.minus_half[:, 0:CT], ALU.pow).then_inc(rstd_done, 1)

            def low(c):
                hold(pool, S, keep_done, nth(1, c, 0))
                hi, lo = halves(c, 0)
                pool.tensor_tensor(lo, by_batch(xt), hi.bitcast(FP32), ALU.subtract).then_inc(xlo_done, 1)

            power(start)
            power(start + 1)
            for c in range(start, last + 1):
                low(c)
                if c + 2 <= last:
                    power(c + 2)


def store(nc, S, dram):
    with ExitStack() as ctx:
        out_done = ctx.enter_context(nc.semaphore("out_done"))
        block = ctx.enter_context(nc.Block())

        @block.sync
        def _(sp):
            sp.dma_start(dram["out"].rearrange("(t p) d -> p t d", p=P), S.x[:, :, :]).then_inc(out_done, 16)
            sp.wait_ge(out_done, 16)


def macaron(nc, dram):
    with ExitStack() as ctx:
        def sb(n, shape, dt=FP32):
            return ctx.enter_context(nc.sbuf_tensor(n, shape, dt))

        S = Shared()
        S.sems = ctx
        S.x = sb("x", [P, TILES, D])
        S.whi, S.wlo = sb("whi", [P, WCOLS], F32R), sb("wlo", [P, WCOLS], F32R)
        S.fold_hi, S.fold_lo = sb("fold_hi", [P, 4 * D], F32R), sb("fold_lo", [P, 4 * D], F32R)
        S.sel = sb("sel", [P, EXPERTS * P], F32R)
        S.ident = sb("ident", [P, P])
        S.rev = sb("rev", [P, CT * EXPERTS])
        S.rev3 = S.rev[:, :].rearrange("p (t e) -> p t e", e=EXPERTS)
        S.vec, S.half_alpha, S.one_minus_mu = sb("vec", [P, 9]), sb("half_alpha", [P, 1]), sb("one_minus_mu", [P, 2])
        S.gamma, S.beta = sb("gamma", [P, D]), sb("beta", [P, D])
        S.ident_bf, S.mask = sb("ident_bf", [P, P], BF16), sb("mask", [P, 6 * P], BF16)
        S.up = sb("up", [96, UCOLS], F32R)
        S.combp = sb("combp", [P, CT, P])
        S.minus_half, S.eps_ln, S.eps_rms = (sb(n, [P, CT]) for n in ("minus_half", "eps_ln", "eps_rms"))
        S.held = ctx.enter_context(nc.semaphore("held"))
        S.psum = ctx.enter_context(nc.psum_tensor("psum", [P, 8 * 512], FP32))
        S.bank = [S.psum[:, i * 512:(i + 1) * 512] for i in range(8)]
        setup(nc, S, dram)
        moe_sems, mix_sems = {}, {}
        moe(nc, S, "moe1", moe_sems, 0)
        attention(nc, S, "attn")
        moe(nc, S, "moe2", moe_sems, CHUNKS)
        mix(nc, S, "mix1", mix_sems, 0)
        rolls(nc, S, "rolls", {}, 0)
        mix(nc, S, "mix2", mix_sems, CHUNKS)
        store(nc, S, dram)


def kernel(**inputs):
    import numpy as np
    import concourse.bacc as bacc
    from concourse.bass_utils import run_bass_kernel_spmd

    def grab(n):
        return np.asarray(inputs[n])

    f = np.float32
    gate_up = grab("L0_ffn_gate_up_weight").transpose(2, 0, 1).reshape(D, EXPERTS * 2 * HID)
    down = np.zeros((EXPERTS, 3 * P, D), f)
    down[:, :HID, :] = grab("L0_ffn_down_weight").transpose(0, 2, 1)
    down = down.reshape(EXPERTS, 3, P, D).transpose(2, 0, 1, 3).reshape(P, EXPERTS * 3 * D)
    sel = np.zeros((P, EXPERTS, P), f)
    for e in range(EXPERTS):
        sel[e, e, :] = 1.0
        sel[LOW0 + e, e, :] = 1.0
    weights = [gate_up, down, grab("L0_ffn_router_weight").T, np.zeros((D, P - EXPERTS), f)]
    weights += [grab(f"L1_ffn_W_{n}").T for n in "rkv"]
    weights += [grab("L1_attn_value_W").T, grab("L1_attn_gate_W").T, grab("L0_attn_W_o")]
    weights += [grab("L0_attn_W_dq")] * 3 + [grab("L0_attn_W_dkv")] * 3
    up = np.zeros((DC, UCOLS), f)
    for n, at in (("uq", UQ0), ("uk", UK0)):
        v = up[:, at:at + GROUPS * P].reshape(DC, HEADS, 32)
        w = grab(f"L0_attn_W_{n}").reshape(DC, HEADS, DK)
        for r in range(3):
            v[:, :, r * DK:(r + 1) * DK] = w
    up[:, UV0:] = grab("L0_attn_W_uv")
    row = np.arange(P) % 32 // DK
    one = np.ones(P, f)
    vec = [grab("L0_ffn_norm_weight"), np.broadcast_to(grab("L0_ffn_residual_alpha"), (P,)),
           np.array([1, 1, -1, 0], f)[row], np.array([0, 0, 1, 0], f)[row],
           np.array([1, -1, 1, 0], f)[row], np.array([0, 1, 0, 0], f)[row],
           np.isin(np.arange(P) % 32, (MAX_ROW, MAX_ROW + 1)).astype(f),
           grab("L1_ffn_mu_r"), grab("L1_ffn_mu_k")]
    later = np.where(np.arange(P)[None, :] > np.arange(P)[:, None], f(MASKED), f(0))
    none = np.zeros((P, P), f)
    arrays = {
        "x": grab("L0_attn_x").reshape(TOKENS, D),
        "weights": np.concatenate(weights, axis=1),
        "up": np.concatenate([up] * 3, axis=0),
        "vec": np.stack(vec, axis=1),
        "gamma": np.broadcast_to(grab("L1_attn_gamma"), (P, D)),
        "beta": np.broadcast_to(grab("L1_attn_beta"), (P, D)),
        "mask": np.concatenate([none, later, later, none, later.T, later.T], axis=1),
        "sel": sel.reshape(P, EXPERTS * P),
        "ident": np.eye(P, dtype=f),
        "rev": np.broadcast_to(np.tile(np.arange(EXPERTS, 0, -1, dtype=f), CT), (P, CT * EXPERTS)),
    }
    nc = bacc.Bacc("TRN2", target_bir_lowering=False, num_devices=1)
    dram, sent = {}, {}
    for n, a in arrays.items():
        a = np.ascontiguousarray(a)
        sent[f"in_{n}"] = a
        dram[n] = nc.dram_tensor(f"in_{n}", a.shape, mybir.dt.from_np(a.dtype), kind="ExternalInput").ap()
    dram["out"] = nc.dram_tensor("out_x", (TOKENS, D), FP32, kind="ExternalOutput").ap()
    macaron(nc, dram)
    r = run_bass_kernel_spmd(nc, [sent], core_ids=[0])
    return r.results[0]["out_x"].reshape(BATCH, SEQ, D)
```

```python
import concourse.bass as bass
from concourse import mybir
from contextlib import ExitStack

FP32 = mybir.dt.float32
F32R = mybir.dt.float32r
BF16 = mybir.dt.bfloat16
ALU = mybir.AluOpType
ACT = mybir.ActivationFunctionType
AX = mybir.AxisListType

P = 128
D = 128
BATCH, SEQ = 8, 256
TOKENS = BATCH * SEQ
TILES = TOKENS // P
CHUNK = 512
CT = CHUNK // P
CHUNKS = TOKENS // CHUNK

EXPERTS, HID = 8, 352
STEPS = EXPERTS * HID // P
SHARES = sorted({(j * P // HID, ((j + 1) * P - 1) // HID) for j in range(STEPS)})
SHARE = [SHARES.index((j * P // HID, ((j + 1) * P - 1) // HID)) for j in range(STEPS)]
FIRST, LAST = ([f(j for j in range(STEPS) if SHARE[j] == g) for g in range(len(SHARES))] for f in (min, max))
LOW0 = 32
NEG_BIG = -3.0e38
MASKED = -1.0e30
SHARE_LAG, WEIGH_LAG, SPLIT_LAG, LAG = 5, 6, 8, 9
CATCH_UP, LAST_LAG = 8, 4
FIRST_WAIT = 1
RING, HALVES = 11, 4

TILE_COLS = 3 * P
PIECE_TILES = 2
ROUTER0 = 0
EXPERTS0 = ROUTER0 + P
V0 = EXPERTS0 + STEPS * TILE_COLS
VALUE0 = V0 + D
GATES0 = VALUE0 + D
CQ0 = GATES0 + 9 * D
CKV0 = CQ0 + 96
WCOLS = CKV0 + 96
RK0 = WCOLS
PIECES = [(ROUTER0, EXPERTS0)]
PIECES += [(EXPERTS0 + j * TILE_COLS, EXPERTS0 + min(j + PIECE_TILES, STEPS) * TILE_COLS) for j in range(0, STEPS, PIECE_TILES)]
PIECES += [(V0, V0 + 704), (V0 + 704, CQ0), (CQ0, WCOLS)]
STAGES = 3
POOL_PIECES = range(3, 5)

HEADS, DK, DC = 16, 8, 32
SLOTS = 4
GROUPS = HEADS // SLOTS
PAIRS = HEADS // 2
BT = SEQ // P
UQ0, UK0, UV0 = 0, GROUPS * P, 2 * GROUPS * P
UCOLS = UV0 + HEADS * DK
BEHIND = 3
MAX_ROW = 24

RANK_STAGES = ("t", "thi", "tx", "tlo", "c", "chi", "clo")

SHIFTS = (0, -32, -16, -4, -1, 1, 4, 16, 32)
PAD = 32

NORM_W, ALPHA, Q_SIGN, Q_LOW, K_SIGN, K_LOW, K_ONES, MU_R, MU_K = range(9)


def nth(per, c, i):
    return c * per + (i + 1)


def wait_reuse(eng, sem, value):
    if not isinstance(value, int) or value > 0:
        eng.wait_ge(sem, value)


class Chunks:

    def __init__(self, start):
        self.first, self.last = start, start + CHUNKS - 1

    def each(self, eng, body):
        body(self.first)
        with eng.Fori(self.first + 1, self.last) as c:
            body(c)
        body(self.last)

    def is_first(self, c):
        return isinstance(c, int) and c == self.first

    def is_last(self, c):
        return isinstance(c, int) and c == self.last

    def tokens(self, c):
        return bass.ds((c - self.first) * CHUNK, CHUNK)

    def tiles(self, c):
        return bass.ds((c - self.first) * CT, CT)

    def tile(self, c, t):
        return bass.ds((c - self.first) * CT + t, 1)


class Shared:
    pass


class Chain:

    def __init__(self, eng, sem, per, c):
        self.eng, self.sem, self.per, self.c, self.n = eng, sem, per, c, 0

    def link(self, ins):
        ins.then_inc(self.sem, 1)
        self.n += 1
        self.eng.wait_ge(self.sem, self.c * self.per + self.n)

    def end(self):
        assert self.n == self.per, (self.n, self.per)


def hold(eng, S, sem, value):
    eng.wait_ge(sem, value)
    eng.sem_inc(S.held, 1)


class Ahead:

    def __init__(self, S, name, sems, c, tiles=CT, batches=1, base=False):
        def sem(n):
            if n not in sems:
                sems[n] = S.sems.enter_context(S.nc.semaphore(f"{name}_{n}"))
            return sems[n]

        S.turn = 1 - S.turn
        self.xn, self.st, self.mv, self.rstd, self.rms, self.tmp = S.ahead[S.turn]
        self.S, self.c, self.tiles, self.batches, self.base = S, c, tiles, batches, base
        self.st_done, self.mv_done, self.rstd_done, self.xn_done = sem("st_done"), sem("mv_done"), sem("rstd_done"), sem("xn_done")
        if base:
            self.order, self.base_done, self.nr_done = sem("rstd_order"), sem("base_done"), sem("nr_done")
        else:
            self.eps_done = sem("eps_done")

    def statistics(self, dve):
        for t in range(self.tiles):
            dve.bn_stats(self.st[:, t, :], self.S.x[:, t, :]).then_inc(self.st_done, 1)
        dve.wait_ge(self.st_done, nth(CT, self.c, self.tiles - 1))
        for t in range(self.tiles):
            dve.bn_aggr(self.mv[:, t, :], self.st[:, t, :]).then_inc(self.mv_done, 1)

    def power(self, pool):
        S, n = self.S, self.tiles
        var, half, tmp, rstd, rms = self.mv[:, 0:n, 1], S.minus_half[:, 0:n], self.tmp[:, 0:n], self.rstd[:, 0:n], self.rms[:, 0:n]
        pool.wait_ge(self.mv_done, nth(CT, self.c, self.tiles - 1))
        if self.base:
            ch = Chain(pool, self.order, 5, self.c)
            ch.link(pool.tensor_tensor(tmp, var, S.eps_ln[:, 0:n], ALU.add))
            ch.link(pool.tensor_tensor(rstd, tmp, half, ALU.pow))
            ch.link(pool.tensor_tensor(tmp, var, rstd, ALU.mult))
            ch.link(pool.tensor_tensor(tmp, tmp, rstd, ALU.mult))
            ch.link(pool.tensor_tensor(tmp, tmp, S.eps_rms[:, 0:n], ALU.add))
            pool.tensor_tensor(rms, tmp, half, ALU.pow).then_inc(self.rstd_done, 1)
            ch.end()
        else:
            pool.tensor_tensor(tmp, var, S.eps_ln[:, 0:n], ALU.add).then_inc(self.eps_done, self.batches)
            pool.wait_ge(self.eps_done, self.c + self.batches)
            pool.tensor_tensor(rstd, tmp, half, ALU.pow).then_inc(self.rstd_done, self.batches)

    def apply(self, dve):
        dve.wait_ge(self.rstd_done, self.c + self.batches)
        for t in range(self.tiles):
            dve.tensor_scalar(self.xn[:, t, :], self.S.x[:, t, :], self.mv[:, t, 0:1], self.rstd[:, t:t + 1],
                              ALU.subtract, ALU.mult).then_inc(self.xn_done, 1)
        if self.base:
            x = self.S.x[:, 0:self.tiles, :]
            dve.wait_ge(self.xn_done, nth(CT, self.c, self.tiles - 1))
            dve.scalar_tensor_tensor(x, self.xn[:, 0:self.tiles, :], 0.5, x, ALU.mult, ALU.add).then_inc(self.base_done, 1)
            dve.wait_ge(self.base_done, nth(1, self.c, 0))
            for t in range(self.tiles):
                dve.tensor_scalar(self.xn[:, t, :], self.xn[:, t, :], self.rms[:, t:t + 1], None, ALU.mult).then_inc(self.nr_done, 1)


class AheadRanks(Ahead):

    def __init__(self, S, name, sems):
        super().__init__(S, name, sems, 0, batches=CT // BT)
        self.t, self.thi, self.tx, self.tlo, self.c_done, self.chi, self.clo = (
            S.sems.enter_context(S.nc.semaphore(f"{name}_{n}")) for n in RANK_STAGES)
        sems.update(zip(RANK_STAGES, (self.t, self.thi, self.tx, self.tlo, self.c_done, self.chi, self.clo)))

    def place(self, bank, high, low, plain):
        self.bank, self.t_hi, self.t_lo, self.t_x = bank, high, low, plain

    def transposes(self, pe):
        pe.wait_ge(self.xn_done, BT)
        for t in range(BT):
            mm = pe.transpose(self.bank[:, t * P:(t + 1) * P], self.xn[:, t, :], self.S.ident[:, :])
        mm.then_inc(self.t, 1)

    def keep_tokens(self, act):
        act.wait_ge(self.t, 1)
        act.activation(self.t_hi, self.bank[:, 0:SEQ], ACT.Copy).then_inc(self.thi, 1)
        act.activation(self.t_x, self.bank[:, 0:SEQ], ACT.Copy).then_inc(self.tx, 1)

    def low(self, pool):
        pool.wait_ge(self.tx, 1)
        pool.tensor_tensor(self.t_lo, self.t_x, self.t_hi.bitcast(FP32), ALU.subtract).then_inc(self.tlo, 1)

    def ranks(self, pe):
        pe.wait_ge(self.tlo, 1)
        three(pe, self.bank[0:96, 0:SEQ], *columns(self.S, CQ0, 96), self.t_hi, self.t_lo)
        three(pe, self.bank[0:96, SEQ:], *columns(self.S, CKV0, 96), self.t_hi, self.t_lo).then_inc(self.c_done, 1)

    def split_ranks(self, act):
        act.wait_ge(self.c_done, 1)
        act.activation(self.S.low_rank[:, :], self.bank[0:96, :], ACT.Copy).then_inc(self.chi, 1)

    def low_ranks(self, dve):
        dve.wait_ge(self.chi, 1)
        lo = self.S.low_rank[DC:2 * DC, :]
        dve.tensor_tensor(lo, self.bank[DC:2 * DC, :], lo.bitcast(FP32), ALU.subtract).then_inc(self.clo, 1)


class Loading:

    def __init__(self, nc, S, dram, ctx):
        def sb(n, shape, dt=FP32):
            return ctx.enter_context(nc.sbuf_tensor(n, shape, dt))

        def sem(name):
            return S.sems.enter_context(nc.semaphore(name))

        self.S, self.dram = S, dram
        self.stage = sb("stage", [P, STAGES, PIECE_TILES * TILE_COLS])
        self.rk_stage, self.sel_stage = sb("rk_stage", [P, 2 * D]), sb("sel_stage", [P, len(SHARES) * P])
        self.up_stage, self.mask_stage = self.sel_stage[0:96, 0:UCOLS], self.sel_stage[:, UCOLS:UCOLS + 4 * P]
        self.x_in, self.rest_in = sem("x_in"), sem("rest_in")
        self.w_in = [sem(f"w_in{n}") for n in range(STAGES)]
        self.small_in, self.sel_in, self.late_in = sem("small_in"), sem("sel_in"), sem("late_in")
        self.w_hi, self.w_lo, self.w_lo_pool = sem("w_hi"), sem("w_lo"), sem("w_lo_pool")
        self.factors, self.zeros = sem("factors"), sem("zeros")
        self.late_hi, self.sel_kept = sem("late_hi"), sem("sel_kept")
        self.xv = dram["x"].rearrange("(c t p) d -> c p t d", p=P, t=CT)

    def staged(self, n):
        a, b = PIECES[n]
        return self.stage[:, n % STAGES, 0:b - a]

    def issue(self, sp):
        S, dram = self.S, self.dram
        sp.dma_start(S.x[:, 0:CT, :], self.xv[0]).then_inc(self.x_in, 16)
        for n, (a, b) in enumerate(PIECES):
            if n >= STAGES:
                self.split(sp, n - STAGES)
            sp.dma_start(self.staged(n), dram["weights"][:, a:b]).then_inc(self.w_in[n % STAGES], 16)
            if n == 2:
                sp.dma_start(self.sel_stage[0:2 * LOW0, :], dram["sel"]).then_inc(self.sel_in, 16)
                for c in range(1, CHUNKS):
                    sp.dma_start(S.x[:, c * CT:(c + 1) * CT, :], self.xv[c]).then_inc(self.rest_in, 16)
        sp.wait_ge(self.sel_kept, 1)
        for dst, src in ((self.rk_stage[:, :], dram["weights"][:, RK0:RK0 + 2 * D]), (S.gamma[:, :], dram["gamma"]),
                         (S.beta[:, :], dram["beta"]), (S.wo[:, :], dram["wo"]), (self.up_stage[:, :], dram["up"]), (self.mask_stage[:, :], dram["mask"])):
            sp.dma_start(dst, src).then_inc(self.late_in, 16)

    def issue_small(self, act):
        S, dram = self.S, self.dram
        for dst, src in ((S.vec, dram["vec"]), (S.ident, dram["ident"]), (S.rev, dram["rev"])):
            act.dma_start(dst[:, :], src).then_inc(self.small_in, 16)

    def high(self, act, n):
        a, b = PIECES[n]
        act.wait_ge(self.w_in[n % STAGES], 16 * (n // STAGES + 1))
        act.activation(self.S.whi[:, a:b], self.staged(n), ACT.Copy).then_inc(self.w_hi, 1)

    def low(self, eng, n):
        a, b = PIECES[n]
        eng.wait_ge(self.w_hi, n + 1)
        eng.tensor_tensor(self.S.wlo[:, a:b], self.staged(n), self.S.whi[:, a:b].bitcast(FP32), ALU.subtract)\
            .then_inc(self.w_lo_pool if n in POOL_PIECES else self.w_lo, 1)

    def split(self, eng, n):
        if n in POOL_PIECES:
            eng.wait_ge(self.w_lo_pool, n - POOL_PIECES[0] + 1)
        else:
            eng.wait_ge(self.w_lo, n + 1 - sum(m < n for m in POOL_PIECES))

    def select(self, act):
        act.wait_ge(self.sel_in, 16)
        act.wait_ge(self.zeros, 5)
        act.activation(self.S.sel[:, :], self.sel_stage[:, :], ACT.Copy).then_inc(self.sel_kept, 1)

    def constants(self, pool):
        S = self.S
        for n, (tile, value) in enumerate(((S.minus_half, -0.5), (S.eps_ln, 1e-5), (S.eps_rms, 1e-6))):
            pool.memset(tile[:, :], value).then_inc(self.zeros, 1)
        pool.memset(S.combp[:, :, :], 0.0).then_inc(self.zeros, 1)
        pool.wait_ge(self.zeros, 4)
        pool.memset(self.sel_stage[2 * LOW0:, :], 0.0).then_inc(self.zeros, 1)
        pool.wait_ge(self.zeros, 5)

    def scalars(self, dve):
        S = self.S
        dve.wait_ge(self.small_in, 48)
        dve.tensor_scalar(S.half_alpha[:, :], S.vec[:, ALPHA:ALPHA + 1], -0.5, 2.0, ALU.max, ALU.min).then_inc(self.factors, 1)
        dve.wait_ge(self.factors, 1)
        dve.tensor_scalar(S.half_alpha[:, :], S.half_alpha[:, :], 0.5, None, ALU.mult).then_inc(self.factors, 1)
        dve.tensor_scalar(S.one_minus_mu[:, :], S.vec[:, MU_R:MU_K + 1], -1.0, 1.0, ALU.mult, ALU.add).then_inc(self.factors, 1)
        dve.wait_ge(self.factors, 3)

    def folded(self, n):
        w, shift = divmod(n, 2)
        mu = self.S.vec[:, MU_R + w:MU_R + w + 1] if shift == 0 else self.S.one_minus_mu[:, w:w + 1]
        return self.rk_stage[:, w * D:(w + 1) * D], mu, slice(n * D, (n + 1) * D)

    def late_high(self, act):
        S = self.S
        act.wait_ge(self.late_in, 6 * 16)
        act.wait_ge(self.factors, 3)
        for n in range(4):
            w, mu, at = self.folded(n)
            act.activation(S.fold_hi[:, at], w, ACT.Copy, scale=mu).then_inc(self.late_hi, 1)
        act.activation(S.up[:, :], self.up_stage[:, :], ACT.Copy).then_inc(self.late_hi, 1)
        act.activation(S.mask[:, :], self.mask_stage[:, :], ACT.Copy)
        act.activation(S.ident_bf[:, :], S.ident[:, :], ACT.Copy)

    def late_low(self, dve):
        S = self.S
        for n in range(4):
            w, mu, at = self.folded(n)
            dve.wait_ge(self.late_hi, n + 1)
            dve.scalar_tensor_tensor(S.fold_lo[:, at], w, mu, S.fold_hi[:, at].bitcast(FP32), ALU.mult, ALU.subtract)
        dve.wait_ge(self.late_hi, 5)
        dve.tensor_tensor(S.up[64:96, :], self.up_stage[64:96, :], S.up[64:96, :].bitcast(FP32), ALU.subtract)

    def piece(self, j):
        n = 2 * (j // 3) + j % 3 + 2
        return n if j % 3 < 2 and n < len(PIECES) else None


def moe(nc, S, name, sems, start, ready, ahead, dram=None):
    with ExitStack() as ctx:
        def sb(n, shape, dt=FP32):
            return ctx.enter_context(nc.sbuf_tensor(f"{name}_{n}", shape, dt))

        def sem(n):
            if n not in sems:
                sems[n] = S.sems.enter_context(nc.semaphore(f"{name}_{n}"))
            return sems[n]

        norm_hi, norm_lo = sb("norm_hi", [P, TOKENS], F32R), sb("norm_lo", [P, TOKENS], F32R)
        comb_t = sb("comb_t", [P, CHUNK], F32R)
        xn = sb("xn", [P, CT, D])
        st, mv = sb("st", [P, CT, 6]), sb("mv", [P, CT, 2])
        rstd, rms, tmp = (sb(n, [P, CT]) for n in ("rstd", "rms", "tmp"))
        silu = [sb(f"silu{i}", [P, CHUNK]) for i in range(2)]
        hid = [sb(f"hid{i}", [P, CHUNK]) for i in range(RING)]
        hid_hi = [sb(f"hid_hi{i}", [P, CHUNK], F32R) for i in range(HALVES)]
        hid_lo = [sb(f"hid_lo{i}", [P, CHUNK], F32R) for i in range(HALVES)]
        cb = [sb(f"cb{i}", [P, CHUNK]) for i in range(2)]
        out = sb("out", [P, CHUNK])
        lgt = sb("lgt", [P, CHUNK])
        lg, lg2, one1, one2, eq = (sb(n, [P, CT, EXPERTS]) for n in ("lg", "lg2", "one1", "one2", "eq"))
        top1, top2, key1, key2, diff, tanh, w1, w2 = (
            sb(n, [P, CT, 1]) for n in ("top1", "top2", "key1", "key2", "diff", "tanh", "w1", "w2"))

        gate_ps, up_ps, bc_ps = S.bank[0:2], S.bank[2:4], S.bank[4:6]
        out_ps, misc_ps = S.bank[6], S.bank[7]

        nr_done, base_done, xt_done = sem("nr_done"), sem("base_done"), sem("xt_done")
        nhi_done, nlo_done, lg_done = sem("nhi_done"), sem("nlo_done"), sem("lg_done")
        diff_done, tanh_done, comb_done = sem("diff_done"), sem("tanh_done"), sem("comb_done")
        ct_done, cte_done, bc_done, cb_done = sem("ct_done"), sem("cte_done"), sem("bc_done"), sem("cb_done")
        gate_done, up_done, down_done = sem("gate_done"), sem("up_done"), sem("down_done")
        silu_done, hid_done, hi_done, lo_done = sem("silu_done"), sem("hid_done"), sem("hi_done"), sem("lo_done")
        weighed, out_done, fin_done, x_done = sem("weighed"), sem("out_done"), sem("fin_done"), sem("x_done")
        first_order, second_order = sem("first_order"), sem("second_order")
        comb_order, st_done, mv_done, rstd_order = sem("comb_order"), sem("st_done"), sem("mv_done"), sem("rstd_order")
        lgt_done, lge_done, xn_done, rstd_done = sem("lgt_done"), sem("lge_done"), sem("xn_done"), sem("rstd_done")
        chunks = Chunks(start)
        ranked = isinstance(ahead, AheadRanks)
        if ranked:
            ahead.place(misc_ps, norm_hi[:, 0:SEQ], norm_lo[:, 0:SEQ], lgt[:, 0:SEQ])
        load = Loading(nc, S, dram, ctx) if dram else None
        block = ctx.enter_context(nc.Block())

        def weight(half, j, part):
            a = EXPERTS0 + j * TILE_COLS + part * P
            return half[:, a:a + P]

        def earlier(j):
            return j - HALVES if j >= HALVES else max(m for m in range(STEPS) if m % HALVES == j) - STEPS

        def trailing(c, j, lag, stage):
            def tile(j):
                return j - lag + (min(max(j - CATCH_UP - lag, 0), LAG - LAST_LAG) if chunks.is_last(c) else 0)

            for k in range(tile(j - 1) + 1, tile(j) + 1):
                if 0 <= k < STEPS:
                    stage(c, k)
                elif k < 0 and not chunks.is_first(c):
                    stage(c - 1, k + STEPS)

        def weights_step(c):
            return SHARE_LAG + FIRST_WAIT if chunks.is_first(c) else SHARE_LAG - 1

        def shares(c, j, stage):
            for back in (1, 0):
                if c - back >= chunks.first if isinstance(c, int) else True:
                    for g, k in enumerate(FIRST):
                        soon = chunks.is_last(c) and back == 0
                        at = k + (max(0, SHARE_LAG - k // 3) if soon else SHARE_LAG)
                        if j + back * STEPS == max(at, weights_step(c - back) + 1):
                            stage(c - back, g)

        def loading(c):
            return load is not None and chunks.is_first(c)

        if load is not None:
            @block.sync
            def _(sp):
                load.issue(sp)

        @block.tensor
        def _(pe):
            def transposes(c):
                pe.wait_ge(nr_done, nth(CT, c, CT - 1))
                wait_reuse(pe, x_done, c - 1)
                source = ready.xn if ready and chunks.is_first(c) else xn
                for t in range(CT):
                    mm = pe.transpose(misc_ps[:, t * P:(t + 1) * P], source[:, t, :], S.ident[:, :])
                mm.then_inc(xt_done, 1)

            def logits(c):
                if loading(c):
                    load.split(pe, 0)
                pe.wait_ge(nlo_done, nth(1, c, 0))
                tok = chunks.tokens(c)
                router = slice(ROUTER0, ROUTER0 + P)
                three(pe, misc_ps[:, :], S.whi[:, router], S.wlo[:, router], norm_hi[:, tok], norm_lo[:, tok])\
                    .then_inc(lgt_done, 1)

            def logit_transposes(c):
                pe.wait_ge(lge_done, nth(1, c, 0))
                for t in range(CT):
                    mm = pe.transpose(misc_ps[:, t * P:(t + 1) * P], lgt[:, t * P:(t + 1) * P], S.ident[:, :])
                mm.then_inc(lg_done, 1)

            def comb_transposes(c):
                pe.wait_ge(comb_done, nth(1, c, 0))
                for t in range(CT):
                    mm = pe.transpose(misc_ps[0:P, t * P:(t + 1) * P], S.combp[:, t, :], S.ident[:, :])
                mm.then_inc(ct_done, 1)

            def up_and_gate(c, j):
                tok = chunks.tokens(c)
                hi, lo = norm_hi[:, tok], norm_lo[:, tok]
                if loading(c) and j % PIECE_TILES == 0:
                    load.split(pe, j // PIECE_TILES + 1)
                wait_reuse(pe, silu_done, nth(STEPS, c, j - 2))
                three(pe, gate_ps[j % 2][:, :], weight(S.whi, j, 0), weight(S.wlo, j, 0), hi, lo).then_inc(gate_done, 1)
                wait_reuse(pe, hid_done, nth(STEPS, c, j - 2))
                three(pe, up_ps[j % 2][:, :], weight(S.whi, j, 1), weight(S.wlo, j, 1), hi, lo).then_inc(up_done, 1)

            def down(c, j):
                if j == 0:
                    wait_reuse(pe, out_done, c)
                pe.wait_ge(lo_done, nth(STEPS, c, j))
                hi, lo = hid_hi[j % HALVES][:, :], hid_lo[j % HALVES][:, :]
                pe.matmul(out_ps[:, :], weight(S.whi, j, 2), hi, start=(j == 0), stop=False)
                pe.matmul(out_ps[:, :], weight(S.whi, j, 2), lo, start=False, stop=False)
                pe.matmul(out_ps[:, :], weight(S.wlo, j, 2), hi, start=False, stop=(j == STEPS - 1)).then_inc(down_done, 1)

            def broadcast(c, g):
                pe.wait_ge(cte_done, nth(1, c, 0))
                wait_reuse(pe, cb_done, nth(len(SHARES), c, g - 2))
                pe.matmul(bc_ps[g % 2][:, :], S.sel[:, g * P:(g + 1) * P], comb_t[:, :],
                          start=True, stop=True).then_inc(bc_done, 1)

            def result(c):
                pe.wait_ge(out_done, nth(1, c, 0))
                if ranked and chunks.is_last(c):
                    pe.wait_ge(ahead.clo, 1)
                for t in range(CT):
                    mm = pe.transpose(misc_ps[:, t * P:(t + 1) * P], out[:, t * P:(t + 1) * P], S.ident[:, :])
                mm.then_inc(fin_done, 1)

            def body(c):
                for j in range(STEPS):
                    up_and_gate(c, j)
                    trailing(c, j, LAG, down)
                    if j == 1 and chunks.is_first(c):
                        logit_transposes(c)
                    if j == weights_step(c):
                        comb_transposes(c)
                    shares(c, j, broadcast)
                    if j == 10 and not chunks.is_first(c):
                        result(c - 1)
                    if ranked and chunks.is_last(c):
                        if j == 12:
                            pe.wait_ge(x_done, nth(1, c - 1, 0))
                            ahead.transposes(pe)
                        if j == 15:
                            ahead.ranks(pe)
                    if not chunks.is_last(c):
                        if j == 12:
                            transposes(c + 1)
                        if j == 14:
                            logits(c + 1)
                        if j == 16:
                            logit_transposes(c + 1)

            if load is not None:
                pe.wait_ge(load.small_in, 48)
            transposes(chunks.first)
            logits(chunks.first)
            chunks.each(pe, body)
            for j in range(STEPS, STEPS + LAG):
                shares(chunks.last, j, broadcast)
                trailing(chunks.last, j, LAG, down)
            result(chunks.last)

        @block.scalar
        def _(act):
            def split_norm(c):
                act.wait_ge(xt_done, nth(1, c, 0))
                act.activation(norm_hi[:, chunks.tokens(c)], misc_ps[:, :], ACT.Copy,
                               scale=S.vec[:, NORM_W:NORM_W + 1]).then_inc(nhi_done, 1)

            def keep_logits(c):
                act.wait_ge(lgt_done, nth(1, c, 0))
                act.activation(lgt[:, :], misc_ps[:, :], ACT.Copy).then_inc(lge_done, 1)

            def weights_tanh(c):
                act.wait_ge(diff_done, nth(1, c, 0))
                act.activation(tanh[:, :, 0], diff[:, :, 0], ACT.Tanh, scale=0.5).then_inc(tanh_done, 1)

            def keep_comb(c):
                act.wait_ge(ct_done, nth(1, c, 0))
                wait_reuse(act, bc_done, nth(len(SHARES), c, -1))
                act.activation(comb_t[:, :], misc_ps[:, :], ACT.Copy).then_inc(cte_done, 1)

            def gate(c, j):
                act.wait_ge(gate_done, nth(STEPS, c, j))
                wait_reuse(act, hid_done, nth(STEPS, c, j - 2))
                act.activation(silu[j % 2][:, :], gate_ps[j % 2][:, :], ACT.Silu).then_inc(silu_done, 1)

            def high(c, j):
                act.wait_ge(weighed, nth(STEPS, c, j))
                wait_reuse(act, down_done, nth(STEPS, c, earlier(j)))
                act.activation(hid_hi[j % HALVES][:, :], hid[j % RING][:, :], ACT.Copy).then_inc(hi_done, 1)

            def keep_broadcast(c, g):
                act.wait_ge(bc_done, nth(len(SHARES), c, g))
                before = LAST[g - 2] if g >= 2 else LAST[g - 2] - STEPS
                wait_reuse(act, weighed, nth(STEPS, c, before))
                act.activation(cb[g % 2][:, :], bc_ps[g % 2][:, :], ACT.Copy).then_inc(cb_done, 1)

            def keep_out(c):
                act.wait_ge(down_done, nth(STEPS, c, STEPS - 1))
                wait_reuse(act, fin_done, c)
                act.activation(out[:, :], out_ps[:, :], ACT.Copy).then_inc(out_done, 1)

            def body(c):
                for j in range(STEPS):
                    if j == LAG and not chunks.is_first(c):
                        keep_out(c - 1)
                    gate(c, j)
                    trailing(c, j, SPLIT_LAG, high)
                    if chunks.is_first(c):
                        if j == 0:
                            keep_logits(c)
                        if j == 3:
                            weights_tanh(c)
                    if j == weights_step(c):
                        keep_comb(c)
                    if loading(c):
                        if load.piece(j) is not None:
                            load.high(act, load.piece(j))
                        if j == 2:
                            load.select(act)
                        if j == STEPS - 1:
                            load.late_high(act)
                    shares(c, j, keep_broadcast)
                    if ranked and chunks.is_last(c):
                        if j == 12:
                            ahead.keep_tokens(act)
                        if j == 15:
                            ahead.split_ranks(act)
                    if not chunks.is_last(c):
                        if j == 12:
                            split_norm(c + 1)
                        if j == 14:
                            keep_logits(c + 1)
                        if j == 19:
                            weights_tanh(c + 1)

            if load is not None:
                load.issue_small(act)
                load.high(act, 0)
                load.high(act, 1)
                act.wait_ge(load.small_in, 48)
            split_norm(chunks.first)
            chunks.each(act, body)
            for j in range(STEPS, STEPS + SPLIT_LAG):
                shares(chunks.last, j, keep_broadcast)
                trailing(chunks.last, j, SPLIT_LAG, high)
            keep_out(chunks.last)

        @block.vector
        def _(dve):
            def statistics(c):
                for t in range(CT):
                    dve.bn_stats(st[:, t, :], S.x[:, chunks.tile(c, t), :]).then_inc(st_done, 1)
                hold(dve, S, st_done, nth(CT, c, CT - 1))
                for t in range(CT):
                    dve.bn_aggr(mv[:, t, :], st[:, t, :]).then_inc(mv_done, 1)

            def apply_norm(c, *tiles):
                dve.wait_ge(rstd_done, nth(1, c, 0))
                wait_reuse(dve, xt_done, c)
                for t in tiles:
                    dve.tensor_scalar(xn[:, t, :], S.x[:, chunks.tile(c, t), :], mv[:, t, 0:1], rstd[:, t:t + 1],
                                      ALU.subtract, ALU.mult).then_inc(xn_done, 1)

            def apply_rms(c):
                dve.wait_ge(base_done, nth(1, c, 0))
                for t in range(CT):
                    dve.tensor_scalar(xn[:, t, :], xn[:, t, :], rms[:, t:t + 1], None, ALU.mult).then_inc(nr_done, 1)

            def base(c):
                x = S.x[:, chunks.tiles(c), :]
                dve.wait_ge(xn_done, nth(CT, c, CT - 1))
                dve.scalar_tensor_tensor(x, xn[:, :, :], 0.5, x, ALU.mult, ALU.add).then_inc(base_done, 1)

            def low_norm(c):
                dve.wait_ge(nhi_done, nth(1, c, 0))
                tok = chunks.tokens(c)
                dve.scalar_tensor_tensor(norm_lo[:, tok], misc_ps[:, :], S.vec[:, NORM_W:NORM_W + 1],
                                         norm_hi[:, tok].bitcast(FP32), ALU.mult, ALU.subtract).then_inc(nlo_done, 1)

            def all8(a):
                return a[:, :, :].to_broadcast([P, CT, EXPERTS])

            def best(ch, logit, top, key, one):
                ch.link(dve.reduce_max(top[:, :, 0], logit[:, :, :], axis=AX.X))
                ch.link(dve.tensor_tensor(eq[:, :, :], logit[:, :, :], all8(top), ALU.is_equal))
                ch.link(dve.tensor_tensor(eq[:, :, :], eq[:, :, :], S.rev3, ALU.mult))
                ch.link(dve.reduce_max(key[:, :, 0], eq[:, :, :], axis=AX.X))
                ch.link(dve.tensor_tensor(one[:, :, :], eq[:, :, :], all8(key), ALU.is_equal))

            def route_first(c):
                ch = Chain(dve, first_order, 7, c)
                dve.wait_ge(lg_done, nth(1, c, 0))
                ch.link(dve.tensor_copy(lg[:, :, :], misc_ps[:, :].rearrange("p (t e) -> p t e", t=CT)[:, :, 0:EXPERTS]))
                best(ch, lg, top1, key1, one1)
                ch.link(dve.scalar_tensor_tensor(lg2[:, :, :], one1[:, :, :], NEG_BIG, lg[:, :, :], ALU.mult, ALU.add))
                ch.end()

            def route_second(c):
                ch = Chain(dve, second_order, 5, c)
                best(ch, lg2, top2, key2, one2)
                dve.tensor_tensor(diff[:, :, :], top2[:, :, :], top1[:, :, :], ALU.subtract).then_inc(diff_done, 1)
                ch.end()

            def combine(c):
                ch = Chain(dve, comb_order, 6, c)
                dve.wait_ge(tanh_done, nth(1, c, 0))
                ch.link(dve.tensor_scalar(w2[:, :, :], tanh[:, :, :], 0.5, 0.5, ALU.mult, ALU.add))
                ch.link(dve.tensor_scalar(w1[:, :, :], tanh[:, :, :], -0.5, 0.5, ALU.mult, ALU.add))
                ch.link(dve.tensor_tensor(one1[:, :, :], one1[:, :, :], all8(w1), ALU.mult))
                ch.link(dve.tensor_tensor(one2[:, :, :], one2[:, :, :], all8(w2), ALU.mult))
                ch.link(dve.tensor_tensor(lg[:, :, :], one1[:, :, :], one2[:, :, :], ALU.add))
                if not chunks.is_first(c):
                    dve.wait_ge(ct_done, c)
                ch.link(dve.tensor_copy(S.combp[:, :, 0:EXPERTS].bitcast(F32R), lg[:, :, :]))
                ch.end()
                dve.tensor_tensor(S.combp[:, :, LOW0:LOW0 + EXPERTS], lg[:, :, :], S.combp[:, :, 0:EXPERTS], ALU.subtract)\
                    .then_inc(comb_done, 1)

            def hidden(c, j):
                dve.wait_ge(up_done, nth(STEPS, c, j))
                dve.wait_ge(silu_done, nth(STEPS, c, j))
                wait_reuse(dve, lo_done, nth(STEPS, c, j - RING))
                dve.tensor_tensor(hid[j % RING][:, :], up_ps[j % 2][:, :], silu[j % 2][:, :], ALU.mult).then_inc(hid_done, 1)

            def low(c, j):
                dve.wait_ge(hi_done, nth(STEPS, c, j))
                dve.tensor_tensor(hid_lo[j % HALVES][:, :], hid[j % RING][:, :], hid_hi[j % HALVES][:, :].bitcast(FP32),
                                  ALU.subtract).then_inc(lo_done, 1)

            def update(c):
                dve.wait_ge(fin_done, nth(1, c, 0))
                dve.wait_ge(base_done, nth(1, c, 0))
                x = S.x[:, chunks.tiles(c), :]
                dve.scalar_tensor_tensor(x, misc_ps[:, :].rearrange("p (t d) -> p t d", d=D), S.half_alpha[:, 0:1], x,
                                         ALU.mult, ALU.add).then_inc(x_done, 1)

            def body(c):
                for j in range(STEPS):
                    hidden(c, j)
                    trailing(c, j, SPLIT_LAG, low)
                    if j == 11 and not chunks.is_first(c):
                        update(c - 1)
                    if chunks.is_first(c):
                        if j == 1:
                            route_first(c)
                        if j == 2:
                            route_second(c)
                        if j == 3:
                            combine(c)
                    if loading(c):
                        if load.piece(j) is not None:
                            if load.piece(j) not in POOL_PIECES:
                                load.low(dve, load.piece(j))
                        if j == 0:
                            dve.wait_ge(load.rest_in, (CHUNKS - 1) * 16)
                        if j == STEPS - 1:
                            load.late_low(dve)
                    if chunks.is_last(c):
                        if j == 4:
                            ahead.statistics(dve)
                        if j == 9:
                            ahead.apply(dve)
                        if j == 16 and ranked:
                            ahead.low_ranks(dve)
                    else:
                        if j == 4:
                            statistics(c + 1)
                        if j == 8:
                            apply_norm(c + 1, 0, 1)
                        if j == 9:
                            apply_norm(c + 1, 2, 3)
                        if j == 10:
                            base(c + 1)
                        if j == 11:
                            apply_rms(c + 1)
                        if j == 13:
                            low_norm(c + 1)
                        if j == 17:
                            route_first(c + 1)
                        if j == 18:
                            route_second(c + 1)
                        if j == 20:
                            combine(c + 1)

            if load is not None:
                dve.wait_ge(load.x_in, 16)
            if load is not None:
                statistics(chunks.first)
                load.scalars(dve)
                load.low(dve, 0)
                dve.wait_ge(load.zeros, 4)
                apply_norm(chunks.first, *range(CT))
                base(chunks.first)
                apply_rms(chunks.first)
                load.low(dve, 1)
            low_norm(chunks.first)
            chunks.each(dve, body)
            for j in range(STEPS, STEPS + SPLIT_LAG):
                trailing(chunks.last, j, SPLIT_LAG, low)
            update(chunks.last)

        @block.gpsimd
        def _(pool):
            def rstds(c):
                ch = Chain(pool, rstd_order, 5, c)
                var, half = mv[:, :, 1], S.minus_half[:, 0:CT]
                pool.wait_ge(mv_done, nth(CT, c, CT - 1))
                ch.link(pool.tensor_tensor(tmp[:, :], var, S.eps_ln[:, 0:CT], ALU.add))
                ch.link(pool.tensor_tensor(rstd[:, :], tmp[:, :], half, ALU.pow))
                ch.link(pool.tensor_tensor(tmp[:, :], var, rstd[:, :], ALU.mult))
                ch.link(pool.tensor_tensor(tmp[:, :], tmp[:, :], rstd[:, :], ALU.mult))
                ch.link(pool.tensor_tensor(tmp[:, :], tmp[:, :], S.eps_rms[:, 0:CT], ALU.add))
                pool.tensor_tensor(rms[:, :], tmp[:, :], half, ALU.pow).then_inc(rstd_done, 1)
                ch.end()

            def weigh(c, j):
                pool.wait_ge(hid_done, nth(STEPS, c, j))
                pool.wait_ge(cb_done, nth(len(SHARES), c, SHARE[j]))
                pool.tensor_tensor(hid[j % RING][:, :], hid[j % RING][:, :], cb[SHARE[j] % 2][:, :], ALU.mult)\
                    .then_inc(weighed, 1)

            def body(c):
                for j in range(STEPS):
                    if loading(c) and load.piece(j) in POOL_PIECES:
                        load.low(pool, load.piece(j))
                    if j == WEIGH_LAG:
                        if chunks.is_last(c):
                            ahead.power(pool)
                        else:
                            rstds(c + 1)
                    trailing(c, j, WEIGH_LAG, weigh)
                    if j == 14 and ranked and chunks.is_last(c):
                        ahead.low(pool)

            if load is not None:
                load.constants(pool)
                rstds(chunks.first)
            chunks.each(pool, body)
            for j in range(STEPS, STEPS + WEIGH_LAG):
                trailing(chunks.last, j, WEIGH_LAG, weigh)


def three(pe, out, whi, wlo, hi, lo):
    pe.matmul(out, whi, hi, start=True, stop=False)
    pe.matmul(out, whi, lo, start=False, stop=False)
    return pe.matmul(out, wlo, hi, start=False, stop=True)


def columns(S, a, n=D):
    return S.whi[:, a:a + n], S.wlo[:, a:a + n]


def attention(nc, S, name, sems, ready, ahead):
    with ExitStack() as ctx:
        def sb(n, shape, dt=FP32):
            return ctx.enter_context(nc.sbuf_tensor(f"{name}_{n}", shape, dt))

        st, mv = sb("st", [P, BT, 6]), sb("mv", [P, BT, 2])
        rstd, tmp = sb("rstd", [P, BT]), sb("tmp", [P, BT])
        xn = sb("xn", [P, BT, D])
        t_x, t_hi, t_lo = sb("t_x", [P, SEQ]), sb("t_hi", [P, SEQ], F32R), sb("t_lo", [P, SEQ], F32R)
        low_rank = S.low_rank
        q_part, k_part = sb("q_part", [P, SEQ], F32R), sb("k_part", [P, SEQ], F32R)
        q_st, k_st = sb("q_st", [P, GROUPS, SEQ], F32R), sb("k_st", [P, 2, SEQ], F32R)
        k_head = sb("k_head", [P, GROUPS, SLOTS, SEQ], F32R)
        q_max = sb("q_max", [P, GROUPS, SEQ], F32R)
        block_max = sb("block_max", [P, HEADS, 3])
        max_rows = sb("max_rows", [P, BT, HEADS, 32])
        probs = [sb(f"probs{i}", [P, 2, 3 * P]) for i in range(4)]
        value_in = sb("value_in", [P, BT, HEADS, DK])
        values = sb("values", [P, BT, HEADS, 32])
        heads_t = [sb(f"heads_t{i}", [P, BT, P]) for i in range(2)]
        rsum, heads = sb("rsum", [P, BT, HEADS, 1]), sb("heads", [P, BT, HEADS, DK])
        h_t = sb("h_t", [P, BT, P])

        def two_banks(i):
            a = S.psum[:, i * 512:(i + 2) * 512].rearrange("p (s c) -> p s c", s=2)
            return a[:, :, 0:3 * P], a[:, :, 3 * P:]

        score_t_ps, extra_t_ps = zip(two_banks(0), two_banks(2))
        score_ps, extra_ps = two_banks(4)
        head_ps = S.bank[6][:, 0:SEQ]
        out_ps = S.bank[6][:, SEQ:].rearrange("p (t d) -> p t d", t=BT)
        qk_ps = rank_ps = S.bank[7]

        names = ("vmm vs v qk tqk kq ka kp s max both mhi mneg mt q2 sc exp pv ot ott rs "
                 "at att ah wo x set zeros").split()
        N = {n: S.sems.enter_context(nc.semaphore(f"{name}_{n}")) for n in names}
        N.update({n: sems[n] for n in RANK_STAGES})
        N.update({n: sems[n + "_done"] for n in ("st", "mv", "eps", "rstd", "xn")})
        block = ctx.enter_context(nc.Block())
        later, earlier = S.mask[:, 0:SEQ], S.mask[:, SEQ:]
        inv_sqrt = float(DK) ** -0.5

        ALL_SET = 3 + GROUPS // 2

        def slot(j):
            return slice(32 * j, 32 * j + 32)

        def pair(u):
            return u // 2, (2 * (u % 2), 2 * (u % 2) + 1)

        def has(b):
            return not isinstance(b, int) or 0 <= b < BATCH

        def is_ready(b):
            return isinstance(b, int) and b < CT // BT

        def behind(b, u):
            return (b + 1, u - BEHIND) if u >= BEHIND else (b, u - BEHIND + PAIRS)

        def weighed(b, u):
            return (b, (u - 3) // 2) if u >= 3 else (b - 1, GROUPS - 1)

        def projected(u):
            return {0: 0, 1: 1, 3: 2, 5: 3}.get(u)

        def shifted(b, u):
            return (b + 1, 0) if u == 6 else (b, u // 2 + 1)

        def is_end(b):
            return isinstance(b, int) and b == BATCH - 1

        def over_batches(eng, body):
            for b in range(-1, 1):
                body(b)
            with eng.Fori(1, BATCH - 3) as b:
                body(b)
            for b in range(BATCH - 3, BATCH + 1):
                body(b)

        @block.tensor
        def _(pe):
            def transposes(b):
                pe.wait_ge(N["xn"], nth(BT, b, BT - 1))
                for t in range(BT):
                    source = ready.xn[:, b * BT + t, :] if is_ready(b) else xn[:, t, :]
                    mm = pe.transpose(extra_t_ps[0][:, t, :], source, S.ident[:, :])
                mm.then_inc(N["t"], 1)

            def ranks(b):
                pe.wait_ge(N["tlo"], nth(1, b, 0))
                wait_reuse(pe, N["kq"], GROUPS * b)
                three(pe, rank_ps[0:96, 0:SEQ], *columns(S, CQ0, 96), t_hi[:, :], t_lo[:, :])
                three(pe, rank_ps[0:96, SEQ:], *columns(S, CKV0, 96), t_hi[:, :], t_lo[:, :]).then_inc(N["c"], 1)

            def value(b):
                pe.wait_ge(N["clo"], nth(1, b, 0))
                for t in range(BT):
                    mm = pe.matmul(extra_t_ps[0][:, t, :], low_rank[:, SEQ + t * P:SEQ + (t + 1) * P],
                                   S.up[:, UV0:UCOLS], start=True, stop=True)
                mm.then_inc(N["vmm"], 1)

            def project(b, g):
                pe.wait_ge(N["clo"], nth(1, b, 0))
                wait_reuse(pe, N["kq"], nth(GROUPS, b, g - 1))
                pe.matmul(qk_ps[:, 0:SEQ], S.up[:, UQ0 + g * P:UQ0 + (g + 1) * P], low_rank[:, 0:SEQ],
                          start=True, stop=True)
                pe.matmul(qk_ps[:, SEQ:], S.up[:, UK0 + g * P:UK0 + (g + 1) * P], low_rank[:, SEQ:],
                          start=True, stop=True).then_inc(N["qk"], 1)

            def scores(b, u, s):
                g, js = pair(u)
                j = js[s]
                pe.wait_ge(N["ka"], nth(GROUPS, b, g))
                pe.wait_ge(N["kp"], nth(2 * GROUPS, b, 2 * g + 1))
                pe.matmul(score_ps[:, s, 0:SEQ], q_st[:, g, P:SEQ], k_head[:, g, j, :], start=True, stop=False)
                pe.matmul(score_ps[:, s, SEQ:], q_st[:, g, 0:P], k_head[:, g, j, 0:P], start=False, stop=False)
                pe.matmul(score_ps[:, s, P:], S.ident_bf[:, :], later, start=False, stop=True).then_inc(N["s"], 1)

            def max_transposes(b, g, i):
                pe.wait_ge(N["mneg"], nth(GROUPS, b, g))
                pe.transpose(extra_ps[:, i, :], max_rows[:, 1 - i, g * SLOTS:(g + 1) * SLOTS, :], S.ident[:, :])\
                    .then_inc(N["mt"], 1)

            def scores_t(b, u):
                g, js = pair(u)
                pe.wait_ge(N["q2"], nth(GROUPS, b, g))
                out = score_t_ps[u % 2]
                for s, j in enumerate(js):
                    pe.matmul(out[:, s, 0:SEQ], k_head[:, g, j, 0:P], q_max[:, g, :], start=True, stop=False)
                    pe.matmul(out[:, s, SEQ:], k_head[:, g, j, P:SEQ], q_max[:, g, 0:P], start=False, stop=False)
                for s in range(2):
                    mm = pe.matmul(out[:, s, P:], S.ident_bf[:, :], earlier, start=False, stop=True)
                mm.then_inc(N["sc"], 1)

            def weigh(b, g):
                pe.wait_ge(N["exp"], nth(PAIRS, b, 2 * g + 1))
                pe.wait_ge(N["v"], nth(1, b, 0))
                out = extra_t_ps[1]

                def product(i, t, at, start, stop):
                    for j in range(SLOTS):
                        p = probs[(2 * g + j // 2) % 4]
                        mm = pe.matmul(out[slot(j), i, :], values[:, t, g * SLOTS + j, :], p[:, j % 2, at:at + P],
                                       start=start, stop=stop)
                    return mm

                product(0, 0, 0, True, False)
                product(0, 1, 2 * P, False, True)
                product(1, 0, P, True, True).then_inc(N["pv"], 1)

            def head_transposes(b, g):
                pe.wait_ge(N["ot"], nth(GROUPS, b, g))
                wait_reuse(pe, N["at"], nth(GROUPS, b, g - 1))
                if g == 2 and has(b - 1):
                    wait_reuse(pe, N["x"], nth(1, b - 1, 0))
                for t in range(BT):
                    mm = pe.transpose(head_ps[:, t * P:(t + 1) * P], heads_t[g % 2][:, 1 - t, :], S.ident[:, :])
                mm.then_inc(N["ott"], 1)

            def back_transposes(b):
                pe.wait_ge(N["at"], nth(GROUPS, b, GROUPS - 1))
                for t in range(BT):
                    mm = pe.transpose(out_ps[:, t, :], heads[:, t, :, :], S.ident[:, :])
                mm.then_inc(N["att"], 1)

            def output(b):
                pe.wait_ge(N["ah"], nth(1, b, 0))
                if has(b + 1):
                    pe.wait_ge(N["at"], nth(GROUPS, b + 1, 0))
                for t in range(BT):
                    mm = pe.matmul(out_ps[:, t, :], h_t[:, t, :], S.wo[:, :], start=True, stop=True)
                mm.then_inc(N["wo"], 1)

            def score_t_banks_read(b, u):
                before = (b, u - 2) if u >= 2 else (b - 1, u - 2 + PAIRS)
                if has(before[0]):
                    wait_reuse(pe, N["exp"], nth(PAIRS, *before))
                if u % 2 == 1:
                    wb, wg = weighed(*before)
                    if has(wb):
                        wait_reuse(pe, N["ot"], nth(GROUPS, wb, wg))
                elif u == 4 and has(b + 1):
                    pe.wait_ge(N["vs"], nth(1, b + 1, 0))
                elif u == 6 and has(b + 2):
                    pe.wait_ge(N["tx"], nth(1, b + 2, 0))

            def score_bank_read(b, u, s):
                sb, su = behind(b, u - 1) if u > 0 else behind(b - 1, PAIRS - 1)
                if has(sb):
                    wait_reuse(pe, N["max"], nth(HEADS, sb, 2 * su + s))
                if u % 2 == 1:
                    mb, mg = shifted(b, u - 1)
                    if has(mb):
                        wait_reuse(pe, N["q2"], nth(GROUPS, mb, mg))

            def body(b):
                for u in range(PAIRS):
                    score_t_banks_read(b, u)
                    if u == 2 and has(b + 1):
                        value(b + 1)
                    if u == 4 and has(b + 2):
                        transposes(b + 2)
                    if u % 2 == 1 and has(weighed(b, u)[0]):
                        weigh(*weighed(b, u))
                    if has(b):
                        scores_t(b, u)
                    done = weighed(b, u - 1) if u > 0 else weighed(b - 1, PAIRS - 1)
                    for s in range(2):
                        score_bank_read(b, u, s)
                        if u % 2 == 0 and has(shifted(b, u)[0]):
                            max_transposes(*shifted(b, u), s)
                        if has(behind(b, u)[0]):
                            scores(*behind(b, u), s)
                    if u == 4 and has(b - 1):
                        back_transposes(b - 1)
                    if u == 6 and has(b - 1):
                        output(b - 1)
                    if u % 2 == 0 and has(done[0]):
                        head_transposes(*done)
                    if has(b + 1) and projected(u) is not None:
                        project(b + 1, projected(u))
                    if u == 7 and has(b + 2):
                        ranks(b + 2)

            over_batches(pe, body)

        @block.scalar
        def _(act):
            def keep_tokens(b):
                act.wait_ge(N["t"], nth(1, b, 0))
                wait_reuse(act, N["c"], b)
                act.activation(t_hi[:, :].rearrange("p (t q) -> p t q", t=BT), extra_t_ps[0], ACT.Copy).then_inc(N["thi"], 1)
                wait_reuse(act, N["tlo"], b)
                act.activation(t_x[:, :].rearrange("p (t q) -> p t q", t=BT), extra_t_ps[0], ACT.Copy).then_inc(N["tx"], 1)

            def split_ranks(b):
                act.wait_ge(N["c"], nth(1, b, 0))
                wait_reuse(act, N["vmm"], b)
                wait_reuse(act, N["qk"], GROUPS * b)
                act.activation(low_rank[:, :], rank_ps[0:96, :], ACT.Copy).then_inc(N["chi"], 1)

            def keep_value(b):
                act.wait_ge(N["vmm"], nth(1, b, 0))
                wait_reuse(act, N["v"], b)
                act.activation(value_in[:, :, :, :].rearrange("p t h d -> p t (h d)"), extra_t_ps[0], ACT.Copy)\
                    .then_inc(N["vs"], 1)

            def parts(b, g):
                act.wait_ge(N["qk"], nth(GROUPS, b, g))
                wait_reuse(act, N["kq"], nth(GROUPS, b, g - 1))
                act.activation(q_part[:, :], qk_ps[:, 0:SEQ], ACT.Identity, scale=S.vec[:, Q_SIGN:Q_SIGN + 1])\
                    .then_inc(N["tqk"], 1)
                act.activation(k_part[:, :], qk_ps[:, SEQ:], ACT.Identity, scale=S.vec[:, K_SIGN:K_SIGN + 1],
                               bias=S.vec[:, K_ONES:K_ONES + 1]).then_inc(N["tqk"], 1)

            def exps(b, u):
                act.wait_ge(N["sc"], nth(PAIRS, b, u))
                wait_reuse(act, N["pv"], nth(GROUPS, b, u // 2 - 2))
                act.activation(probs[u % 4][:, :, :], score_t_ps[u % 2], ACT.Exp, scale=inv_sqrt).then_inc(N["exp"], 1)

            def place_keys(b, g):
                act.wait_ge(N["zeros"], GROUPS // 2)
                act.wait_ge(N["set"], ALL_SET)
                act.wait_ge(N["kq"], nth(GROUPS, b, g))
                if has(b - 1):
                    act.wait_ge(N["sc"], nth(PAIRS, b - 1, 2 * g + 1))
                for j in (0, 1):
                    mm = act.activation(k_head[slot(j), g, j, :], k_st[slot(j), g % 2, :].bitcast(FP32), ACT.Copy)
                mm.then_inc(N["ka"], 1)

            def keep_heads(b, g):
                act.wait_ge(N["pv"], nth(GROUPS, b, g))
                wait_reuse(act, N["ott"], nth(GROUPS, b, g - 2))
                act.activation(heads_t[g % 2][:, :, :], extra_t_ps[1], ACT.Copy).then_inc(N["ot"], 1)

            def body(b):
                for u in range(PAIRS):
                    if u % 2 == 1 and has(weighed(b, u)[0]):
                        if has(b):
                            act.wait_ge(N["sc"], nth(PAIRS, b, u))
                        keep_heads(*weighed(b, u))
                    if has(b):
                        exps(b, u)
                    if u == 2 and has(b + 1):
                        keep_value(b + 1)
                    if u == 4 and has(b + 2):
                        keep_tokens(b + 2)
                    if u % 2 == 1 and has(b + 1):
                        place_keys(b + 1, u // 2)
                    if has(b + 1) and projected(u) is not None:
                        parts(b + 1, projected(u))
                    if u == 7 and has(b + 2):
                        split_ranks(b + 2)

            over_batches(act, body)

        @block.vector
        def _(dve):
            def statistics(b):
                for t in range(BT):
                    dve.bn_stats(st[:, t, :], S.x[:, bass.ds(b * BT + t, 1), :]).then_inc(N["st"], 1)
                hold(dve, S, N["st"], nth(BT, b, BT - 1))
                for t in range(BT):
                    dve.bn_aggr(mv[:, t, :], st[:, t, :]).then_inc(N["mv"], 1)

            def apply_norm(b):
                dve.wait_ge(N["rstd"], nth(1, b, 0))
                wait_reuse(dve, N["t"], b)
                for t in range(BT):
                    dve.tensor_scalar(xn[:, t, :], S.x[:, bass.ds(b * BT + t, 1), :], mv[:, t, 0:1], rstd[:, t:t + 1],
                                      ALU.subtract, ALU.mult).then_inc(N["xn"], 1)

            def low_ranks(b):
                dve.wait_ge(N["chi"], nth(1, b, 0))
                dve.tensor_tensor(low_rank[DC:2 * DC, :], rank_ps[DC:2 * DC, :], low_rank[DC:2 * DC, :].bitcast(FP32),
                                  ALU.subtract).then_inc(N["clo"], 1)

            def stack_q(b, g):
                dve.wait_ge(N["tqk"], nth(2 * GROUPS, b, 2 * g + 1))
                wait_reuse(dve, N["q2"], nth(GROUPS, b - 1, g))
                dve.scalar_tensor_tensor(q_st[:, g, :], qk_ps[:, 0:SEQ], S.vec[:, Q_LOW:Q_LOW + 1],
                                         q_part[:, :].bitcast(FP32), ALU.mult, ALU.add)

            def stack_k(b, g):
                wait_reuse(dve, N["ka"], nth(GROUPS, b, g - 2))
                wait_reuse(dve, N["kp"], nth(2 * GROUPS, b, 2 * g - 3))
                dve.scalar_tensor_tensor(k_st[:, g % 2, :], qk_ps[:, SEQ:], S.vec[:, K_LOW:K_LOW + 1],
                                         k_part[:, :].bitcast(FP32), ALU.mult, ALU.add).then_inc(N["kq"], 1)

            def maxima(b, u, s):
                dve.wait_ge(N["s"], nth(HEADS, b, 2 * u + s))
                wait_reuse(dve, N["mneg"], nth(GROUPS, b - 1, u // 2))
                dve.reduce_max(block_max[:, 2 * u + s, :], score_ps[:, s, :].rearrange("p (k q) -> p k q", q=P),
                               axis=AX.X, negate=True).then_inc(N["max"], 1)

            def split_maxima(b, g, part):
                h = slice(g * SLOTS, (g + 1) * SLOTS)
                hi = max_rows[:, :, h, MAX_ROW]
                both = block_max[:, h, 2:0:-1].rearrange("p h t -> p t h")
                if part == 0:
                    dve.wait_ge(N["max"], nth(HEADS, b, SLOTS * g + SLOTS - 1))
                    dve.tensor_tensor(block_max[:, h, 1], block_max[:, h, 0], block_max[:, h, 1], ALU.min).then_inc(N["both"], 1)
                elif part == 1:
                    wait_reuse(dve, N["mt"], nth(2 * GROUPS, b - 1, 2 * g + 1))
                    dve.wait_ge(N["both"], nth(GROUPS, b, g))
                    dve.tensor_copy(hi.bitcast(F32R), both).then_inc(N["mhi"], 1)
                else:
                    dve.wait_ge(N["mhi"], nth(GROUPS, b, g))
                    dve.tensor_tensor(max_rows[:, :, h, MAX_ROW + 1], both, hi, ALU.subtract).then_inc(N["mneg"], 1)

            def add_maxima(b, g, i):
                dve.wait_ge(N["mt"], nth(2 * GROUPS, b, 2 * g + i))
                q = slice((1 - i) * P, (2 - i) * P)
                mm = dve.tensor_tensor(q_max[:, g, i * P:(i + 1) * P], extra_ps[:, i, :], q_st[:, g, q].bitcast(FP32), ALU.add)
                if i == BT - 1:
                    mm.then_inc(N["q2"], 1)

            def divide(b, g, part):
                h = slice(g * SLOTS, (g + 1) * SLOTS)
                out = head_ps.rearrange("p (t h c) -> p t h c", t=BT, h=SLOTS)
                if part == 0:
                    dve.wait_ge(N["ott"], nth(GROUPS, b, g))
                    wait_reuse(dve, N["at"], nth(GROUPS, b, g - 1))
                    dve.reciprocal(rsum[:, :, h, :], out[:, :, :, DK:DK + 1]).then_inc(N["rs"], 1)
                    return
                dve.wait_ge(N["rs"], nth(GROUPS, b, g))
                if g == 0:
                    wait_reuse(dve, N["att"], b)
                for t in range(BT):
                    mm = dve.tensor_tensor(heads[:, t, h, :], out[:, t, :, 0:DK],
                                           rsum[:, t, h, :].to_broadcast([P, SLOTS, DK]), ALU.mult)
                mm.then_inc(N["at"], 1)

            def keep_outputs(b):
                dve.wait_ge(N["att"], nth(1, b, 0))
                dve.tensor_copy(h_t[:, :, :], out_ps).then_inc(N["ah"], 1)

            def update(b):
                dve.wait_ge(N["wo"], nth(1, b, 0))
                x = S.x[:, bass.ds(b * BT, BT), :]
                dve.tensor_tensor(x, out_ps, x, ALU.add).then_inc(N["x"], 1)

            def two_steps(b, u):
                even, odd = behind(b, u), behind(b, u + 1)
                g = even[1] // 2
                done = weighed(b, u - 1) if u > 0 else weighed(b - 1, PAIRS - 1)
                for s in range(2):
                    if has(even[0]):
                        dve.wait_ge(N["s"], nth(HEADS, even[0], 2 * even[1] + s))
                    if has(shifted(b, u)[0]):
                        add_maxima(*shifted(b, u), s)
                    if has(even[0]):
                        maxima(*even, s)
                if has(b + 1):
                    stack_q(b + 1, u // 2)
                if has(even[0]):
                    split_maxima(even[0], g, 0)
                if has(b + 1):
                    stack_k(b + 1, u // 2)
                if u == 0 and has(b + 2) and not is_ready(b + 2):
                    apply_norm(b + 2)
                if has(even[0]):
                    split_maxima(even[0], g, 1)
                    split_maxima(even[0], g, 2)
                if has(odd[0]):
                    for s in range(2):
                        maxima(*odd, s)
                if has(done[0]):
                    divide(*done, 0)
                if u == 4 and has(b - 1):
                    keep_outputs(b - 1)
                if u == 6 and has(b - 1):
                    update(b - 1)
                if has(done[0]):
                    divide(*done, 1)
                if u == 4 and has(b + 3) and not is_ready(b + 3):
                    statistics(b + 3)
                if is_end(b):
                    if u == 0:
                        ahead.statistics(dve)
                    if u == 4:
                        ahead.apply(dve)
                if u == 6 and has(b + 2):
                    low_ranks(b + 2)

            def body(b):
                for u in range(0, PAIRS, 2):
                    two_steps(b, u)

            for g in range(GROUPS // 2):
                dve.memset(k_head[:, g, :, :].bitcast(FP32), 0.0).then_inc(N["zeros"], 1)
            dve.wait_ge(N["set"], 3)
            over_batches(dve, body)

        @block.gpsimd
        def _(pool):
            def power(b):
                pool.wait_ge(N["mv"], nth(BT, b, BT - 1))
                pool.tensor_tensor(tmp[:, :], mv[:, :, 1], S.eps_ln[:, 0:BT], ALU.add).then_inc(N["eps"], 1)
                pool.wait_ge(N["eps"], nth(1, b, 0))
                pool.tensor_tensor(rstd[:, :], tmp[:, :], S.minus_half[:, 0:BT], ALU.pow).then_inc(N["rstd"], 1)
                hold(pool, S, N["rstd"], nth(1, b, 0))

            def place_values(b):
                hold(pool, S, N["vs"], nth(1, b, 0))
                if has(b - 1):
                    hold(pool, S, N["pv"], nth(GROUPS, b - 1, GROUPS - 1))
                pool.tensor_copy(values[:, :, :, 0:DK], value_in[:, :, :, :]).then_inc(N["v"], 1)
                hold(pool, S, N["v"], nth(1, b, 0))

            def place_keys(b, g):
                hold(pool, S, N["zeros"], GROUPS // 2)
                hold(pool, S, N["kq"], nth(GROUPS, b, g))
                if has(b - 1):
                    hold(pool, S, N["sc"], nth(PAIRS, b - 1, 2 * g + 1))
                for i, j in enumerate((2, 3)):
                    pool.tensor_copy(k_head[slot(j), g, j, :], k_st[slot(j), g % 2, :]).then_inc(N["kp"], 1)
                    hold(pool, S, N["kp"], nth(2 * GROUPS, b, 2 * g + i))

            def low(b):
                pool.wait_ge(N["tx"], nth(1, b, 0))
                wait_reuse(pool, N["c"], b)
                pool.tensor_tensor(t_lo[:, :], t_x[:, :], t_hi[:, :].bitcast(FP32), ALU.subtract).then_inc(N["tlo"], 1)
                hold(pool, S, N["tlo"], nth(1, b, 0))

            def body(b):
                if has(b):
                    place_values(b)
                for g in range(GROUPS):
                    if has(b + 1):
                        place_keys(b + 1, g)
                    if g == 3 and has(b + 3) and not is_ready(b + 3):
                        power(b + 3)
                    if g == 0 and is_end(b):
                        ahead.power(pool)
                    if g == 1 and has(b + 2):
                        low(b + 2)

            pool.memset(values[:, :, :, :], 0.0).then_inc(N["set"], 1)
            pool.wait_ge(N["set"], 1)
            pool.memset(values[:, :, :, DK:DK + 1], 1.0).then_inc(N["set"], 1)
            pool.memset(max_rows[:, :, :, :], 0.0).then_inc(N["set"], 1)
            for g in range(GROUPS // 2, GROUPS):
                pool.memset(k_head[:, g, :, :].bitcast(FP32), 0.0).then_inc(N["set"], 1)
            pool.wait_ge(N["set"], ALL_SET)
            over_batches(pool, body)


def rolls(nc, S, name, sems, start, ready, ahead):
    with ExitStack() as ctx:
        def sb(n, shape, dt=FP32):
            return ctx.enter_context(nc.sbuf_tensor(f"{name}_{n}", shape, dt))

        def sem(n):
            if n not in sems:
                sems[n] = S.sems.enter_context(nc.semaphore(f"{name}_{n}"))
            return sems[n]

        NG = len(SHIFTS)
        TERMS = (NG + 1) // 2
        xn = sb("xn", [P, CT, D])
        t_hi, t_lo = sb("t_hi", [P, CHUNK], F32R), sb("t_lo", [P, CHUNK], F32R)
        value = sb("value", [P, 2, SEQ + 2 * PAD])
        gate = [sb(f"gate{i}", [P, CHUNK]) for i in range(3)]
        prod = [sb(f"prod{i}", [P, CHUNK]) for i in range(NG)]
        st, mv = sb("st", [P, CT, 6]), sb("mv", [P, CT, 2])
        st2, mv2 = sb("st2", [P, CT, 6]), sb("mv2", [P, CT, 2])
        rstd, tmp, rstd2, tmp2 = (sb(n, [P, CT]) for n in ("rstd", "tmp", "rstd2", "tmp2"))
        total, centred, x_beta = (sb(n, [P, CT, D]) for n in ("total", "centred", "x_beta"))
        xt_ps, val_ps, sum_ps = S.bank[0], S.bank[1], S.bank[2]
        gate_ps = S.bank[3:6]

        st_done, mv_done, rstd_done, xn_done = sem("st_done"), sem("mv_done"), sem("rstd_done"), sem("xn_done")
        xt_done, hi_done, lo_done, val_done = sem("xt_done"), sem("hi_done"), sem("lo_done"), sem("val_done")
        vpad_done, gmm_done, gate_done, prod_done = sem("vpad_done"), sem("gmm_done"), sem("gate_done"), sem("prod_done")
        pair_done, sum_done, total_done = sem("pair_done"), sem("sum_done"), sem("total_done")
        st2_done, mv2_done, rstd2_done = sem("st2_done"), sem("mv2_done"), sem("rstd2_done")
        centred_done, x_beta_done, x_done = sem("centred_done"), sem("x_beta_done"), sem("x_done")
        eps_done, eps2_done = sem("eps_done"), sem("eps2_done")
        chunks = Chunks(start)
        block = ctx.enter_context(nc.Block())

        def single(c, k):
            return chunks.is_last(c) and k >= TERMS - 2

        @block.tensor
        def _(pe):
            def front(c):
                pe.wait_ge(xn_done, nth(CT, c, CT - 1))
                wait_reuse(pe, lo_done, c)
                source = ready.xn if chunks.is_first(c) else xn
                for t in range(CT):
                    mm = pe.transpose(xt_ps[:, t * P:(t + 1) * P], source[:, t, :], S.ident[:, :])
                mm.then_inc(xt_done, 1)

            def values(c):
                pe.wait_ge(lo_done, nth(1, c, 0))
                wait_reuse(pe, vpad_done, 3 * c)
                three(pe, val_ps[:, :], *columns(S, VALUE0), t_hi[:, :], t_lo[:, :]).then_inc(val_done, 1)

            def gates(c, *ns):
                for n in ns:
                    wait_reuse(pe, gate_done, nth(NG, c, n - 3))
                    three(pe, gate_ps[n % 3][:, :], *columns(S, GATES0 + n * D), t_hi[:, :], t_lo[:, :])\
                        .then_inc(gmm_done, 1)

            def add_term(c, k):
                if k == 0:
                    pe.wait_ge(prod_done, nth(NG, c, 0))
                    wait_reuse(pe, total_done, c)
                elif not single(c, k):
                    pe.wait_ge(pair_done, nth(TERMS - 1, c, k - 1))
                rolls = (2 * k - 1, 2 * k) if single(c, k) else (max(0, 2 * k - 1),)
                for n in rolls:
                    if single(c, k):
                        pe.wait_ge(prod_done, nth(NG, c, n))
                    for t in range(CT):
                        mm = pe.matmul(sum_ps[:, t * P:(t + 1) * P], prod[n][:, t * P:(t + 1) * P], S.ident[:, :],
                                       start=n == 0 and t == 0, stop=k == TERMS - 1 and n == rolls[-1] and t == CT - 1)
                mm.then_inc(sum_done, 1)

            def body(c):
                values(c)
                gates(c, 0, 1, 2)
                if not chunks.is_first(c):
                    add_term(c - 1, 3)
                    add_term(c - 1, 4)
                gates(c, 3, 4, 5)
                add_term(c, 0)
                gates(c, 6, 7, 8)
                if not chunks.is_last(c):
                    front(c + 1)
                add_term(c, 1)
                add_term(c, 2)

            front(chunks.first)
            chunks.each(pe, body)
            add_term(chunks.last, 3)
            add_term(chunks.last, 4)

        @block.scalar
        def _(act):
            def front(c):
                act.wait_ge(xt_done, nth(1, c, 0))
                wait_reuse(act, gmm_done, NG * c)
                act.activation(t_hi[:, :], xt_ps[:, :], ACT.Copy).then_inc(hi_done, 1)

            def keep_value(c):
                act.wait_ge(val_done, nth(1, c, 0))
                wait_reuse(act, prod_done, NG * c)
                v = val_ps[:, :].rearrange("p (b s) -> p b s", b=2)
                act.activation(value[:, :, PAD:PAD + SEQ], v, ACT.Copy).then_inc(vpad_done, 1)
                act.activation(value[:, :, 0:PAD], v[:, :, SEQ - PAD:SEQ], ACT.Copy).then_inc(vpad_done, 1)
                act.activation(value[:, :, PAD + SEQ:], v[:, :, 0:PAD], ACT.Copy).then_inc(vpad_done, 1)

            def gates(c, *ns):
                for n in ns:
                    act.wait_ge(gmm_done, nth(NG, c, n))
                    wait_reuse(act, prod_done, nth(NG, c, n - 3))
                    act.activation(gate[n % 3][:, :], gate_ps[n % 3][:, :], ACT.Sigmoid).then_inc(gate_done, 1)

            def keep_total(c):
                act.wait_ge(sum_done, nth(TERMS, c, TERMS - 1))
                wait_reuse(act, centred_done, CT * c)
                act.activation(total[:, :, :].rearrange("p t d -> p (t d)"), sum_ps[:, :], ACT.Copy).then_inc(total_done, 1)

            def body(c):
                keep_value(c)
                gates(c, 0, 1, 2)
                if not chunks.is_first(c):
                    keep_total(c - 1)
                gates(c, 3, 4, 5, 6, 7, 8)
                if not chunks.is_last(c):
                    front(c + 1)

            front(chunks.first)
            chunks.each(act, body)
            keep_total(chunks.last)

        @block.vector
        def _(dve):
            def statistics(c):
                for t in range(CT):
                    dve.bn_stats(st[:, t, :], S.x[:, chunks.tile(c, t), :]).then_inc(st_done, 1)
                hold(dve, S, st_done, nth(CT, c, CT - 1))
                for t in range(CT):
                    dve.bn_aggr(mv[:, t, :], st[:, t, :]).then_inc(mv_done, 1)

            def apply_norm(c):
                dve.wait_ge(rstd_done, nth(1, c, 0))
                wait_reuse(dve, xt_done, c)
                for t in range(CT):
                    dve.tensor_scalar(xn[:, t, :], S.x[:, chunks.tile(c, t), :], mv[:, t, 0:1], rstd[:, t:t + 1],
                                      ALU.subtract, ALU.mult).then_inc(xn_done, 1)

            def low(c):
                dve.wait_ge(hi_done, nth(1, c, 0))
                dve.tensor_tensor(t_lo[:, :], xt_ps[:, :], t_hi[:, :].bitcast(FP32), ALU.subtract).then_inc(lo_done, 1)

            def roll(c, *ns):
                for n in ns:
                    if n == 0:
                        dve.wait_ge(vpad_done, nth(3, c, 2))
                    dve.wait_ge(gate_done, nth(NG, c, n))
                    wait_reuse(dve, sum_done, nth(TERMS, c - 1, (n + 1) // 2))
                    at = PAD + SHIFTS[n]
                    dve.tensor_tensor(prod[n][:, :].rearrange("p (b s) -> p b s", b=2),
                                      gate[n % 3][:, :].rearrange("p (b s) -> p b s", b=2),
                                      value[:, :, at:at + SEQ], ALU.mult).then_inc(prod_done, 1)

            def sum_statistics(c):
                hold(dve, S, total_done, nth(1, c, 0))
                for t in range(CT):
                    dve.bn_stats(st2[:, t, :], total[:, t, :]).then_inc(st2_done, 1)
                hold(dve, S, st2_done, nth(CT, c, CT - 1))
                for t in range(CT):
                    dve.bn_aggr(mv2[:, t, :], st2[:, t, :]).then_inc(mv2_done, 1)

            def centre(c):
                hold(dve, S, mv2_done, nth(CT, c, CT - 1))
                wait_reuse(dve, x_done, CT * c)
                for t in range(CT):
                    dve.scalar_tensor_tensor(centred[:, t, :], total[:, t, :], mv2[:, t, 0:1], S.gamma[:, :],
                                             ALU.subtract, ALU.mult).then_inc(centred_done, 1)

            def update(c):
                dve.wait_ge(rstd2_done, nth(1, c, 0))
                dve.wait_ge(centred_done, nth(CT, c, CT - 1))
                dve.wait_ge(x_beta_done, nth(1, c, 0))
                for t in range(CT):
                    dve.scalar_tensor_tensor(S.x[:, chunks.tile(c, t), :], centred[:, t, :], rstd2[:, t:t + 1], x_beta[:, t, :],
                                             ALU.mult, ALU.add).then_inc(x_done, 1)

            def body(c):
                if not chunks.is_last(c):
                    statistics(c + 1)
                else:
                    ahead.statistics(dve)
                roll(c, 0, 1, 2)
                if not chunks.is_last(c):
                    apply_norm(c + 1)
                else:
                    ahead.apply(dve)
                roll(c, 3)
                if not chunks.is_first(c):
                    sum_statistics(c - 1)
                roll(c, 4, 5)
                if not chunks.is_first(c):
                    centre(c - 1)
                roll(c, 6, 7)
                if not chunks.is_last(c):
                    low(c + 1)
                roll(c, 8)
                if not chunks.is_first(c):
                    update(c - 1)

            low(chunks.first)
            chunks.each(dve, body)
            sum_statistics(chunks.last)
            centre(chunks.last)
            update(chunks.last)

        @block.gpsimd
        def _(pool):
            def power(c, mv, ready, tmp, eps_done, out, done):
                pool.wait_ge(ready, nth(CT, c, CT - 1))
                pool.tensor_tensor(tmp[:, :], mv[:, :, 1], S.eps_ln[:, 0:CT], ALU.add).then_inc(eps_done, 1)
                pool.wait_ge(eps_done, nth(1, c, 0))
                pool.tensor_tensor(out[:, :], tmp[:, :], S.minus_half[:, 0:CT], ALU.pow).then_inc(done, 1)

            def add_pair(c, k):
                pool.wait_ge(prod_done, nth(NG, c, 2 * k + 2))
                pool.tensor_tensor(prod[2 * k + 1][:, :], prod[2 * k + 1][:, :], prod[2 * k + 2][:, :], ALU.add)\
                    .then_inc(pair_done, 1)

            def add_beta(c):
                if not isinstance(c, int) or c > 0:
                    hold(pool, S, x_done, CT * c)
                pool.tensor_tensor(x_beta[:, :, :], S.x[:, chunks.tiles(c), :],
                                   S.beta[:, :].unsqueeze(1).to_broadcast([P, CT, D]), ALU.add).then_inc(x_beta_done, 1)

            def body(c):
                if not chunks.is_last(c):
                    power(c + 1, mv, mv_done, tmp, eps_done, rstd, rstd_done)
                else:
                    ahead.power(pool)
                add_pair(c, 0)
                if not chunks.is_first(c):
                    power(c - 1, mv2, mv2_done, tmp2, eps2_done, rstd2, rstd2_done)
                add_pair(c, 1)
                if not chunks.is_last(c):
                    add_pair(c, 2)
                    add_pair(c, 3)
                add_beta(c)

            chunks.each(pool, body)
            power(chunks.last, mv2, mv2_done, tmp2, eps2_done, rstd2, rstd2_done)


def mix(nc, S, name, sems, start, ready, ahead=None, out_dram=None):
    with ExitStack() as ctx:
        def sb(n, shape, dt=FP32):
            return ctx.enter_context(nc.sbuf_tensor(f"{name}_{n}", shape, dt))

        def sem(n):
            if n not in sems:
                sems[n] = S.sems.enter_context(nc.semaphore(f"{name}_{n}"))
            return sems[n]

        xn = sb("xn", [P, TILES, D])
        st, mv = sb("st", [P, TILES, 6]), sb("mv", [P, TILES, 2])
        rstd, tmp = sb("rstd", [P, TILES]), sb("tmp", [P, TILES])
        xt = sb("xt", [P, CHUNK])
        x_hi = sb("x_hi", [P, BATCH, SEQ + 1], F32R)
        x_lo = sb("x_lo", [P, BATCH, SEQ + 1], F32R)
        recept = sb("recept", [P, CHUNKS, CHUNK])
        relu, key = (sb(n, [P, CHUNK]) for n in ("relu", "key"))
        key_hi, key_lo = sb("key_hi", [P, CHUNK], F32R), sb("key_lo", [P, CHUNK], F32R)
        out = sb("out", [P, CHUNK])
        r_ps, k_ps, v_ps, o_ps = S.bank[0:4]
        xt_ps = S.bank[4:6]

        st_done, mv_done, rstd_done, xn_done = sem("st_done"), sem("mv_done"), sem("rstd_done"), sem("xn_done")
        eps_done, xt_done, xhi_done, keep_done = sem("eps_done"), sem("xt_done"), sem("xhi_done"), sem("keep_done")
        xlo_done, k_done, r_done, sig_done = sem("xlo_done"), sem("k_done"), sem("r_done"), sem("sig_done")
        key_done, khi_done, klo_done, v_done = sem("key_done"), sem("khi_done"), sem("klo_done"), sem("v_done")
        out_done, o_done, x_done, zero_done = sem("out_done"), sem("o_done"), sem("x_done"), sem("zero_done")
        relu_done = sem("relu_done")
        chunks = Chunks(start)
        block = ctx.enter_context(nc.Block())
        last, given = chunks.last, ready.tiles // CT

        def halves(c, shift):
            b = bass.ds((c - start) * 2, 2)
            return x_hi[:, b, 1 - shift:1 - shift + SEQ], x_lo[:, b, 1 - shift:1 - shift + SEQ]

        def gates_of(c):
            return recept[:, bass.ds(c - start, 1), :].rearrange("p c t -> p (c t)")

        def tiles(c):
            return range((c - start) * CT, (c - start + 1) * CT)

        def by_batch(a):
            return a[:, :].rearrange("p (b s) -> p b s", b=2)

        if out_dram is not None:
            sent = sem("sent")

            @block.sync
            def _(sp):
                for c in range(start, last + 1):
                    sp.wait_ge(x_done, nth(1, c, 0))
                    sp.dma_start(out_dram[c - start], S.x[:, (c - start) * CT:(c - start + 1) * CT, :]).then_inc(sent, 16)
                sp.wait_ge(sent, 16 * CHUNKS)

        @block.tensor
        def _(pe):
            def front(c):
                pe.wait_ge(xn_done, nth(CT, c, CT - 1))
                wait_reuse(pe, keep_done, c - 1)
                source = ready.xn if c - start < given else xn
                for n, t in enumerate(tiles(c)):
                    mm = pe.transpose(xt_ps[c % 2][:, n * P:(n + 1) * P], source[:, t, :], S.ident[:, :])
                mm.then_inc(xt_done, 1)

            def mixed(c, out, w):
                for shift in range(2):
                    hi, lo = halves(c, shift)
                    whi, wlo = (a[:, (2 * w + shift) * D:(2 * w + shift + 1) * D] for a in (S.fold_hi, S.fold_lo))
                    pe.matmul(out, whi, hi, start=(shift == 0), stop=False)
                    pe.matmul(out, whi, lo, start=False, stop=False)
                    mm = pe.matmul(out, wlo, hi, start=False, stop=(shift == 1))
                return mm

            def keys_and_gates(c):
                pe.wait_ge(xlo_done, nth(1, c, 0))
                wait_reuse(pe, relu_done, c)
                mixed(c, k_ps[:, :], 1).then_inc(k_done, 1)
                wait_reuse(pe, sig_done, c)
                mixed(c, r_ps[:, :], 0).then_inc(r_done, 1)

            def v(c):
                pe.wait_ge(klo_done, nth(1, c, 0))
                wait_reuse(pe, out_done, c)
                three(pe, v_ps[:, :], *columns(S, V0), key_hi[:, :], key_lo[:, :]).then_inc(v_done, 1)

            def back(c):
                pe.wait_ge(out_done, nth(1, c, 0))
                wait_reuse(pe, x_done, c)
                for t in range(CT):
                    mm = pe.transpose(o_ps[:, t * P:(t + 1) * P], out[:, t * P:(t + 1) * P], S.ident[:, :])
                mm.then_inc(o_done, 1)

            front(start)
            front(start + 1)
            keys_and_gates(start)
            for c in range(start + 2, last + 1):
                front(c)
            keys_and_gates(start + 1)
            v(start)
            with pe.Fori(start + 2, last + 1) as c:
                keys_and_gates(c)
                back(c - 2)
                v(c - 1)
            back(last - 1)
            v(last)
            back(last)

        @block.scalar
        def _(act):
            def front(c):
                act.wait_ge(xt_done, nth(1, c, 0))
                act.activation(halves(c, 0)[0], by_batch(xt_ps[c % 2]), ACT.Copy).then_inc(xhi_done, 1)
                wait_reuse(act, xlo_done, c)
                act.activation(xt[:, :], xt_ps[c % 2][:, :], ACT.Copy).then_inc(keep_done, 1)

            def gate(c):
                act.wait_ge(r_done, nth(1, c, 0))
                act.activation(gates_of(c), r_ps[:, :], ACT.Sigmoid).then_inc(sig_done, 1)

            def positive(c):
                act.wait_ge(k_done, nth(1, c, 0))
                wait_reuse(act, key_done, c)
                wait_reuse(act, khi_done, c)
                act.activation(relu[:, :], k_ps[:, :], ACT.Relu).then_inc(relu_done, 1)

            def key_high(c):
                act.wait_ge(relu_done, nth(1, c, 0))
                wait_reuse(act, v_done, c)
                act.activation(key_hi[:, :], relu[:, :], ACT.Square).then_inc(khi_done, 1)

            act.wait_ge(zero_done, start // CHUNKS + 1)
            front(start)
            front(start + 1)
            positive(start)
            gate(start)
            key_high(start)
            for c in range(start + 2, last + 1):
                front(c)
            with act.Fori(start + 1, last + 1) as c:
                positive(c)
                gate(c)
                key_high(c)

        @block.vector
        def _(dve):
            def statistics(c):
                for t in tiles(c):
                    dve.bn_stats(st[:, t, :], S.x[:, t, :]).then_inc(st_done, 1)
                dve.wait_ge(st_done, nth(CT, c, CT - 1))
                for t in tiles(c):
                    dve.bn_aggr(mv[:, t, :], st[:, t, :]).then_inc(mv_done, 1)

            def apply_norm(c):
                dve.wait_ge(rstd_done, nth(1, c, 0))
                for t in tiles(c):
                    dve.tensor_scalar(xn[:, t, :], S.x[:, t, :], mv[:, t, 0:1], rstd[:, t:t + 1], ALU.subtract, ALU.mult)\
                        .then_inc(xn_done, 1)

            def square(c):
                dve.wait_ge(relu_done, nth(1, c, 0))
                wait_reuse(dve, klo_done, c)
                dve.tensor_tensor(key[:, :], relu[:, :], relu[:, :], ALU.mult).then_inc(key_done, 1)

            def key_low(c):
                dve.wait_ge(khi_done, nth(1, c, 0))
                dve.wait_ge(key_done, nth(1, c, 0))
                dve.tensor_tensor(key_lo[:, :], key[:, :], key_hi[:, :].bitcast(FP32), ALU.subtract).then_inc(klo_done, 1)

            def output(c):
                dve.wait_ge(v_done, nth(1, c, 0))
                dve.wait_ge(sig_done, nth(1, c, 0))
                wait_reuse(dve, o_done, c)
                dve.tensor_tensor(out[:, :], v_ps[:, :], gates_of(c), ALU.mult).then_inc(out_done, 1)

            def update(c):
                dve.wait_ge(o_done, nth(1, c, 0))
                x = S.x[:, chunks.tiles(c), :]
                dve.scalar_tensor_tensor(x, o_ps[:, :].rearrange("p (t d) -> p t d", d=D), 0.5, x, ALU.mult, ALU.add)\
                    .then_inc(x_done, 1)

            for a in (x_hi, x_lo):
                mm = dve.memset(a[:, :, 0:1].bitcast(FP32), 0.0)
            mm.then_inc(zero_done, 1)
            statistics(start + given)
            for c in range(start + given, last):
                statistics(c + 1)
                apply_norm(c)
            apply_norm(last)
            square(start)
            key_low(start)
            with dve.Fori(start + 1, last) as c:
                square(c)
                output(c - 1)
                key_low(c)
                update(c - 1)
            square(last)
            output(last - 1)
            key_low(last)
            if ahead:
                ahead.statistics(dve)
            update(last - 1)
            output(last)
            if ahead:
                ahead.apply(dve)
            update(last)

        @block.gpsimd
        def _(pool):
            def power(c):
                t = slice(tiles(c)[0], tiles(c)[-1] + 1)
                pool.wait_ge(mv_done, nth(CT, c, CT - 1))
                pool.tensor_tensor(tmp[:, t], mv[:, t, 1], S.eps_ln[:, 0:CT], ALU.add).then_inc(eps_done, 1)
                pool.wait_ge(eps_done, nth(1, c, 0))
                pool.tensor_tensor(rstd[:, t], tmp[:, t], S.minus_half[:, 0:CT], ALU.pow).then_inc(rstd_done, 1)

            def low(c):
                hold(pool, S, keep_done, nth(1, c, 0))
                hi, lo = halves(c, 0)
                pool.tensor_tensor(lo, by_batch(xt), hi.bitcast(FP32), ALU.subtract).then_inc(xlo_done, 1)

            for c in range(start, last + 1):
                low(c)
                if c == start:
                    power(start + given)
                if start + given < c + 2 <= last:
                    power(c + 2)
            if ahead:
                ahead.power(pool)


def macaron(nc, dram):
    with ExitStack() as ctx:
        def sb(n, shape, dt=FP32):
            return ctx.enter_context(nc.sbuf_tensor(n, shape, dt))

        S = Shared()
        S.sems = ctx
        S.x = sb("x", [P, TILES, D])
        S.whi, S.wlo = sb("whi", [P, WCOLS], F32R), sb("wlo", [P, WCOLS], F32R)
        S.fold_hi, S.fold_lo = sb("fold_hi", [P, 4 * D], F32R), sb("fold_lo", [P, 4 * D], F32R)
        S.sel = sb("sel", [P, len(SHARES) * P], F32R)
        S.ident = sb("ident", [P, P])
        S.rev = sb("rev", [P, CT * EXPERTS])
        S.rev3 = S.rev[:, :].rearrange("p (t e) -> p t e", e=EXPERTS)
        S.vec, S.half_alpha, S.one_minus_mu = sb("vec", [P, 9]), sb("half_alpha", [P, 1]), sb("one_minus_mu", [P, 2])
        S.wo = sb("wo", [D, D])
        S.gamma, S.beta = sb("gamma", [P, D]), sb("beta", [P, D])
        S.ident_bf, S.mask = sb("ident_bf", [P, P], BF16), sb("mask", [P, 4 * P], BF16)
        S.up = sb("up", [96, UCOLS], F32R)
        S.combp = sb("combp", [P, CT, P])
        S.minus_half, S.eps_ln, S.eps_rms = (sb(n, [P, 2 * CT]) for n in ("minus_half", "eps_ln", "eps_rms"))
        S.nc, S.turn = nc, 0
        S.ahead = [[sb(f"ahead_{n}{i}", [P, (i + 1) * CT] + w) for n, w in (("xn", [D]), ("st", [6]), ("mv", [2]), ("rstd", []), ("rms", []), ("tmp", []))]
                   for i in range(2)]
        S.low_rank = sb("low_rank", [96, 2 * SEQ], F32R)
        S.held = ctx.enter_context(nc.semaphore("held"))
        S.psum = ctx.enter_context(nc.psum_tensor("psum", [P, 8 * 512], FP32))
        S.bank = [S.psum[:, i * 512:(i + 1) * 512] for i in range(8)]
        moe_sems, mix_sems, attn_sems, rolls_sems = {}, {}, {}, {}
        for_attn = AheadRanks(S, "attn", attn_sems)
        for_moe2 = Ahead(S, "moe1", moe_sems, CHUNKS, base=True)
        for_mix1 = Ahead(S, "mix1", mix_sems, 0, tiles=2 * CT, batches=2)
        for_rolls = Ahead(S, "rolls", rolls_sems, 0)
        for_mix2 = Ahead(S, "mix1", mix_sems, CHUNKS)
        moe(nc, S, "moe1", moe_sems, 0, None, for_attn, dram)
        attention(nc, S, "attn", attn_sems, for_attn, for_moe2)
        moe(nc, S, "moe2", moe_sems, CHUNKS, for_moe2, for_mix1)
        mix(nc, S, "mix1", mix_sems, 0, for_mix1, for_rolls)
        rolls(nc, S, "rolls", rolls_sems, 0, for_rolls, for_mix2)
        mix(nc, S, "mix2", mix_sems, CHUNKS, for_mix2, out_dram=dram["out"].rearrange("(c t p) d -> c p t d", p=P, t=CT))


def kernel(**inputs):
    import numpy as np
    import concourse.bacc as bacc
    from concourse.bass_utils import run_bass_kernel_spmd

    def grab(n):
        return np.asarray(inputs[n])

    f = np.float32
    gate_up = grab("L0_ffn_gate_up_weight")
    tiles = [gate_up[:, :HID].reshape(STEPS, P, D).transpose(2, 0, 1), gate_up[:, HID:].reshape(STEPS, P, D).transpose(2, 0, 1),
             grab("L0_ffn_down_weight").transpose(0, 2, 1).reshape(STEPS, P, D).transpose(1, 0, 2)]
    experts = np.concatenate(tiles, axis=2).reshape(P, STEPS * TILE_COLS)
    sel = np.zeros((2 * LOW0, len(SHARES), P), f)
    for g, j in enumerate(FIRST):
        for p in range(P):
            e = (j * P + p) // HID
            sel[[e, LOW0 + e], g, p] = 1.0
    weights = [grab("L0_ffn_router_weight").T, np.zeros((D, P - EXPERTS), f), experts]
    weights += [grab("L1_ffn_W_v").T, grab("L1_attn_value_W").T, grab("L1_attn_gate_W").T]
    weights += [grab("L0_attn_W_dq")] * 3 + [grab("L0_attn_W_dkv")] * 3
    weights += [grab(f"L1_ffn_W_{n}").T for n in "rk"]
    up = np.zeros((DC, UCOLS), f)
    for n, at in (("uq", UQ0), ("uk", UK0)):
        v = up[:, at:at + GROUPS * P].reshape(DC, HEADS, 32)
        w = grab(f"L0_attn_W_{n}").reshape(DC, HEADS, DK)
        for r in range(3):
            v[:, :, r * DK:(r + 1) * DK] = w
    up[:, UV0:] = grab("L0_attn_W_uv")
    row = np.arange(P) % 32 // DK
    one = np.ones(P, f)
    vec = [grab("L0_ffn_norm_weight"), np.broadcast_to(grab("L0_ffn_residual_alpha"), (P,)),
           np.array([1, 1, -1, 0], f)[row], np.array([0, 0, 1, 0], f)[row],
           np.array([1, -1, 1, 0], f)[row], np.array([0, 1, 0, 0], f)[row],
           np.isin(np.arange(P) % 32, (MAX_ROW, MAX_ROW + 1)).astype(f),
           grab("L1_ffn_mu_r"), grab("L1_ffn_mu_k")]
    later = np.where(np.arange(P)[None, :] > np.arange(P)[:, None], f(MASKED), f(0))
    arrays = {
        "x": grab("L0_attn_x").reshape(TOKENS, D),
        "weights": np.concatenate(weights, axis=1),
        "up": np.concatenate([up] * 3, axis=0),
        "vec": np.stack(vec, axis=1),
        "wo": grab("L0_attn_W_o"),
        "gamma": np.broadcast_to(grab("L1_attn_gamma"), (P, D)),
        "beta": np.broadcast_to(grab("L1_attn_beta"), (P, D)),
        "mask": np.concatenate([later, later, later.T, later.T], axis=1),
        "sel": sel.reshape(2 * LOW0, len(SHARES) * P),
        "ident": np.eye(P, dtype=f),
        "rev": np.broadcast_to(np.tile(np.arange(EXPERTS, 0, -1, dtype=f), CT), (P, CT * EXPERTS)),
    }
    nc = bacc.Bacc("TRN2", target_bir_lowering=False, num_devices=1)
    dram, sent = {}, {}
    for n, a in arrays.items():
        a = np.ascontiguousarray(a)
        sent[f"in_{n}"] = a
        dram[n] = nc.dram_tensor(f"in_{n}", a.shape, mybir.dt.from_np(a.dtype), kind="ExternalInput").ap()
    dram["out"] = nc.dram_tensor("out_x", (TOKENS, D), FP32, kind="ExternalOutput").ap()
    macaron(nc, dram)
    r = run_bass_kernel_spmd(nc, [sent], core_ids=[0])
    return r.results[0]["out_x"].reshape(BATCH, SEQ, D)
```
